# Optimizing a Trainium2 kernel written in Bass

```python
import numpy as np
import os as _os
import jax
import jax.numpy as jnp

def _softmax(x, axis=-1):
    return jax.nn.softmax(x, axis=axis)

def _gelu(x):
    return jax.nn.gelu(x, approximate=True)

def _silu(x):
    return jax.nn.silu(x)

def _sigmoid(x):
    return jax.nn.sigmoid(x)

def _layernorm(x, axis=-1, eps=1e-05):
    m = jnp.mean(x, axis=axis, keepdims=True)
    v = jnp.var(x, axis=axis, keepdims=True)
    return (x - m) / jnp.sqrt(v + eps)

def _scatter_add(tgt, idx, src, axis=0):
    return tgt.at[idx].add(src)

def _segment_sum(src, seg, n):
    return jax.ops.segment_sum(src, seg, n)
kernel_name = 'mk_seq_postln_d1_jaxref_r8_7fd003'

def setup_inputs(seed: int=0):
    np.random.seed(seed)
    _w = jnp.asarray

    def _L0_attn_setup():
        import jax, jax.numpy as jnp
        import numpy as np
        D_MODEL = 128
        NUM_HEADS = 16
        HEAD_DIM = D_MODEL // NUM_HEADS
        DILATION = 2
        SEGMENT = 128
        OFFSET = 0
        key = jax.random.key(seed)
        x = jax.random.normal(key, (4, 1024, D_MODEL), dtype=jnp.float32)
        return {'x': x}
    _L0_attn_in = _L0_attn_setup()

    def _L0_ffn_setup():
        import jax, jax.numpy as jnp
        import numpy as np
        DIM = 128
        DEPTH = 2
        HEADS = 8
        DIM_HEAD = 64
        WINDOW = 64
        INNER = HEADS * DIM_HEAD
        HID = int(DIM * 4 * 2 / 3)
        B, N = (2, 1024)
        QK_SCALE = 8.0

        def shift_token(t):
            t1, t2 = jnp.split(t, 2, axis=-1)
            t2 = jnp.pad(t2, ((0, 0), (1, 0), (0, 0)))[:, :-1]
            return jnp.concatenate([t1, t2], axis=-1)

        def l2norm(t):
            return t / jnp.clip(jnp.linalg.norm(t, axis=-1, keepdims=True), 1e-12)

        def rotate_half(x):
            x1, x2 = jnp.split(x, 2, axis=-1)
            return jnp.concatenate([-x2, x1], axis=-1)

        def rotary_xpos(q, k):
            n = q.shape[-2]
            half_idx = jnp.arange(0, DIM_HEAD, 2, dtype=jnp.float32)
            inv_freq = 1.0 / 10000.0 ** (half_idx / DIM_HEAD)
            t = jnp.arange(n, dtype=jnp.float32)
            freqs = t[:, None] * inv_freq[None, :]
            freqs = jnp.concatenate([freqs, freqs], axis=-1)
            base = (half_idx + 0.4 * DIM_HEAD) / (1.4 * DIM_HEAD)
            power = (t - n // 2) / float(WINDOW // 2)
            scale = base[None, :] ** power[:, None]
            scale = jnp.concatenate([scale, scale], axis=-1)
            cos, sin = (jnp.cos(freqs), jnp.sin(freqs))
            q = q * cos * scale + rotate_half(q) * sin * scale
            k = k * cos / scale + rotate_half(k) * sin / scale
            return (q, k)

        def local_attention(q, k, v):
            b, h, n, d = q.shape
            w = n // WINDOW
            bq = q.reshape(b, h, w, WINDOW, d) * QK_SCALE
            bk = k.reshape(b, h, w, WINDOW, d)
            bv = v.reshape(b, h, w, WINDOW, d)

            def look_around(t):
                p = jnp.pad(t, ((0, 0), (0, 0), (1, 0), (0, 0), (0, 0)))
                return jnp.concatenate([p[:, :, :w], p[:, :, 1:]], axis=3)
            bk, bv = (look_around(bk), look_around(bv))
            bt = jnp.arange(n).reshape(w, WINDOW)
            btp = jnp.pad(bt, ((1, 0), (0, 0)), constant_values=-1)
            btk = jnp.concatenate([btp[:w], btp[1:]], axis=1)
            sim = jnp.einsum('bhwid,bhwjd->bhwij', bq, bk)
            i = bt[:, :, None]
            j = btk[:, None, :]
            mask = (i < j) | (i > j + WINDOW) | (j == -1)
            sim = jnp.where(mask, -jnp.finfo(sim.dtype).max, sim)
            attn = jax.nn.softmax(sim, axis=-1)
            out = jnp.einsum('bhwij,bhwjd->bhwid', attn, bv)
            return out.reshape(b, h, n, d)

        def _layer(x, wqkv, qs, ksc, wo, lg, lb, w1, b1, w2, b2):
            b, n, _ = x.shape
            h = shift_token(x)
            qkv = h @ wqkv
            q, k, v = jnp.split(qkv, 3, axis=-1)
            to_heads = lambda t: t.reshape(b, n, HEADS, DIM_HEAD).transpose(0, 2, 1, 3)
            q, k, v = (to_heads(q), to_heads(k), to_heads(v))
            q = l2norm(q) * qs
            k = l2norm(k) * ksc
            q, k = rotary_xpos(q, k)
            o = local_attention(q, k, v)
            o = o.transpose(0, 2, 1, 3).reshape(b, n, INNER)
            x = x + o @ wo
            h = shift_token(x)
            mu = h.mean(-1, keepdims=True)
            var = h.var(-1, keepdims=True)
            h = (h - mu) / jnp.sqrt(var + 1e-05) * lg + lb
            h = h @ w1 + b1
            a, g = jnp.split(h, 2, axis=-1)
            h = a * jax.nn.gelu(g, approximate=False)
            x = x + h @ w2 + b2
            return x
        key = jax.random.key(seed)
        ks = jax.random.split(key, 6)
        return {'x': jax.random.normal(ks[0], (B, N, DIM), jnp.float32), 'wqkv': jax.random.normal(ks[1], (DEPTH, DIM, 3 * INNER), jnp.float32) * 0.02, 'q_scale': jnp.ones((DEPTH, DIM_HEAD), jnp.float32), 'k_scale': jnp.ones((DEPTH, DIM_HEAD), jnp.float32), 'wo': jax.random.normal(ks[2], (DEPTH, INNER, DIM), jnp.float32) * 0.02, 'ln_g': jnp.ones((DEPTH, DIM), jnp.float32), 'ln_b': jnp.zeros((DEPTH, DIM), jnp.float32), 'w1': jax.random.normal(ks[3], (DEPTH, DIM, 2 * HID), jnp.float32) * 0.02, 'b1': jnp.zeros((DEPTH, 2 * HID), jnp.float32), 'w2': jax.random.normal(ks[4], (DEPTH, HID, DIM), jnp.float32) * 0.02, 'b2': jnp.zeros((DEPTH, DIM), jnp.float32)}
    _L0_ffn_in = _L0_ffn_setup()
    _d = {'L0_attn_x': _L0_attn_in['x'], 'L0_ffn_wqkv': _L0_ffn_in['wqkv'], 'L0_ffn_q_scale': _L0_ffn_in['q_scale'], 'L0_ffn_k_scale': _L0_ffn_in['k_scale'], 'L0_ffn_wo': _L0_ffn_in['wo'], 'L0_ffn_ln_g': _L0_ffn_in['ln_g'], 'L0_ffn_ln_b': _L0_ffn_in['ln_b'], 'L0_ffn_w1': _L0_ffn_in['w1'], 'L0_ffn_b1': _L0_ffn_in['b1'], 'L0_ffn_w2': _L0_ffn_in['w2'], 'L0_ffn_b2': _L0_ffn_in['b2']}
    _x0 = _d['L0_attn_x']
    _d['L0_attn_x'] = jax.random.normal(jax.random.fold_in(jax.random.key(seed), 1), (8, 256, 128), dtype=_x0.dtype)
    del _x0
    return _d

def reference(L0_attn_x, L0_ffn_wqkv, L0_ffn_q_scale, L0_ffn_k_scale, L0_ffn_wo, L0_ffn_ln_g, L0_ffn_ln_b, L0_ffn_w1, L0_ffn_b1, L0_ffn_w2, L0_ffn_b2):

    def _L0_attn_ref(x):
        import jax, jax.numpy as jnp
        import numpy as np
        D_MODEL = 128
        NUM_HEADS = 16
        HEAD_DIM = D_MODEL // NUM_HEADS
        DILATION = 2
        SEGMENT = 128
        OFFSET = 0
        b, n, d = x.shape
        n_seg = n // SEGMENT
        k = SEGMENT // DILATION
        local_idx = OFFSET + DILATION * jnp.arange(k)
        global_idx = SEGMENT * jnp.arange(n_seg)[:, None] + local_idx[None, :]
        xs = x[:, global_idx, :]
        qh = xs.reshape(b, n_seg, k, NUM_HEADS, HEAD_DIM)
        scale = 1.0 / jnp.sqrt(jnp.asarray(HEAD_DIM, dtype=xs.dtype))
        scores = jnp.einsum('bsqhd,bskhd->bshqk', qh, qh) * scale
        attn = jax.nn.softmax(scores, axis=-1)
        seg_out = jnp.einsum('bshqk,bskhd->bsqhd', attn, qh)
        a_os = seg_out.reshape(b, n_seg * k, d)
        idx = jnp.broadcast_to(global_idx.reshape(-1), (b, n_seg * k))
        a_denoms = a_os.sum(axis=-1)

        def mix(o_b, den_b, idx_b):
            sums = jnp.zeros((n,), o_b.dtype).at[idx_b].add(den_b)
            alphas = den_b / sums[idx_b]
            return jnp.zeros((n, d), o_b.dtype).at[idx_b].add(o_b * alphas[:, None])
        return jax.vmap(mix)(a_os, a_denoms, idx)

    def _L0_ffn_ref(x, wqkv, q_scale, k_scale, wo, ln_g, ln_b, w1, b1, w2, b2):
        import jax, jax.numpy as jnp
        import numpy as np
        DIM = 128
        DEPTH = 2
        HEADS = 8
        DIM_HEAD = 64
        WINDOW = 64
        INNER = HEADS * DIM_HEAD
        HID = int(DIM * 4 * 2 / 3)
        B, N = (2, 1024)
        QK_SCALE = 8.0

        def shift_token(t):
            t1, t2 = jnp.split(t, 2, axis=-1)
            t2 = jnp.pad(t2, ((0, 0), (1, 0), (0, 0)))[:, :-1]
            return jnp.concatenate([t1, t2], axis=-1)

        def l2norm(t):
            return t / jnp.clip(jnp.linalg.norm(t, axis=-1, keepdims=True), 1e-12)

        def rotate_half(x):
            x1, x2 = jnp.split(x, 2, axis=-1)
            return jnp.concatenate([-x2, x1], axis=-1)

        def rotary_xpos(q, k):
            n = q.shape[-2]
            half_idx = jnp.arange(0, DIM_HEAD, 2, dtype=jnp.float32)
            inv_freq = 1.0 / 10000.0 ** (half_idx / DIM_HEAD)
            t = jnp.arange(n, dtype=jnp.float32)
            freqs = t[:, None] * inv_freq[None, :]
            freqs = jnp.concatenate([freqs, freqs], axis=-1)
            base = (half_idx + 0.4 * DIM_HEAD) / (1.4 * DIM_HEAD)
            power = (t - n // 2) / float(WINDOW // 2)
            scale = base[None, :] ** power[:, None]
            scale = jnp.concatenate([scale, scale], axis=-1)
            cos, sin = (jnp.cos(freqs), jnp.sin(freqs))
            q = q * cos * scale + rotate_half(q) * sin * scale
            k = k * cos / scale + rotate_half(k) * sin / scale
            return (q, k)

        def local_attention(q, k, v):
            b, h, n, d = q.shape
            w = n // WINDOW
            bq = q.reshape(b, h, w, WINDOW, d) * QK_SCALE
            bk = k.reshape(b, h, w, WINDOW, d)
            bv = v.reshape(b, h, w, WINDOW, d)

            def look_around(t):
                p = jnp.pad(t, ((0, 0), (0, 0), (1, 0), (0, 0), (0, 0)))
                return jnp.concatenate([p[:, :, :w], p[:, :, 1:]], axis=3)
            bk, bv = (look_around(bk), look_around(bv))
            bt = jnp.arange(n).reshape(w, WINDOW)
            btp = jnp.pad(bt, ((1, 0), (0, 0)), constant_values=-1)
            btk = jnp.concatenate([btp[:w], btp[1:]], axis=1)
            sim = jnp.einsum('bhwid,bhwjd->bhwij', bq, bk)
            i = bt[:, :, None]
            j = btk[:, None, :]
            mask = (i < j) | (i > j + WINDOW) | (j == -1)
            sim = jnp.where(mask, -jnp.finfo(sim.dtype).max, sim)
            attn = jax.nn.softmax(sim, axis=-1)
            out = jnp.einsum('bhwij,bhwjd->bhwid', attn, bv)
            return out.reshape(b, h, n, d)

        def _layer(x, wqkv, qs, ksc, wo, lg, lb, w1, b1, w2, b2):
            b, n, _ = x.shape
            h = shift_token(x)
            qkv = h @ wqkv
            q, k, v = jnp.split(qkv, 3, axis=-1)
            to_heads = lambda t: t.reshape(b, n, HEADS, DIM_HEAD).transpose(0, 2, 1, 3)
            q, k, v = (to_heads(q), to_heads(k), to_heads(v))
            q = l2norm(q) * qs
            k = l2norm(k) * ksc
            q, k = rotary_xpos(q, k)
            o = local_attention(q, k, v)
            o = o.transpose(0, 2, 1, 3).reshape(b, n, INNER)
            x = x + o @ wo
            h = shift_token(x)
            mu = h.mean(-1, keepdims=True)
            var = h.var(-1, keepdims=True)
            h = (h - mu) / jnp.sqrt(var + 1e-05) * lg + lb
            h = h @ w1 + b1
            a, g = jnp.split(h, 2, axis=-1)
            h = a * jax.nn.gelu(g, approximate=False)
            x = x + h @ w2 + b2
            return x
        for l in range(DEPTH):
            x = _layer(x, wqkv[l], q_scale[l], k_scale[l], wo[l], ln_g[l], ln_b[l], w1[l], b1[l], w2[l], b2[l])
        return x
    x = L0_attn_x
    x = _layernorm(x + _L0_attn_ref(x), axis=-1)
    x = _layernorm(x + _L0_ffn_ref(x, L0_ffn_wqkv, L0_ffn_q_scale, L0_ffn_k_scale, L0_ffn_wo, L0_ffn_ln_g, L0_ffn_ln_b, L0_ffn_w1, L0_ffn_b1, L0_ffn_w2, L0_ffn_b2), axis=-1)
    return x

_drawn_inputs = setup_inputs


def setup_inputs(seed=0):
    import zlib

    import numpy as np

    out = dict(_drawn_inputs(seed))
    spreads = {'L0_ffn_q_scale': (1.0, 0.6),
     'L0_ffn_k_scale': (1.0, 0.6),
     'L0_ffn_ln_g': (1.0, 0.6),
     'L0_ffn_ln_b': (0.0, 0.8),
     'L0_ffn_b1': (0.0, 0.8),
     'L0_ffn_b2': (0.0, 0.456)}
    factors = {'L0_ffn_wqkv': 3.314, 'L0_ffn_wo': 3.306, 'L0_ffn_w1': 6.216, 'L0_ffn_w2': 6.114}
    for name, (base, spread) in spreads.items():
        noise = np.random.default_rng([zlib.crc32(name.encode()), seed]).standard_normal(out[name].shape)
        drawn = base * np.exp(spread * noise) if base else spread * noise
        out[name] = jnp.asarray(drawn.astype(out[name].dtype))
    for name, factor in factors.items():
        out[name] = (out[name] * factor).astype(out[name].dtype)
    return out
```

```python
from contextlib import ExitStack

import concourse.bass as bass
from concourse import mybir

ALU = mybir.AluOpType
ACT = mybir.ActivationFunctionType
AX = mybir.AxisListType
F32 = mybir.dt.float32
BF16 = mybir.dt.bfloat16

P = 128
BATCH, SEQ, DIM = 8, 256, 128
TILES = SEQ // P
DEPTH, HEADS, DH, WINDOW = 2, 8, 64, 64
INNER = HEADS * DH
BLOCKS = INNER // P
HID = int(DIM * 4 * 2 / 3)
CHUNK = -(-HID // 3)
CHUNKS = [(c * CHUNK, min(CHUNK, HID - c * CHUNK)) for c in range(3)]
STEPS = DEPTH * BATCH
QK_SCALE = 8.0
A_HEADS, A_DH = 16, 8
A_KEYS = 64
A_PAIRS = A_HEADS // 2
EPS = 1e-5
MASKED = -1e30
NORM_FLOOR = 1e-24


def table_constants():
    import numpy as np
    half = np.arange(0, DH, 2, dtype=np.float32)
    inv_freq = (1.0 / np.float32(10000.0) ** (half / np.float32(DH))).astype(np.float32)
    t = np.arange(SEQ, dtype=np.float32)
    freqs = (t[:, None] * inv_freq[None, :]).astype(np.float32)
    freqs = np.concatenate([freqs, freqs], axis=-1).astype(np.float64)
    base = (half + 0.4 * DH) / (1.4 * DH)
    scale = base[None, :].astype(np.float64) ** ((t - SEQ // 2) / float(WINDOW // 2))[:, None]
    scale = np.concatenate([scale, scale], axis=-1)
    sign = np.where(np.arange(DH) < DH // 2, -1.0, 1.0)[None, :]
    kinds = [np.cos(freqs) * scale, sign * np.sin(freqs) * scale,
             np.cos(freqs) / scale, sign * np.sin(freqs) / scale]
    rotary = np.stack(kinds, axis=1).reshape(TILES, P, 4, DH).transpose(1, 0, 2, 3)
    r = np.arange(P)[:, None]
    c = np.arange(P)[None, :]
    even = np.where(c < 64, c <= r, c - 64 >= r)
    odd = np.where(c < 64, c >= r - 64, c - 64 <= r - 64)
    allowed = np.stack([np.where(r < 64, even, odd)] * TILES, axis=1)
    allowed[:64, 0, 64:] = False
    mask = np.where(allowed, 0.0, MASKED)
    ident = np.eye(P)
    group = (np.arange(P)[:, None] // A_DH) % 4 == np.arange(4)[None, :]
    return {"rotary": np.ascontiguousarray(rotary, np.float32), "mask": mask.astype(np.float32),
            "ident": ident.astype(np.float32), "group": group.astype(np.float32)}


def build(nc, x, wqkv, q_scale, k_scale, wo, ln_g, ln_b, w1, b1, w2, b2,
          c_rotary, c_mask, c_ident, c_group, out):
    with ExitStack() as ctx:
        def sb(name, shape, dt=F32):
            return ctx.enter_context(nc.sbuf_tensor(name, shape, dt))

        def psum(name, shape):
            return ctx.enter_context(nc.psum_tensor(name, shape, F32))

        def sem(name):
            return ctx.enter_context(nc.semaphore(name))

        def sem2(name):
            return [sem(f"{name}{t}") for t in range(2)]

        banks = psum("banks", [P, 8, 512])
        bank_q, bank_k, bank_v = (banks[:, i, :] for i in range(3))
        bank_s = banks[:, 3:5, :]
        bank_t0, bank_t1, bank_o = (banks[:, i, :] for i in range(5, 8))
        bank_as = banks[:, 1:5, 0:4 * A_KEYS]
        SLOT = [4 * (h % 2) + h // 2 for h in range(HEADS)]

        ident = sb("ident", [P, P])
        ident_bf = sb("ident_bf", [P, P], BF16)
        mask32 = sb("mask32", [P, TILES, P])
        mask_bf = sb("mask_bf", [P, TILES, P], BF16)
        rot_const = sb("rot_const", [P, TILES, 4, DH])
        rot_tab = sb("rot_tab", [P, DEPTH, TILES, 4, DH])
        head_scale = sb("head_scale", [P, DEPTH, 2, DH])
        group = sb("group", [P, 4])
        minus_half = sb("minus_half", [P, 16])
        wqkv_sb = sb("wqkv_sb", [P, DEPTH, 3, INNER])
        wo_sb = sb("wo_sb", [P, DEPTH, BLOCKS, DIM])
        w2_sb = sb("w2_sb", [CHUNK, DEPTH, 3, DIM])
        w1_sb = sb("w1_sb", [P, 2 * HID])
        ln_gb = sb("ln_gb", [P, 2])
        b1_sb = sb("b1_sb", [CHUNK, 2, 3])
        b2_sb = sb("b2_sb", [P, DIM])

        X = sb("X", [P, (DEPTH + 1) * BATCH, TILES, DIM])

        a_x = sb("a_x", [P, BATCH, 2, DIM])
        a_xv = sb("a_xv", [P, BATCH, 2, DIM])
        a_in = sb("a_in", [P, DIM])
        a_xT = sb("a_xT", [P, P])
        a_xTg = sb("a_xTg", [P, 2, 4, A_KEYS])
        a_max = sb("a_max", [P, A_HEADS])
        a_dif = sb("a_dif", [P, A_HEADS, A_KEYS])
        a_exp = sb("a_exp", [P, A_HEADS, A_KEYS])
        a_expT = sb("a_expT", [P, A_PAIRS, P])
        a_v = sb("a_v", [P, 2, A_PAIRS, 2, A_DH + 1])
        a_rec = sb("a_rec", [P, A_HEADS])
        a_o = sb("a_o", [P, A_HEADS, A_DH])
        a_den = sb("a_den", [P, 1])
        a_rden = sb("a_rden", [P, 1])
        a_alpha = sb("a_alpha", [P, 1])
        a_y = sb("a_y", [P, DIM])
        a_st = sb("a_st", [P, 2, 6])
        a_mv = sb("a_mv", [P, 2, 2])
        a_ve = sb("a_ve", [P, 2])
        a_rstd = sb("a_rstd", [P, 2])
        a_xn = sb("a_xn", [P, BATCH, 2, DIM])

        xs = sb("xs", [P, TILES, DIM])
        hT = sb("hT", [P, SEQ])
        rot_c = [sb(f"rot_c{i}", [P, 2, INNER]) for i in range(2)]
        rot_s = [sb(f"rot_s{i}", [P, 2, INNER]) for i in range(2)]
        squares = sb("squares", [P, 2, INNER])
        ss = sb("ss", [P, 2 * HEADS])
        ssf = sb("ssf", [P, 2 * HEADS])
        rnorm = [sb(f"rnorm{i}", [P, 2 * HEADS]) for i in range(2)]
        qrot = [sb(f"qrot{i}", [P, INNER]) for i in range(2)]
        krot = [sb(f"krot{i}", [P, INNER]) for i in range(2)]
        knorm = [sb(f"knorm{i}", [P, INNER]) for i in range(2)]
        qT = [sb(f"qT{i}", [P, BLOCKS, P]) for i in range(2)]
        kT = sb("kT", [P, BLOCKS, SEQ])
        sc8 = [sb(f"sc8_{i}", [P, HEADS]) for i in range(2)]
        smax = [sb(f"smax{i}", [P, HEADS]) for i in range(2)]
        nbias = [sb(f"nbias{i}", [P, HEADS]) for i in range(2)]
        probs = [sb(f"probs{i}", [P, HEADS, P]) for i in range(2)]
        psums = [sb(f"psums{i}", [P, HEADS]) for i in range(2)]
        rsums = [sb(f"rsums{i}", [P, HEADS]) for i in range(2)]
        probsT = sb("probsT", [P, HEADS, P])
        V0 = sb("V0", [P, INNER])
        V1_next = sb("V1_next", [P, INNER])
        V1 = sb("V1", [P, INNER])
        Vmix = sb("Vmix", [P, INNER])
        o_sb = sb("o_sb", [P, INNER])
        oT = sb("oT", [P, BLOCKS, P])
        x1 = sb("x1", [P, TILES, DIM])
        x1b = sb("x1b", [P, TILES, DIM])
        h2 = sb("h2", [P, TILES, DIM])
        h2n = sb("h2n", [P, TILES, DIM])
        st = sb("st", [P, TILES, 6])
        mv = sb("mv", [P, TILES, 2])
        ve = sb("ve", [P, TILES])
        rstd = sb("rstd", [P, TILES])
        h2T = sb("h2T", [P, SEQ])
        gelu = sb("gelu", [CHUNK, 3, SEQ])
        gated = sb("gated", [CHUNK, 3, SEQ])
        f_y = sb("f_y", [P, 2, TILES, DIM])
        f_st = sb("f_st", [P, 2, TILES, 6])
        f_mv = sb("f_mv", [P, 2, TILES, 2])
        f_ve = sb("f_ve", [P, 2, TILES])
        f_rstd = sb("f_rstd", [P, 2, TILES])
        f_out = sb("f_out", [P, 2, TILES, DIM])

        s_ax = sem("s_ax")
        s_const = sem("s_const")
        s_wts = sem("s_wts")
        s_ffnw = sem("s_ffnw")
        s_zero = sem("s_zero")
        s_setup = sem("s_setup")
        s_bf = sem("s_bf")
        s_rot = sem("s_rot")
        s_ain = sem("s_ain")
        s_axT_ps = sem("s_axT_ps")
        s_axT = sem("s_axT")
        s_axTg = sem("s_axTg")
        s_as = sem("s_as")
        s_amax = sem("s_amax")
        s_adif = sem("s_adif")
        s_aexp = sem("s_aexp")
        s_aT_ps = sem2("s_aT_ps")
        s_aT = sem2("s_aT")
        s_av = sem("s_av")
        s_ao_ps = sem("s_ao_ps")
        s_arec = sem("s_arec")
        s_ao = sem("s_ao")
        s_aden = sem("s_aden")
        s_arden = sem("s_arden")
        s_aalpha = sem("s_aalpha")
        s_ay = sem("s_ay")
        s_ast = sem("s_ast")
        s_amv = sem("s_amv")
        s_ave = sem("s_ave")
        s_arstd = sem("s_arstd")
        s_axn = sem("s_axn")
        s_ax_dma = sem("s_ax_dma")
        x_ready = sem("x_ready")
        s_xs = sem("s_xs")
        s_hT_ps = sem("s_hT_ps")
        s_hT = sem("s_hT")
        s_q_ps, s_k_ps, s_v_ps = sem2("s_q_ps"), sem2("s_k_ps"), sem2("s_v_ps")
        s_q_rotd, s_k_rotd = sem2("s_q_rotd"), sem2("s_k_rotd")
        s_q_sq, s_k_sq = sem2("s_q_sq"), sem2("s_k_sq")
        s_v = sem2("s_v")
        s_vmix = sem("s_vmix")
        s_ss, s_ssf, s_rnorm = sem2("s_ss"), sem2("s_ssf"), sem2("s_rnorm")
        s_qrot, s_krot, s_knorm = sem2("s_qrot"), sem2("s_krot"), sem2("s_knorm")
        s_qT_ps, s_kT_ps, s_qT, s_kT = sem2("s_qT_ps"), sem2("s_kT_ps"), sem2("s_qT"), sem2("s_kT")
        s_s_ps = sem2("s_s_ps")
        s_sc8, s_smax, s_nbias = sem2("s_sc8"), sem2("s_smax"), sem2("s_nbias")
        s_pa, s_pb = sem2("s_pa"), sem2("s_pb")
        s_paT_ps, s_pbT_ps, s_paT, s_pbT = sem2("s_paT_ps"), sem2("s_pbT_ps"), sem2("s_paT"), sem2("s_pbT")
        s_o_ps, s_rsum, s_o = sem2("s_o_ps"), sem2("s_rsum"), sem2("s_o")
        s_oT_ps, s_oT, s_wo_ps, s_x1 = sem2("s_oT_ps"), sem2("s_oT"), sem2("s_wo_ps"), sem2("s_x1")
        s_h2 = sem("s_h2")
        s_x1b = sem("s_x1b")
        s_st, s_mv, s_ve, s_rstd, s_h2n = sem("s_st"), sem("s_mv"), sem("s_ve"), sem("s_rstd"), sem("s_h2n")
        s_h2T_ps, s_h2T = sem("s_h2T_ps"), sem("s_h2T")
        s_params = sem("s_params")
        s_w1_ps, s_gelu, s_gated = ([sem(f"{n}{c}") for c in range(3)] for n in ("s_w1_ps", "s_gelu", "s_gated"))
        s_w2_ps = sem("s_w2_ps")
        s_fy, s_fst, s_fmv, s_fve, s_frstd, s_fout, s_fdma = (
            sem2(n) for n in ("s_fy", "s_fst", "s_fmv", "s_fve", "s_frstd", "s_fout", "s_fdma"))

        def exists(n):
            return not isinstance(n, int) or 0 <= n < STEPS

        def layer(n):
            return n // BATCH

        def heads(ap):
            return ap.rearrange("p (h d) -> p h d", h=HEADS)

        AFTER_SETUP = 3

        def walk(eng, body, first=0, split=None):
            for u in range(-1, AFTER_SETUP):
                body(u)
            with eng.Fori(AFTER_SETUP, STEPS - 1) as u:
                body(u)
            for u in range(STEPS - 1, STEPS + 3):
                body(u)

        def ffn_weights(eng, l):
            eng.dma_start(w1_sb[:, :], w1[l]).then_inc(s_ffnw, 16)
            eng.dma_start(ln_gb[:, 0:1], ln_g[l].rearrange("(p o) -> p o", o=1)).then_inc(s_ffnw, 16)
            eng.dma_start(ln_gb[:, 1:2], ln_b[l].rearrange("(p o) -> p o", o=1)).then_inc(s_ffnw, 16)
            for half in range(2):
                for c, (at, size) in enumerate(CHUNKS):
                    eng.dma_start(b1_sb[0:size, half, c:c + 1],
                                  b1[l, half * HID + at:half * HID + at + size].rearrange("(p o) -> p o", o=1)
                                  ).then_inc(s_ffnw, 16)
            eng.dma_start(b2_sb[:, :], b2[l].partition_broadcast(P)).then_inc(s_ffnw, 16)

        FFN_DMAS = 10
        CONST_DMAS = 6
        WTS_DMAS = 6

        block = ctx.enter_context(nc.Block())

        @block.sync
        def _(sp):
            xq = x.rearrange("b (q two) d -> q b two d", two=2)
            sp.dma_start(a_x[:, :, :, :], xq).then_inc(s_ax, 16)
            sp.dma_start(ident[:, :], c_ident).then_inc(s_const, 16)
            sp.dma_start(group[:, :], c_group).then_inc(s_const, 16)
            xv = x.rearrange("b (s j two) d -> j b s two d", s=2, two=2)[:, :, :, 0, :]
            for half in range(2):
                for s in range(2):
                    sp.dma_start(a_xv[64 * half:64 * half + 64, :, s, :], xv[:, :, s, :]).then_inc(s_ax, 16)
            sp.dma_start(mask32[:, :, :], c_mask).then_inc(s_const, 16)
            sp.dma_start(rot_const[:, :, :, :], c_rotary).then_inc(s_const, 16)
            sp.dma_start(head_scale[:, :, 0, :], q_scale.partition_broadcast(P)).then_inc(s_const, 16)
            sp.dma_start(head_scale[:, :, 1, :], k_scale.partition_broadcast(P)).then_inc(s_const, 16)
            for l in range(DEPTH):
                sp.dma_start(wqkv_sb[:, l, :, :], wqkv[l].rearrange("p (k n) -> p k n", k=3)).then_inc(s_wts, 16)
            sp.dma_start(wo_sb[:, :, :, :].rearrange("p l k n -> p (l k) n"),
                         wo.rearrange("l (k p) n -> p (l k) n", p=P)).then_inc(s_wts, 16)
            for l in range(DEPTH):
                sp.dma_start(w2_sb[:, l, 0:2, :],
                             w2[l, 0:2 * CHUNK, :].rearrange("(c p) n -> p c n", p=CHUNK)).then_inc(s_wts, 16)
            sp.dma_start(w2_sb[0:HID - 2 * CHUNK, :, 2, :],
                         w2[:, 2 * CHUNK:HID, :].rearrange("l p n -> p l n")).then_inc(s_wts, 16)
            ffn_weights(sp, 0)

            with sp.Fori(0, BATCH) as b:
                sp.wait_ge(s_axn, b + 1)
                for s in range(2):
                    for odd in range(2):
                        sp.dma_start(X[odd:P:2, bass.ds(b, 1), s, :],
                                     a_xn[64 * s:64 * s + 64, bass.ds(b, 1), odd, :]).then_inc(s_ax_dma, 16)
                sp.wait_ge(s_ax_dma, 64 * b + 64)
                sp.sem_inc(x_ready, 1)

            def body(n):
                o = n - 3
                if exists(n):
                    sp.wait_ge(x_ready, n + 1)
                    if exists(n - 1):
                        sp.wait_ge(s_hT_ps, n)
                    sp.dma_start(xs[:, :, :], X[:, bass.ds(n, 1), :, :].rearrange("p o t d -> p (o t) d")
                                 ).then_inc(s_xs, 16)
                if exists(o):
                    if exists(o - 1):
                        sp.wait_ge(s_h2n, o)
                    sp.sem_inc(s_params, 1)
                    sp.wait_ge(s_x1[0], o + 1)
                    sp.wait_ge(s_x1[1], o + 1)
                    sp.dma_start(h2[:, :, 0:64], x1[:, :, 0:64]).then_inc(s_h2, 16)
                    sp.dma_start(h2[1:P, :, 64:DIM], x1[0:P - 1, :, 64:DIM]).then_inc(s_h2, 16)
                    sp.dma_start(h2[0:1, 1, 64:DIM], x1[P - 1:P, 0, 64:DIM]).then_inc(s_h2, 16)

            sp.wait_ge(s_ffnw, 16 * FFN_DMAS)
            switch = BATCH + 3
            for n in range(0, AFTER_SETUP + 1):
                body(n)
            with sp.Fori(AFTER_SETUP + 1, switch) as n:
                body(n)
            sp.wait_ge(s_x1b, BATCH)
            for c in range(3):
                sp.wait_ge(s_gated[c], BATCH)
            ffn_weights(sp, 1)
            sp.wait_ge(s_ffnw, 32 * FFN_DMAS)
            with sp.Fori(switch, STEPS) as n:
                body(n)
            for n in range(STEPS, STEPS + 3):
                body(n)

            out_v = out.rearrange("b (t p) d -> p b t d", p=P)
            with sp.Fori(0, BATCH // 2) as v:
                for i in range(2):
                    sp.wait_ge(s_fout[i], v + 1)
                    sp.dma_start(out_v[:, bass.ds(2 * v + i, 1), :, :].rearrange("p o t d -> p (o t) d"),
                                 f_out[:, i, :, :]).then_inc(s_fdma[i], 16)
            for i in range(2):
                sp.wait_ge(s_fdma[i], 16 * (BATCH // 2))

        @block.gpsimd
        def _(pool):
            pool.wait_ge(s_const, 16 * CONST_DMAS)
            for l in range(DEPTH):
                for t in range(TILES):
                    for kind in range(4):
                        scale = head_scale[:, l, kind // 2, :]
                        table, to = rot_const[:, t, kind, :], rot_tab[:, l, t, kind, :]
                        if kind % 2:
                            scale, table, to = (a.rearrange("p (s d) -> p s d", s=2) for a in (scale, table, to))
                            scale = scale[:, ::-1, :]
                        nc.gpsimd.tensor_tensor(to, table, scale, ALU.mult).then_inc(s_rot, 1)

            pool.wait_ge(s_setup, 5)
            with pool.Fori(0, BATCH) as b:
                pool.wait_ge(s_ave, b + 1)
                nc.gpsimd.tensor_tensor(a_rstd[:, :], a_ve[:, :], minus_half[:, 0:2], ALU.pow).then_inc(s_arstd, 1)

            def rotated(n, t):
                pool.wait_ge(s_q_rotd[t], n + 1)
                if exists(n - 1):
                    pool.wait_ge(s_qT_ps[t], n)
                nc.gpsimd.tensor_tensor(qrot[t][:, :], rot_c[t][:, 0, :], rot_s[t][:, 0, :], ALU.add
                                        ).then_inc(s_qrot[t], 1)
                pool.wait_ge(s_k_rotd[t], n + 1)
                nc.gpsimd.tensor_tensor(krot[t][:, :], rot_c[t][:, 1, :], rot_s[t][:, 1, :], ALU.add
                                        ).then_inc(s_krot[t], 1)
                pool.wait_ge(s_ssf[t], n + 1)
                if exists(n - 1):
                    pool.wait_ge(s_sc8[t], n)
                nc.gpsimd.tensor_tensor(rnorm[t][:, :], ssf[:, :], minus_half[:, :], ALU.pow).then_inc(s_rnorm[t], 1)
                pool.wait_ge(s_rnorm[t], n + 1)
                pool.wait_ge(s_krot[t], n + 1)
                if exists(n - 1):
                    pool.wait_ge(s_kT_ps[t], n)
                nc.gpsimd.tensor_tensor(heads(knorm[t][:, :]), heads(krot[t][:, :]),
                                        rnorm[t][:, HEADS:].unsqueeze(2).broadcast_to([P, HEADS, DH]), ALU.mult
                                        ).then_inc(s_knorm[t], 1)

            def body(u):
                o = u - 2
                if exists(u):
                    rotated(u, 0)
                if exists(o):
                    pool.wait_ge(s_x1[0], o + 1)
                    pool.wait_ge(s_x1[1], o + 1)
                    pool.wait_ge(s_params, o + 1)
                    if exists(o - 1):
                        pool.wait_ge(x_ready, BATCH + o)
                    nc.gpsimd.tensor_tensor(x1b[:, :, :], x1[:, :, :],
                                            b2_sb[:, :].unsqueeze(1).broadcast_to([P, TILES, DIM]), ALU.add
                                            ).then_inc(s_x1b, 1)
                if exists(u):
                    rotated(u, 1)
                if exists(o):
                    pool.wait_ge(s_ve, o + 1)
                    nc.gpsimd.tensor_tensor(rstd[:, :], ve[:, :], minus_half[:, 0:TILES], ALU.pow).then_inc(s_rstd, 1)

            walk(pool, body)

            with pool.Fori(0, BATCH // 2) as v:
                for i in range(2):
                    pool.wait_ge(s_fve[i], v + 1)
                    nc.gpsimd.tensor_tensor(f_rstd[:, i, :], f_ve[:, i, :], minus_half[:, 0:TILES], ALU.pow
                                            ).then_inc(s_frstd[i], 1)

        @block.tensor
        def _(pe):
            def a_scores(b):
                pe.wait_ge(s_ain, b + 1)
                nc.tensor.transpose(bank_q[:, 0:P], a_in[:, :], ident[:, :]).then_inc(s_axT_ps, 1)
                pe.wait_ge(s_axT, b + 1)
                pe.wait_ge(s_axTg, b + 1)
                if exists(b - 1):
                    pe.wait_ge(s_adif, b)
                for s in range(2):
                    for g in range(4):
                        dims = slice(32 * g, 32 * g + 32)
                        last = nc.tensor.matmul(
                            bank_as[64 * s:64 * s + 64, g, :],
                            a_xT[dims, 64 * s:64 * s + 64],
                            a_xTg[dims, s, :, :].rearrange("p m j -> p (m j)"), start=True, stop=True)
                last.then_inc(s_as, 1)

            def a_values(b):
                pe.wait_ge(s_aexp, b + 1)
                for half, bank in ((0, bank_t0), (1, bank_t1)):
                    if exists(b - 1):
                        pe.wait_ge(s_aT[half], b)
                    for j in range(4):
                        pair = 4 * half + j
                        last = nc.tensor.transpose(
                            bank[:, P * j:P * j + P],
                            a_exp[:, 2 * pair:2 * pair + 2, :].rearrange("p h j -> p (h j)"), ident[:, :])
                    last.then_inc(s_aT_ps[half], 1)
                pe.wait_ge(s_av, b + 1)
                if exists(b - 1):
                    pe.wait_ge(s_ao, b)
                for half in range(2):
                    pe.wait_ge(s_aT[half], b + 1)
                    for pair in range(4 * half, 4 * half + 4):
                        for s in range(2):
                            last = nc.tensor.matmul(
                                bank_o[64 * s:64 * s + 64, 18 * pair:18 * pair + 18],
                                a_expT[:, pair, 64 * s:64 * s + 64],
                                a_v[:, s, pair, :, :].rearrange("p h d -> p (h d)"), start=True, stop=True)
                last.then_inc(s_ao_ps, 1)

            pe.wait_ge(s_const, 16 * CONST_DMAS)
            pe.wait_ge(s_setup, 5)
            a_scores(0)
            a_scores(1)
            a_values(0)
            with pe.Fori(1, BATCH - 1) as b:
                a_scores(b + 1)
                a_values(b)
            a_values(BATCH - 1)

            def transpose_h(n):
                pe.wait_ge(s_xs, 16 * n + 16)
                if exists(n - 2):
                    pe.wait_ge(s_oT[0], n - 1)
                elif exists(n - 1):
                    pe.wait_ge(s_hT, n)
                else:
                    pe.wait_ge(s_aT[1], BATCH)
                for t in range(TILES):
                    last = nc.tensor.transpose(bank_t1[:, P * t:P * t + P], xs[:, t, :], ident[:, :])
                last.then_inc(s_hT_ps, 1)

            def project(n, t, which):
                bank, done = [(bank_q, s_q_ps), (bank_k, s_k_ps), (bank_v, s_v_ps)][which]
                pe.wait_ge(s_hT, n + 1)
                if which == 0:
                    if t == 1:
                        pe.wait_ge(s_q_sq[0], n + 1)
                    elif exists(n - 1):
                        pe.wait_ge(s_q_sq[1], n)
                elif which == 1:
                    if t == 1:
                        pe.wait_ge(s_k_sq[0], n + 1)
                    elif exists(n - 1):
                        pe.wait_ge(s_k_sq[1], n)
                else:
                    if t == 0:
                        pe.wait_ge(s_v[1], n + 1)
                    elif exists(n - 1):
                        pe.wait_ge(s_v[0], n)
                if t == 0 and which < 2 and exists(n - 3):
                    pe.wait_ge(s_gated[which], n - 2)
                if t == 1 and which == 2 and exists(n - 3):
                    pe.wait_ge(s_gated[which], n - 2)
                nc.tensor.matmul(bank[:, :], hT[:, P * t:P * t + P],
                                 wqkv_sb[:, bass.ds(layer(n), 1), which, :].rearrange("p o n -> p (o n)"),
                                 start=True, stop=True).then_inc(done[t], 1)

            def transpose_qk(n, t):
                for src, ready, bank, done in ((qrot[t], s_qrot, bank_t0, s_qT_ps),
                                               (knorm[t], s_knorm, bank_t1, s_kT_ps)):
                    pe.wait_ge(ready[t], n + 1)
                    if bank is bank_t0:
                        if t == 0 and exists(n - 1):
                            pe.wait_ge(s_x1[0], n)
                        if t == 1:
                            if exists(n - 1):
                                pe.wait_ge(s_paT[1], n)
                            pe.wait_ge(s_qT[0], n + 1)
                    else:
                        if t == 0:
                            pe.wait_ge(s_hT, (n + 2) if exists(n + 1) else STEPS)
                        if t == 1:
                            if exists(n - 1):
                                pe.wait_ge(s_pbT[1], n)
                            pe.wait_ge(s_kT[0], n + 1)
                    for j in range(BLOCKS):
                        last = nc.tensor.transpose(bank[:, P * j:P * j + P], src[:, P * j:P * j + P], ident[:, :])
                    last.then_inc(done[t], 1)

            def scores(n, t):
                pe.wait_ge(s_qT[t], n + 1)
                pe.wait_ge(s_kT[t], n + 1)
                if t == 1:
                    pe.wait_ge(s_pb[0], n + 1)
                elif exists(n - 1):
                    pe.wait_ge(s_pb[1], n)
                for half in range(2):
                    nc.tensor.matmul(bank_s[:, half, :].rearrange("p (h j) -> p h j", h=4), ident_bf[:, :],
                                     mask_bf[:, t, :].unsqueeze(1).broadcast_to([P, 4, P]),
                                     start=True, stop=False, skip_group_check=True)
                for h in range(HEADS):
                    dims = slice(64 * (h % 2), 64 * (h % 2) + 64)
                    bank, col = bank_s[:, h % 2, :], P * (h // 2)
                    keys = kT[dims, h // 2, :].rearrange("p (w j) -> p w j", j=64)
                    if t == 0:
                        even, width = keys[:, 0:1, :], 64
                    else:
                        even, width = keys[:, 2:0:-1, :], P
                    nc.tensor.matmul(bank[0:64, col:col + width].rearrange("p (w j) -> p w j", j=64),
                                     qT[t][dims, h // 2, 0:64], even,
                                     start=False, stop=True, skip_group_check=True)
                    last = nc.tensor.matmul(bank[64:P, col:col + P],
                                            qT[t][dims, h // 2, 64:P],
                                            kT[dims, h // 2, P * t:P * t + P],
                                            start=False, stop=True, skip_group_check=True)
                last.then_inc(s_s_ps[t], 1)

            def transpose_p(n, t):
                for half, (ready, bank, done) in enumerate(((s_pa, bank_t0, s_paT_ps), (s_pb, bank_t1, s_pbT_ps))):
                    pe.wait_ge(ready[t], n + 1)
                    if t == 1:
                        if exists(n + 1):
                            pe.wait_ge((s_qT, s_kT)[half][0], n + 2)
                        else:
                            pe.wait_ge((s_x1[0], s_oT[0])[half], n + 1)
                            pe.wait_ge(s_hT, STEPS)
                    else:
                        if exists(n - 1):
                            pe.wait_ge((s_oT, s_x1)[half][1], n)
                        pe.wait_ge((s_qT, s_kT)[half][1], n + 1)
                    for j in range(4):
                        last = nc.tensor.transpose(bank[:, P * j:P * j + P], probs[t][:, 4 * half + j, :], ident[:, :])
                    last.then_inc(done[t], 1)

            def attend(n, t):
                if t == 0:
                    pe.wait_ge(s_v[0], n + 1)
                    if exists(n - 1):
                        pe.wait_ge(s_o[1], n)
                else:
                    pe.wait_ge(s_vmix, n + 1)
                    pe.wait_ge(s_o[0], n + 1)
                    if exists(n - 1):
                        pe.wait_ge(x_ready, BATCH + n)
                for half in range(2):
                    pe.wait_ge((s_paT, s_pbT)[half][t], n + 1)
                    for h in range(half, HEADS, 2):
                        cols = slice(DH * h, DH * h + DH)
                        last = nc.tensor.matmul(bank_o[64:P, cols], probsT[:, SLOT[h], 64:P],
                                                (V1 if t else V0)[:, cols], start=True, stop=True)
                        if t == 1:
                            last = nc.tensor.matmul(bank_o[0:64, cols], probsT[:, SLOT[h], 0:64], Vmix[:, cols],
                                                    start=True, stop=True)
                if t == 0:
                    for h in range(HEADS):
                        cols = slice(DH * h, DH * h + DH)
                        last = nc.tensor.matmul(bank_o[0:64, cols], probsT[0:64, SLOT[h], 0:64], V0[0:64, cols],
                                                start=True, stop=True)
                last.then_inc(s_o_ps[t], 1)

            def transpose_o(n, t):
                bank = bank_t0 if t else bank_t1
                pe.wait_ge(s_o[t], n + 1)
                if t == 1:
                    pe.wait_ge(s_paT[1], n + 1)
                    if exists(n + 1):
                        pe.wait_ge(s_qT[1], n + 2)
                else:
                    pe.wait_ge(s_pbT[0], n + 1)
                    if exists(n - 1):
                        pe.wait_ge(s_pbT[1], n)
                for j in range(BLOCKS):
                    last = nc.tensor.transpose(bank[:, P * j:P * j + P], o_sb[:, P * j:P * j + P], ident[:, :])
                last.then_inc(s_oT_ps[t], 1)

            def project_o(n, t):
                bank = bank_t1 if t else bank_t0
                pe.wait_ge(s_oT[t], n + 1)
                if t == 1:
                    pe.wait_ge(s_pbT[1], n + 1)
                    if exists(n + 1):
                        pe.wait_ge(s_kT[1], n + 2)
                else:
                    pe.wait_ge(s_paT[0], n + 1)
                    if exists(n - 1):
                        pe.wait_ge(s_h2T, n)
                for j in range(BLOCKS):
                    last = nc.tensor.matmul(bank[:, 0:DIM], oT[:, j, :],
                                            wo_sb[:, bass.ds(layer(n), 1), j, :].rearrange("p o n -> p (o n)"),
                                            start=(j == 0), stop=(j == BLOCKS - 1))
                last.then_inc(s_wo_ps[t], 1)

            def transpose_h2(n):
                pe.wait_ge(s_h2n, n + 1)
                if exists(n + 1):
                    pe.wait_ge(s_paT[0], n + 2)
                pe.wait_ge(s_oT[1], n + 1)
                for t in range(TILES):
                    last = nc.tensor.transpose(bank_t0[:, P * t:P * t + P], h2n[:, t, :], ident[:, :])
                last.then_inc(s_h2T_ps, 1)

            def ffn_up(n):
                pe.wait_ge(s_params, n + 1)
                pe.wait_ge(s_h2T, n + 1)
                m = n + 2
                for c, (at, size) in enumerate(CHUNKS):
                    last_reader = (s_q_sq[1], s_k_sq[1], s_v[1])[c]
                    pe.wait_ge(last_reader, (m + 1) if exists(m) else STEPS)
                    if c == 2:
                        pe.wait_ge(s_v[0], (m + 1) if exists(m) else STEPS)
                    if exists(n - 1):
                        pe.wait_ge(s_gated[c], n)
                    bank = (bank_q, bank_k, bank_v)[c]
                    for half in range(2):
                        last = nc.tensor.matmul(bank[0:size, SEQ * half:SEQ * half + SEQ],
                                                w1_sb[:, half * HID + at:half * HID + at + size], h2T[:, :],
                                                start=True, stop=True)
                    last.then_inc(s_w1_ps[c], 1)

            def ffn_down(n):
                pe.wait_ge(s_o[0], (n + 2) if exists(n + 1) else STEPS)
                for t in range(TILES):
                    for c, (at, size) in enumerate(CHUNKS):
                        pe.wait_ge(s_gated[c], n + 1)
                        last = nc.tensor.matmul(bank_o[:, DIM * t:DIM * t + DIM],
                                                gated[0:size, c, P * t:P * t + P],
                                                w2_sb[0:size, bass.ds(layer(n), 1), c, :].rearrange("p o n -> p (o n)"),
                                                start=(c == 0), stop=(c == 2))
                last.then_inc(s_w2_ps, 1)

            def body(u):
                p, o, f = u - 1, u - 2, u - 3
                if exists(p):
                    transpose_qk(p, 0)
                if exists(u):
                    project(u, 0, 0)
                    project(u, 0, 1)
                if exists(p):
                    scores(p, 0)
                if exists(f):
                    ffn_down(f)
                if exists(o):
                    transpose_p(o, 1)
                if exists(p):
                    transpose_qk(p, 1)
                if exists(o):
                    attend(o, 1)
                if exists(u):
                    project(u, 1, 0)
                    project(u, 1, 1)
                if exists(o):
                    transpose_o(o, 1)
                if exists(u):
                    project(u, 1, 2)
                if exists(o):
                    project_o(o, 1)
                if exists(p):
                    scores(p, 1)
                    transpose_p(p, 0)
                    attend(p, 0)
                if exists(u):
                    project(u, 0, 2)
                if exists(u + 1) and not exists(p):
                    transpose_h(u + 1)
                if exists(o):
                    transpose_h2(o)
                if exists(p):
                    transpose_o(p, 0)
                if exists(o):
                    ffn_up(o)
                if exists(p):
                    project_o(p, 0)
                if exists(p) and exists(u + 1):
                    transpose_h(u + 1)

            pe.wait_ge(s_wts, 16 * WTS_DMAS)
            pe.wait_ge(s_bf, 2)
            walk(pe, body)

        @block.scalar
        def _(act):
            def a_batch(b):
                act.wait_ge(s_adif, b + 1)
                if exists(b - 1):
                    act.wait_ge(s_aT_ps[1], b)
                nc.scalar.activation(a_exp[:, :, :], a_dif[:, :, :], ACT.Exp, scale=A_DH ** -0.5).then_inc(s_aexp, 1)
                act.wait_ge(s_aT_ps[0], b + 1)
                if exists(b - 1):
                    act.wait_ge(s_ao_ps, b)
                nc.scalar.activation(a_expT[:, 0:4, :].rearrange("p a b -> p (a b)"), bank_t0[:, :], ACT.Copy
                                     ).then_inc(s_aT[0], 1)

            a_batch(0)
            with act.Fori(1, BATCH) as b:
                a_batch(b)

            def squares_of(n, t, which):
                rotd, done = ((s_q_rotd, s_q_sq), (s_k_rotd, s_k_sq))[which]
                act.wait_ge(rotd[t], n + 1)
                if t == 1:
                    act.wait_ge(s_ss[0], n + 1)
                elif exists(n - 1):
                    act.wait_ge(s_ss[1], n)
                nc.scalar.activation(squares[:, which, :], (bank_q, bank_k)[which][:, :], ACT.Square
                                     ).then_inc(done[t], 1)

            def exps(n, t, half):
                act.wait_ge(s_nbias[t], n + 1)
                if half == 0 and exists(n - 1):
                    act.wait_ge(s_pbT_ps[t], n)
                for h in range(4 * half, 4 * half + 4):
                    last = nc.scalar.activation(probs[t][:, h, :], bank_s[:, half, P * (h % 4):P * (h % 4) + P],
                                                ACT.Exp, bias=nbias[t][:, h:h + 1], scale=sc8[t][:, h:h + 1],
                                                accum_out=psums[t][:, h:h + 1])
                last.then_inc((s_pa, s_pb)[half][t], 1)

            def body(u):
                p, o = u - 1, u - 2
                if exists(p):
                    act.wait_ge(s_qT_ps[0], p + 1)
                    nc.scalar.activation(qT[0][:, :, :].rearrange("p a b -> p (a b)"), bank_t0[:, :], ACT.Copy
                                         ).then_inc(s_qT[0], 1)
                if exists(u):
                    squares_of(u, 0, 0)
                    squares_of(u, 0, 1)
                if exists(p):
                    exps(p, 0, 0)
                    exps(p, 0, 1)
                    act.wait_ge(s_qT_ps[1], p + 1)
                    nc.scalar.activation(qT[1][:, :, :].rearrange("p a b -> p (a b)"), bank_t0[:, :], ACT.Copy
                                         ).then_inc(s_qT[1], 1)
                if exists(o):
                    act.wait_ge(s_oT_ps[1], o + 1)
                    nc.scalar.activation(oT[:, :, :].rearrange("p a b -> p (a b)"), bank_t0[:, :], ACT.Copy
                                         ).then_inc(s_oT[1], 1)
                if exists(u):
                    squares_of(u, 1, 0)
                    squares_of(u, 1, 1)
                    act.wait_ge(s_v_ps[1], u + 1)
                    if exists(u - 1):
                        act.wait_ge(s_vmix, u)
                    nc.scalar.activation(V1_next[:, :], bank_v[:, :], ACT.Copy).then_inc(s_v[1], 1)
                if exists(p):
                    exps(p, 1, 0)
                    exps(p, 1, 1)
                if exists(u):
                    act.wait_ge(s_v_ps[0], u + 1)
                    if exists(u - 1):
                        act.wait_ge(s_vmix, u)
                    nc.scalar.activation(V0[:, :], bank_v[:, :], ACT.Copy).then_inc(s_v[0], 1)
                if exists(p):
                    act.wait_ge(s_oT_ps[0], p + 1)
                    nc.scalar.activation(oT[:, :, :].rearrange("p a b -> p (a b)"), bank_t1[:, :], ACT.Copy
                                         ).then_inc(s_oT[0], 1)
                if exists(o):
                    for c, (at, size) in enumerate(CHUNKS):
                        act.wait_ge(s_w1_ps[c], o + 1)
                        if exists(o - 1):
                            act.wait_ge(s_gated[c], o)
                        nc.scalar.activation(gelu[0:size, c, :], (bank_q, bank_k, bank_v)[c][0:size, SEQ:2 * SEQ],
                                             ACT.Gelu, bias=b1_sb[0:size, 1, c:c + 1]).then_inc(s_gelu[c], 1)

            walk(act, body)

        @block.vector
        def _(dve):
            def a_transposed(b):
                if exists(b - 1):
                    dve.wait_ge(s_axT_ps, b)
                nc.vector.tensor_scalar(a_in[:, :], a_x[:, bass.ds(b, 1), 0, :].rearrange("p o d -> p (o d)"),
                                        1.0, None, ALU.mult).then_inc(s_ain, 1)
                dve.wait_ge(s_axT_ps, b + 1)
                if exists(b - 1):
                    dve.wait_ge(s_as, b)
                nc.vector.tensor_copy(a_xT[:, :], bank_q[:, 0:P]).then_inc(s_axT, 1)
                for s in range(2):
                    last = nc.vector.tensor_tensor(
                        a_xTg[:, s, :, :],
                        bank_q[:, 64 * s:64 * s + 64].unsqueeze(1).broadcast_to([P, 4, A_KEYS]),
                        group[:, :].unsqueeze(2).broadcast_to([P, 4, A_KEYS]), ALU.mult)
                last.then_inc(s_axTg, 1)

            def a_softmax(b):
                dve.wait_ge(s_as, b + 1)
                scores = bank_as.rearrange("p g (m j) -> p g m j", j=A_KEYS)
                nc.vector.tensor_reduce(a_max[:, :], scores, AX.X, ALU.max).then_inc(s_amax, 1)
                dve.wait_ge(s_amax, b + 1)
                if exists(b - 1):
                    dve.wait_ge(s_aexp, b)
                nc.vector.tensor_tensor(a_dif[:, :, :].rearrange("p (g m) j -> p g m j", g=4), scores,
                                        a_max[:, :].rearrange("p (g m) -> p g m", g=4).unsqueeze(3
                                                              ).broadcast_to([P, 4, 4, A_KEYS]), ALU.subtract
                                        ).then_inc(s_adif, 1)

            def a_normalize(b):
                if exists(b - 1):
                    dve.wait_ge(s_ao_ps, b)
                for half in range(2):
                    rows = slice(64 * half, 64 * half + 64)
                    for s in range(2):
                        last = nc.vector.tensor_scalar(
                            a_v[rows, s, :, half, 0:A_DH],
                            a_xv[rows, bass.ds(b, 1), s, :].rearrange("p o (a h d) -> p (o a) h d", h=2, d=A_DH)[:, :, half, :],
                            1.0, None, ALU.mult)
                last.then_inc(s_av, 1)
                dve.wait_ge(s_aT_ps[1], b + 1)
                nc.vector.tensor_copy(a_expT[:, 4:8, :].rearrange("p a b -> p (a b)"), bank_t1[:, :]).then_inc(s_aT[1], 1)
                dve.wait_ge(s_ao_ps, b + 1)
                o9 = bank_o[:, 0:A_HEADS * (A_DH + 1)].rearrange("p (h d) -> p h d", h=A_HEADS)
                nc.vector.reciprocal(a_rec[:, :].unsqueeze(2), o9[:, :, A_DH:A_DH + 1]).then_inc(s_arec, 1)
                dve.wait_ge(s_arec, b + 1)
                nc.vector.tensor_tensor(a_o[:, :, :], o9[:, :, 0:A_DH],
                                        a_rec[:, :].unsqueeze(2).broadcast_to([P, A_HEADS, A_DH]), ALU.mult
                                        ).then_inc(s_ao, 1)
                dve.wait_ge(s_ao, b + 1)
                flat = a_o[:, :, :].rearrange("p h d -> p (h d)")
                nc.vector.tensor_reduce(a_den[:, :], flat, AX.X, ALU.add).then_inc(s_aden, 1)
                dve.wait_ge(s_aden, b + 1)
                nc.vector.reciprocal(a_rden[:, :], a_den[:, :]).then_inc(s_arden, 1)
                dve.wait_ge(s_arden, b + 1)
                nc.vector.tensor_tensor(a_alpha[:, :], a_den[:, :], a_rden[:, :], ALU.mult).then_inc(s_aalpha, 1)
                dve.wait_ge(s_aalpha, b + 1)
                nc.vector.scalar_tensor_tensor(a_y[:, :], flat, a_alpha[:, 0:1],
                                               a_x[:, bass.ds(b, 1), 0, :].rearrange("p o d -> p (o d)"),
                                               ALU.mult, ALU.add).then_inc(s_ay, 1)
                dve.wait_ge(s_ay, b + 1)
                odd = a_x[:, bass.ds(b, 1), 1, :].rearrange("p o d -> p (o d)")
                nc.vector.bn_stats(a_st[:, 0, :], a_y[:, :])
                nc.vector.bn_stats(a_st[:, 1, :], odd).then_inc(s_ast, 1)
                dve.wait_ge(s_ast, b + 1)
                nc.vector.memset(a_ve[:, :], EPS)
                for i in range(2):
                    last = nc.vector.bn_aggr(a_mv[:, i, :], a_st[:, i, :])
                last.then_inc(s_amv, 1)
                dve.wait_ge(s_amv, b + 1)
                nc.vector.tensor_tensor(a_ve[:, :], a_ve[:, :], a_mv[:, :, 1], ALU.add).then_inc(s_ave, 1)

            def a_finish(b):
                odd = a_x[:, bass.ds(b, 1), 1, :].rearrange("p o d -> p (o d)")
                dve.wait_ge(s_arstd, b + 1)
                for i, src in enumerate((a_y[:, :], odd)):
                    last = nc.vector.tensor_scalar(a_xn[:, bass.ds(b, 1), i, :].rearrange("p o d -> p (o d)"), src,
                                                   a_mv[:, i, 0:1], a_rstd[:, i:i + 1], ALU.subtract, ALU.mult)
                last.then_inc(s_axn, 1)

            nc.vector.memset(a_v[:, :, :, :, :], 0.0).then_inc(s_zero, 1)
            nc.vector.memset(minus_half[:, :], -0.5).then_inc(s_setup, 1)
            nc.vector.memset(hT[64:P, 0:1], 0.0).then_inc(s_setup, 1)
            nc.vector.memset(h2[0:1, 0, 64:DIM], 0.0).then_inc(s_setup, 1)
            dve.wait_ge(s_zero, 1)
            nc.vector.memset(a_v[0:64, :, :, 0, A_DH:A_DH + 1], 1.0).then_inc(s_setup, 1)
            nc.vector.memset(a_v[64:P, :, :, 1, A_DH:A_DH + 1], 1.0).then_inc(s_setup, 1)
            dve.wait_ge(s_ax, 16 * 5)
            dve.wait_ge(s_const, 16 * CONST_DMAS)
            dve.wait_ge(s_setup, 5)
            a_transposed(0)
            nc.vector.tensor_copy(ident_bf[:, :], ident[:, :]).then_inc(s_bf, 1)
            nc.vector.tensor_copy(mask_bf[:, :, :], mask32[:, :, :]).then_inc(s_bf, 1)
            a_softmax(0)

            def a_body(b):
                a_transposed(b + 1)
                a_normalize(b)
                a_softmax(b + 1)
                a_finish(b)

            a_body(0)
            with dve.Fori(1, BATCH - 1) as b:
                a_body(b)
            a_normalize(BATCH - 1)
            a_finish(BATCH - 1)

            def rotate(n, t, which):
                bank, arrived, done = ((bank_q, s_q_ps, s_q_rotd), (bank_k, s_k_ps, s_k_rotd))[which]
                table = rot_tab[:, bass.ds(layer(n), 1), t, :, :]
                dve.wait_ge(arrived[t], n + 1)
                if exists(n - 1):
                    dve.wait_ge((s_qrot, s_krot)[which][t], n)
                nc.vector.tensor_tensor(heads(rot_c[t][:, which, :]), heads(bank[:, :]),
                                        table[:, :, 2 * which, :].broadcast_to([P, HEADS, DH]), ALU.mult)
                half = "p h (s d) -> p h s d"
                nc.vector.tensor_tensor(heads(rot_s[t][:, which, :]).rearrange(half, s=2),
                                        heads(bank[:, :]).rearrange(half, s=2)[:, :, ::-1, :],
                                        table[:, :, 2 * which + 1, :].rearrange(half, s=2
                                                                                ).broadcast_to([P, HEADS, 2, DH // 2]),
                                        ALU.mult).then_inc(done[t], 1)

            def sum_squares(n, t):
                dve.wait_ge(s_q_sq[t], n + 1)
                dve.wait_ge(s_k_sq[t], n + 1)
                nc.vector.tensor_reduce(ss[:, :], squares[:, :, :].rearrange("p w (h d) -> p (w h) d", d=DH),
                                        AX.X, ALU.add).then_inc(s_ss[t], 1)
                dve.wait_ge(s_ss[t], n + 1)
                if t == 1:
                    dve.wait_ge(s_rnorm[0], n + 1)
                elif exists(n - 1):
                    dve.wait_ge(s_rnorm[1], n)
                nc.vector.tensor_scalar(ssf[:, :], ss[:, :], NORM_FLOOR, None, ALU.max).then_inc(s_ssf[t], 1)

            def scale_of_q(n, t):
                dve.wait_ge(s_rnorm[t], n + 1)
                if exists(n - 1):
                    dve.wait_ge(s_pb[t], n)
                nc.vector.tensor_scalar(sc8[t][:, :].rearrange("p (odd j) -> p odd j", odd=2),
                                        rnorm[t][:, 0:HEADS].rearrange("p (j odd) -> p odd j", odd=2),
                                        QK_SCALE, None, ALU.mult).then_inc(s_sc8[t], 1)

            def row_max(n, t):
                dve.wait_ge(s_s_ps[t], n + 1)
                nc.vector.tensor_reduce(smax[t][:, :], bank_s[:, :, :].rearrange("p a (h j) -> p (a h) j", j=P),
                                        AX.X, ALU.max).then_inc(s_smax[t], 1)
                dve.wait_ge(s_smax[t], n + 1)
                dve.wait_ge(s_sc8[t], n + 1)
                nc.vector.scalar_tensor_tensor(nbias[t][:, :], smax[t][:, :], -1.0, sc8[t][:, :],
                                               ALU.mult, ALU.mult).then_inc(s_nbias[t], 1)

            def copy_kT(n, t):
                dve.wait_ge(s_kT_ps[t], n + 1)
                if exists(n - 1):
                    dve.wait_ge(s_s_ps[1], n)
                nc.vector.tensor_copy(kT[:, :, P * t:P * t + P],
                                      bank_t1[:, :].rearrange("p (a b) -> p a b", a=BLOCKS)).then_inc(s_kT[t], 1)

            def copy_pT(n, t):
                for half, (arrived, bank, done) in enumerate(((s_paT_ps, bank_t0, s_paT), (s_pbT_ps, bank_t1, s_pbT))):
                    dve.wait_ge(arrived[t], n + 1)
                    if t == 1:
                        dve.wait_ge(s_o_ps[0], n + 1)
                    elif exists(n - 1):
                        dve.wait_ge(s_o_ps[1], n)
                    nc.vector.tensor_copy(probsT[:, 4 * half:4 * half + 4, :].rearrange("p a b -> p (a b)"),
                                          bank[:, :]).then_inc(done[t], 1)

            def normalize_o(n, t):
                dve.wait_ge(s_pb[t], n + 1)
                nc.vector.reciprocal(rsums[t][:, :], psums[t][:, :]).then_inc(s_rsum[t], 1)
                dve.wait_ge(s_rsum[t], n + 1)
                dve.wait_ge(s_o_ps[t], n + 1)
                if t == 1:
                    dve.wait_ge(s_oT_ps[0], n + 1)
                elif exists(n - 1):
                    dve.wait_ge(s_oT_ps[1], n)
                by_pair = "p (j odd d) -> p j odd d"
                nc.vector.tensor_tensor(o_sb[:, :].rearrange(by_pair, odd=2, d=DH),
                                        bank_o[:, :].rearrange(by_pair, odd=2, d=DH),
                                        rsums[t][:, :].rearrange("p (odd j) -> p j odd", odd=2).unsqueeze(3
                                                                 ).broadcast_to([P, BLOCKS, 2, DH]), ALU.mult
                                        ).then_inc(s_o[t], 1)

            def add_attention(n, t):
                bank = bank_t1 if t else bank_t0
                dve.wait_ge(s_wo_ps[t], n + 1)
                if exists(n - 1):
                    dve.wait_ge(s_h2, 48 * n)
                    dve.wait_ge(s_x1b, n)
                nc.vector.tensor_tensor(x1[:, t, :], bank[:, 0:DIM],
                                        X[:, bass.ds(n, 1), t, :].rearrange("p o d -> p (o d)"), ALU.add
                                        ).then_inc(s_x1[t], 1)

            def copy_hT(n):
                dve.wait_ge(s_hT_ps, n + 1)
                if exists(n - 1):
                    dve.wait_ge(s_v_ps[0], n)
                nc.vector.tensor_copy(hT[0:64, :], bank_t1[0:64, 0:SEQ])
                nc.vector.tensor_copy(hT[64:P, 1:SEQ], bank_t1[64:P, 0:SEQ - 1]).then_inc(s_hT, 1)

            def place_v(n):
                dve.wait_ge(s_v[0], n + 1)
                dve.wait_ge(s_v[1], n + 1)
                if exists(n - 1):
                    dve.wait_ge(s_o_ps[1], n)
                nc.vector.tensor_copy(V1[:, :], V1_next[:, :])
                nc.vector.tensor_copy(Vmix[0:64, :], V1_next[0:64, :])
                nc.vector.tensor_copy(Vmix[64:P, :], V0[64:P, :]).then_inc(s_vmix, 1)

            def statistics(n):
                dve.wait_ge(s_h2, 48 * n + 48)
                for t in range(TILES):
                    last = nc.vector.bn_stats(st[:, t, :], h2[:, t, :])
                last.then_inc(s_st, 1)
                dve.wait_ge(s_st, n + 1)
                nc.vector.memset(ve[:, :], EPS)
                for t in range(TILES):
                    last = nc.vector.bn_aggr(mv[:, t, :], st[:, t, :])
                last.then_inc(s_mv, 1)
                dve.wait_ge(s_mv, n + 1)
                nc.vector.tensor_tensor(ve[:, :], ve[:, :], mv[:, :, 1], ALU.add).then_inc(s_ve, 1)

            def normalize_h2(n):
                dve.wait_ge(s_rstd, n + 1)
                if exists(n - 1):
                    dve.wait_ge(s_h2T_ps, n)
                for t in range(TILES):
                    last = nc.vector.tensor_scalar(h2n[:, t, :], h2[:, t, :], mv[:, t, 0:1], rstd[:, t:t + 1],
                                                   ALU.subtract, ALU.mult)
                last.then_inc(s_h2n, 1)

            def copy_h2T(n):
                dve.wait_ge(s_params, n + 1)
                dve.wait_ge(s_h2T_ps, n + 1)
                if exists(n - 1):
                    dve.wait_ge(s_w1_ps[2], n)
                nc.vector.tensor_scalar(h2T[:, :], bank_t0[:, 0:SEQ], ln_gb[:, 0:1], ln_gb[:, 1:2],
                                        ALU.mult, ALU.add).then_inc(s_h2T, 1)

            def gate(n):
                for c, (at, size) in enumerate(CHUNKS):
                    dve.wait_ge(s_gelu[c], n + 1)
                    if exists(n - 1):
                        dve.wait_ge(s_w2_ps, n)
                    nc.vector.scalar_tensor_tensor(gated[0:size, c, :], (bank_q, bank_k, bank_v)[c][0:size, 0:SEQ],
                                                   b1_sb[0:size, 0, c:c + 1], gelu[0:size, c, :],
                                                   ALU.add, ALU.mult).then_inc(s_gated[c], 1)

            def add_ffn(n):
                dve.wait_ge(s_w2_ps, n + 1)
                dve.wait_ge(s_x1b, n + 1)
                nc.vector.tensor_tensor(X[:, bass.ds(n + BATCH, 1), :, :].rearrange("p o t d -> p (o t) d"),
                                        bank_o[:, 0:SEQ].rearrange("p (t d) -> p t d", t=TILES), x1b[:, :, :], ALU.add
                                        ).then_inc(x_ready, 1)

            def body(u):
                p, o, f = u - 1, u - 2, u - 3
                if exists(p):
                    scale_of_q(p, 0)
                    copy_kT(p, 0)
                if exists(u):
                    rotate(u, 0, 0)
                    rotate(u, 0, 1)
                if exists(p):
                    row_max(p, 0)
                if exists(u):
                    sum_squares(u, 0)
                if exists(f):
                    add_ffn(f)
                if exists(o):
                    copy_pT(o, 1)
                if exists(p):
                    copy_kT(p, 1)
                if exists(o):
                    normalize_o(o, 1)
                if exists(p):
                    place_v(p)
                if exists(u):
                    rotate(u, 1, 0)
                    rotate(u, 1, 1)
                if exists(o):
                    add_attention(o, 1)
                if exists(p):
                    scale_of_q(p, 1)
                    row_max(p, 1)
                if exists(u):
                    sum_squares(u, 1)
                if exists(o):
                    statistics(o)
                if exists(p):
                    copy_pT(p, 0)
                    normalize_o(p, 0)
                if exists(o):
                    normalize_h2(o)
                    copy_h2T(o)
                if exists(u + 1) and not exists(p):
                    copy_hT(u + 1)
                if exists(p):
                    add_attention(p, 0)
                if exists(p) and exists(u + 1):
                    copy_hT(u + 1)
                if exists(o):
                    gate(o)

            dve.wait_ge(s_rot, DEPTH * TILES * 4)
            walk(dve, body)

            def last_norm(v):
                for i in range(2):
                    b = 2 * v + i
                    if exists(v - 1):
                        dve.wait_ge(s_fout[i], v)
                    whole = "p o t d -> p (o t) d"
                    nc.vector.tensor_tensor(f_y[:, i, :, :], X[:, bass.ds(b, 1), :, :].rearrange(whole),
                                            X[:, bass.ds(b + STEPS, 1), :, :].rearrange(whole), ALU.add
                                            ).then_inc(s_fy[i], 1)
                    dve.wait_ge(s_fy[i], v + 1)
                    for t in range(TILES):
                        last = nc.vector.bn_stats(f_st[:, i, t, :], f_y[:, i, t, :])
                    last.then_inc(s_fst[i], 1)
                    dve.wait_ge(s_fst[i], v + 1)
                    nc.vector.memset(f_ve[:, i, :], EPS)
                    for t in range(TILES):
                        last = nc.vector.bn_aggr(f_mv[:, i, t, :], f_st[:, i, t, :])
                    last.then_inc(s_fmv[i], 1)
                    dve.wait_ge(s_fmv[i], v + 1)
                    nc.vector.tensor_tensor(f_ve[:, i, :], f_ve[:, i, :], f_mv[:, i, :, 1], ALU.add).then_inc(s_fve[i], 1)
                for i in range(2):
                    dve.wait_ge(s_frstd[i], v + 1)
                    if exists(v - 1):
                        dve.wait_ge(s_fdma[i], 16 * v)
                    for t in range(TILES):
                        last = nc.vector.tensor_scalar(f_out[:, i, t, :], f_y[:, i, t, :], f_mv[:, i, t, 0:1],
                                                       f_rstd[:, i, t:t + 1], ALU.subtract, ALU.mult)
                    last.then_inc(s_fout[i], 1)

            dve.wait_ge(x_ready, BATCH + STEPS)
            last_norm(0)
            with dve.Fori(1, BATCH // 2) as v:
                last_norm(v)


_INS = ["L0_attn_x", "L0_ffn_wqkv", "L0_ffn_q_scale", "L0_ffn_k_scale", "L0_ffn_wo", "L0_ffn_ln_g",
        "L0_ffn_ln_b", "L0_ffn_w1", "L0_ffn_b1", "L0_ffn_w2", "L0_ffn_b2"]
_OUTS = [((BATCH, SEQ, DIM), "float32")]


def kernel(**inputs):
    import numpy as _np
    import concourse.bacc as _bacc
    from concourse import mybir as _mybir
    from concourse.bass_utils import run_bass_kernel_spmd as _run

    nc = _bacc.Bacc("TRN2", target_bir_lowering=False, num_devices=1)
    arrays, args = {}, []
    named = [(name, inputs[name]) for name in _INS] + list(table_constants().items())
    for name, a in named:
        a = _np.ascontiguousarray(a)
        arrays[f"in_{name}_dram"] = a
        args.append(nc.dram_tensor(f"in_{name}_dram", a.shape, _mybir.dt.from_np(a.dtype), kind="ExternalInput").ap())
    for i, (shape, dtype) in enumerate(_OUTS):
        dt = _mybir.dt.from_np(_np.dtype(dtype))
        args.append(nc.dram_tensor(f"out_{i}_dram", shape, dt, kind="ExternalOutput").ap())
    build(nc, *args)
    r = _run(nc, [arrays], core_ids=[0])
    got = tuple(r.results[0][f"out_{i}_dram"] for i in range(len(_OUTS)))
    return got[0]
```

```python
from contextlib import ExitStack

import concourse.bass as bass
from concourse import mybir

ALU = mybir.AluOpType
ACT = mybir.ActivationFunctionType
AX = mybir.AxisListType
F32 = mybir.dt.float32
F32R = mybir.dt.float32r
BF16 = mybir.dt.bfloat16

P = 128
BATCH, SEQ, DIM = 8, 256, 128
TILES = SEQ // P
DEPTH, HEADS, DH, WINDOW = 2, 8, 64, 64
INNER = HEADS * DH
BLOCKS = INNER // P
HID = int(DIM * 4 * 2 / 3)
CHUNK = -(-HID // 3)
CHUNKS = [(c * CHUNK, min(CHUNK, HID - c * CHUNK)) for c in range(3)]
STEPS = DEPTH * BATCH
QK_SCALE = 8.0
A_HEADS, A_DH = 16, 8
A_KEYS = 64
A_PAIRS = A_HEADS // 2
EPS = 1e-5
MASKED = -1e30
NORM_FLOOR = 1e-24


def table_constants():
    import numpy as np
    half = np.arange(0, DH, 2, dtype=np.float32)
    inv_freq = (1.0 / np.float32(10000.0) ** (half / np.float32(DH))).astype(np.float32)
    t = np.arange(SEQ, dtype=np.float32)
    freqs = (t[:, None] * inv_freq[None, :]).astype(np.float32)
    freqs = np.concatenate([freqs, freqs], axis=-1).astype(np.float64)
    base = (half + 0.4 * DH) / (1.4 * DH)
    scale = base[None, :].astype(np.float64) ** ((t - SEQ // 2) / float(WINDOW // 2))[:, None]
    scale = np.concatenate([scale, scale], axis=-1)
    sign = np.where(np.arange(DH) < DH // 2, -1.0, 1.0)[None, :]
    kinds = [np.cos(freqs) * scale, sign * np.sin(freqs) * scale,
             np.cos(freqs) / scale, sign * np.sin(freqs) / scale]
    rotary = np.stack(kinds, axis=1).reshape(TILES, P, 4, DH).transpose(1, 0, 2, 3)
    r = np.arange(P)[:, None]
    c = np.arange(P)[None, :]
    even = np.where(c < 64, c <= r, c - 64 >= r)
    odd = np.where(c < 64, c >= r - 64, c - 64 <= r - 64)
    allowed = np.stack([np.where(r < 64, even, odd)] * TILES, axis=1)
    allowed[:64, 0, 64:] = False
    mask = np.where(allowed, 0.0, MASKED)
    ident = np.eye(P)
    group = (np.arange(P)[:, None] // A_DH) % 4 == np.arange(4)[None, :]
    return {"rotary": np.ascontiguousarray(rotary, np.float32), "mask": mask.astype(np.float32),
            "ident": ident.astype(np.float32), "group": group.astype(np.float32)}


def build(nc, x, wqkv, q_scale, k_scale, wo, ln_g, ln_b, w1, b1, w2, b2,
          c_rotary, c_mask, c_ident, c_group, out):
    with ExitStack() as ctx:
        def sb(name, shape, dt=F32):
            return ctx.enter_context(nc.sbuf_tensor(name, shape, dt))

        def psum(name, shape):
            return ctx.enter_context(nc.psum_tensor(name, shape, F32))

        def sem(name):
            return ctx.enter_context(nc.semaphore(name))

        def sem2(name):
            return [sem(f"{name}{t}") for t in range(2)]

        banks = psum("banks", [P, 8, 512])
        bank_q, bank_k, bank_v = (banks[:, i, :] for i in range(3))
        bank_s = banks[:, 3:5, :]
        bank_t0, bank_t1, bank_o = (banks[:, i, :] for i in range(5, 8))
        bank_as = banks[:, 1:5, 0:4 * A_KEYS]
        SLOT = [4 * (h % 2) + h // 2 for h in range(HEADS)]

        ident = sb("ident", [P, P])
        ident_bf = sb("ident_bf", [P, P], BF16)
        mask32 = sb("mask32", [P, TILES, P])
        mask_bf = sb("mask_bf", [P, TILES, P], BF16)
        rot_const = sb("rot_const", [P, TILES, 4, DH])
        rot_tab = sb("rot_tab", [P, DEPTH, TILES, 4, DH])
        head_scale = sb("head_scale", [P, DEPTH, 2, DH])
        group = sb("group", [P, 4])
        minus_half = sb("minus_half", [P, 16])
        table_use = sb("table_use", [P, 1])
        wqkv_sb = sb("wqkv_sb", [P, DEPTH, 3, INNER])
        wqkv_hi = sb("wqkv_hi", [P, DEPTH, 3, INNER], F32R)
        wqkv_lo = sb("wqkv_lo", [P, DEPTH, 3, INNER], F32R)
        wo_sb = sb("wo_sb", [P, DEPTH, BLOCKS, DIM])
        w2_sb = sb("w2_sb", [CHUNK, DEPTH, 3, DIM])
        w1_sb = sb("w1_sb", [P, 2 * HID])
        ln_gb = sb("ln_gb", [P, 2])
        b1_sb = sb("b1_sb", [CHUNK, 2, 3])
        b2_sb = sb("b2_sb", [P, DIM])

        X = sb("X", [P, (DEPTH + 1) * BATCH, TILES, DIM])

        a_x = sb("a_x", [P, BATCH, 2, DIM])
        a_xv = sb("a_xv", [P, BATCH, 2, DIM])
        a_in = sb("a_in", [P, DIM])
        a_xT = sb("a_xT", [P, P])
        a_xTg = sb("a_xTg", [P, 2, 4, A_KEYS])
        a_max = sb("a_max", [P, A_HEADS])
        a_dif = sb("a_dif", [P, A_HEADS, A_KEYS])
        a_exp = sb("a_exp", [P, A_HEADS, A_KEYS])
        a_expT = sb("a_expT", [P, A_PAIRS, P])
        a_v = sb("a_v", [P, 2, A_PAIRS, 2, A_DH + 1])
        a_o9 = sb("a_o9", [P, BATCH, A_HEADS, A_DH + 1])
        a_rec = sb("a_rec", [P, BATCH, A_HEADS])
        a_o = sb("a_o", [P, BATCH, A_HEADS, A_DH])
        a_den = sb("a_den", [P, BATCH])
        a_rden = sb("a_rden", [P, BATCH])
        a_alpha = sb("a_alpha", [P, BATCH])
        a_y = sb("a_y", [P, BATCH, DIM])
        a_st = sb("a_st", [P, BATCH, 2, 6])
        a_mv = sb("a_mv", [P, BATCH, 2, 2])
        a_ve = sb("a_ve", [P, BATCH, 2])
        a_rstd = sb("a_rstd", [P, BATCH, 2])
        a_xn = sb("a_xn", [P, BATCH, 2, DIM])

        xs = sb("xs", [P, TILES, DIM])
        hT_hi = sb("hT_hi", [P, SEQ], F32R)
        hT_lo = sb("hT_lo", [P, SEQ], F32R)
        rot_c = [sb(f"rot_c{i}", [P, 2, INNER]) for i in range(2)]
        rot_s = [sb(f"rot_s{i}", [P, 2, INNER]) for i in range(2)]
        squares = sb("squares", [P, 2, INNER])
        ss = sb("ss", [P, 2 * HEADS])
        ssf = sb("ssf", [P, 2 * HEADS])
        rnorm = [sb(f"rnorm{i}", [P, 2 * HEADS]) for i in range(2)]
        qrot = [sb(f"qrot{i}", [P, INNER]) for i in range(2)]
        krot = [sb(f"krot{i}", [P, INNER]) for i in range(2)]
        knorm = [sb(f"knorm{i}", [P, INNER]) for i in range(2)]
        qT = [sb(f"qT{i}", [P, BLOCKS, P]) for i in range(2)]
        kT = sb("kT", [P, BLOCKS, SEQ])
        sc8 = [sb(f"sc8_{i}", [P, HEADS]) for i in range(2)]
        smax = [sb(f"smax{i}", [P, HEADS]) for i in range(2)]
        nbias = [sb(f"nbias{i}", [P, HEADS]) for i in range(2)]
        probs = [sb(f"probs{i}", [P, HEADS, P]) for i in range(2)]
        psums = [sb(f"psums{i}", [P, HEADS]) for i in range(2)]
        rsums = [sb(f"rsums{i}", [P, HEADS]) for i in range(2)]
        probsT = sb("probsT", [P, HEADS, P])
        V0_next = sb("V0_next", [P, INNER])
        V0 = sb("V0", [P, INNER])
        V1_next = sb("V1_next", [P, INNER])
        V1 = sb("V1", [P, INNER])
        Vmix = sb("Vmix", [P, INNER])
        o_sb = sb("o_sb", [P, INNER])
        oT = sb("oT", [P, BLOCKS, P])
        x1 = sb("x1", [P, TILES, DIM])
        x1b = mask32
        h2 = sb("h2", [P, TILES, DIM])
        h2n = sb("h2n", [P, TILES, DIM])
        st = sb("st", [P, TILES, 6])
        mv = sb("mv", [P, TILES, 2])
        ve = sb("ve", [P, TILES])
        rstd = sb("rstd", [P, TILES])
        h2T = sb("h2T", [P, SEQ])
        split = wqkv_sb[:, 0, :, :].rearrange("p k (c n) -> p (k c) n", n=SEQ)
        gelu, gated = split[0:CHUNK, 0:3, :], split[0:CHUNK, 3:6, :]
        split = wqkv_sb[:, 1, :, :].rearrange("p k (c t d) -> p (k c) t d", t=TILES, d=DIM)
        f_y, f_out = split[:, 0, :, :], split[:, 1, :, :]
        f_st = sb("f_st", [P, TILES, 6])
        f_mv = sb("f_mv", [P, TILES, 2])
        f_ve = sb("f_ve", [P, TILES])
        f_rstd = sb("f_rstd", [P, TILES])

        s_ax_first = sem("s_ax_first")
        s_ax = sem("s_ax")
        s_whi, s_wlo = sem("s_whi"), sem("s_wlo")
        s_const = sem("s_const")
        s_tab = sem("s_tab")
        s_wqkv = sem("s_wqkv")
        s_wts = sem("s_wts")
        s_ffnw = sem("s_ffnw")
        s_zero = sem("s_zero")
        s_table = sem("s_table")
        s_setup = sem("s_setup")
        s_bf = sem("s_bf")
        s_rot = sem("s_rot")
        s_ain = sem("s_ain")
        s_axT_ps = sem("s_axT_ps")
        s_axT = sem("s_axT")
        s_axTg = sem("s_axTg")
        s_as = sem("s_as")
        s_amax = sem("s_amax")
        s_adif = sem("s_adif")
        s_aexp = sem("s_aexp")
        s_aT_ps = sem2("s_aT_ps")
        s_aT = sem2("s_aT")
        s_av = sem("s_av")
        s_ao_ps = sem("s_ao_ps")
        s_ao9 = sem("s_ao9")
        s_arec = sem("s_arec")
        s_ao = sem("s_ao")
        s_aden = sem("s_aden")
        s_arden = sem("s_arden")
        s_aalpha = sem("s_aalpha")
        s_ay = sem("s_ay")
        s_ast = sem("s_ast")
        s_amv = sem("s_amv")
        s_ave = sem("s_ave")
        s_arstd = sem("s_arstd")
        s_axn = sem("s_axn")
        s_ax_dma = sem("s_ax_dma")
        x_ready = sem("x_ready")
        s_xs = sem("s_xs")
        s_hT_ps = sem("s_hT_ps")
        s_hT_hi = sem("s_hT_hi")
        s_hT = sem("s_hT")
        s_q_ps, s_k_ps, s_v_ps = sem2("s_q_ps"), sem2("s_k_ps"), sem2("s_v_ps")
        s_q_rotd, s_k_rotd = sem2("s_q_rotd"), sem2("s_k_rotd")
        s_q_sq, s_k_sq = sem2("s_q_sq"), sem2("s_k_sq")
        s_v = sem2("s_v")
        s_V0 = sem("s_V0")
        s_vmix = sem("s_vmix")
        s_ss, s_ssf, s_rnorm = sem2("s_ss"), sem2("s_ssf"), sem2("s_rnorm")
        s_qrot, s_krot, s_knorm = sem2("s_qrot"), sem2("s_krot"), sem2("s_knorm")
        s_qT_ps, s_kT_ps, s_qT, s_kT = sem2("s_qT_ps"), sem2("s_kT_ps"), sem2("s_qT"), sem2("s_kT")
        s_s_ps = sem2("s_s_ps")
        s_sc8, s_smax, s_nbias = sem2("s_sc8"), sem2("s_smax"), sem2("s_nbias")
        s_pa, s_pb = sem2("s_pa"), sem2("s_pb")
        s_paT_ps, s_pbT_ps, s_paT, s_pbT = sem2("s_paT_ps"), sem2("s_pbT_ps"), sem2("s_paT"), sem2("s_pbT")
        s_o_ps, s_rsum, s_o = sem2("s_o_ps"), sem2("s_rsum"), sem2("s_o")
        s_oT_ps, s_oT, s_wo_ps, s_x1 = sem2("s_oT_ps"), sem2("s_oT"), sem2("s_wo_ps"), sem2("s_x1")
        s_h2 = sem("s_h2")
        s_x1b = sem("s_x1b")
        s_st, s_mv, s_ve, s_rstd, s_h2n = sem("s_st"), sem("s_mv"), sem("s_ve"), sem("s_rstd"), sem("s_h2n")
        s_h2T_ps, s_h2T = sem("s_h2T_ps"), sem("s_h2T")
        s_params = sem("s_params")
        s_w1_ps, s_gelu, s_gated = ([sem(f"{n}{c}") for c in range(3)] for n in ("s_w1_ps", "s_gelu", "s_gated"))
        s_w2_ps = sem("s_w2_ps")
        s_fy, s_fst, s_fmv, s_fve, s_frstd, s_fout, s_fdma = (
            sem(n) for n in ("s_fy", "s_fst", "s_fmv", "s_fve", "s_frstd", "s_fout", "s_fdma"))

        def exists(n):
            return not isinstance(n, int) or 0 <= n < STEPS

        def layer(n):
            return n // BATCH

        def heads(ap):
            return ap.rearrange("p (h d) -> p h d", h=HEADS)

        FULL = 3
        LAST_NORM = DEPTH * BATCH - BATCH + 3

        def walk(eng, body, first=-1):
            for u in range(first, FULL):
                body(u, False)
            with eng.Fori(FULL, LAST_NORM) as u:
                body(u, False)
            with eng.Fori(LAST_NORM, STEPS - 1) as u:
                body(u, True)
            for u in range(STEPS - 1, STEPS + 3):
                body(u, True)

        def ffn_weights(eng, l):
            eng.dma_start(w1_sb[:, :], w1[l]).then_inc(s_ffnw, 16)
            eng.dma_start(ln_gb[:, 0:1], ln_g[l].rearrange("(p o) -> p o", o=1)).then_inc(s_ffnw, 16)
            eng.dma_start(ln_gb[:, 1:2], ln_b[l].rearrange("(p o) -> p o", o=1)).then_inc(s_ffnw, 16)
            for half in range(2):
                for c, (at, size) in enumerate(CHUNKS):
                    eng.dma_start(b1_sb[0:size, half, c:c + 1],
                                  b1[l, half * HID + at:half * HID + at + size].rearrange("(p o) -> p o", o=1)
                                  ).then_inc(s_ffnw, 16)
            eng.dma_start(b2_sb[:, :], b2[l].partition_broadcast(P)).then_inc(s_ffnw, 16)

        FFN_DMAS = 10
        CONST_DMAS = 2
        TAB_DMAS = 4
        WTS_DMAS = 4
        A_HALF = BATCH // 2

        block = ctx.enter_context(nc.Block())

        @block.sync
        def _(sp):
            xq = x.rearrange("b (q two) d -> q b two d", two=2)
            sp.dma_start(a_x[:, 0:1, :, :], xq[:, 0:1]).then_inc(s_ax_first, 16)
            sp.dma_start(ident[:, :], c_ident).then_inc(s_const, 16)
            sp.dma_start(group[:, :], c_group).then_inc(s_const, 16)
            sp.dma_start(a_x[:, 1:BATCH, :, :], xq[:, 1:BATCH]).then_inc(s_ax, 16)
            xv = x.rearrange("b (s j two) d -> j b s two d", s=2, two=2)[:, :, :, 0, :]
            for half in range(2):
                for s in range(2):
                    sp.dma_start(a_xv[64 * half:64 * half + 64, :, s, :], xv[:, :, s, :]).then_inc(s_ax, 16)
            sp.dma_start(mask32[:, :, :], c_mask).then_inc(s_tab, 16)
            sp.dma_start(rot_const[:, :, :, :], c_rotary).then_inc(s_tab, 16)
            sp.dma_start(head_scale[:, :, 0, :], q_scale.partition_broadcast(P)).then_inc(s_tab, 16)
            sp.dma_start(head_scale[:, :, 1, :], k_scale.partition_broadcast(P)).then_inc(s_tab, 16)
            for l in range(DEPTH):
                sp.dma_start(wqkv_sb[:, l, :, :], wqkv[l].rearrange("p (k n) -> p k n", k=3)).then_inc(s_wqkv, 16)
            sp.dma_start(wo_sb[:, :, :, :].rearrange("p l k n -> p (l k) n"),
                         wo.rearrange("l (k p) n -> p (l k) n", p=P)).then_inc(s_wts, 16)
            for l in range(DEPTH):
                sp.dma_start(w2_sb[:, l, 0:2, :],
                             w2[l, 0:2 * CHUNK, :].rearrange("(c p) n -> p c n", p=CHUNK)).then_inc(s_wts, 16)
            sp.dma_start(w2_sb[0:HID - 2 * CHUNK, :, 2, :],
                         w2[:, 2 * CHUNK:HID, :].rearrange("l p n -> p l n")).then_inc(s_wts, 16)
            ffn_weights(sp, 0)

            def place_stream(half):
                part = slice(half * A_HALF, half * A_HALF + A_HALF)
                sp.wait_ge(s_axn, half + 1)
                for s in range(2):
                    for odd in range(2):
                        sp.dma_start(X[odd:P:2, part, s, :], a_xn[64 * s:64 * s + 64, part, odd, :]
                                     ).then_inc(s_ax_dma, 16)
                sp.wait_ge(s_ax_dma, 64 * half + 64)
                sp.sem_inc(x_ready, A_HALF)

            def count(value):
                return value if isinstance(value, int) else sp.to_reg(value)

            def body(n, norm):
                u, p, o, b = count(n - 1), count(n - 2), count(n - 3), n - 1 - LAST_NORM
                V0_before, mixed_before = count(16 * n - 16), count(48 * n - 48)
                if exists(n):
                    sp.wait_ge(x_ready, n + 1)
                    if exists(n - 1):
                        sp.wait_ge(s_hT_ps, n)
                    sp.dma_start(xs[:, :, :], X[:, bass.ds(n, 1), :, :].rearrange("p o t d -> p (o t) d")
                                 ).then_inc(s_xs, 16)
                if exists(p):
                    if exists(n - 3):
                        sp.wait_ge(s_o_ps[1], p)
                    sp.wait_ge(s_v[1], u)
                    sp.wait_ge(s_V0, V0_before)
                    sp.dma_start(V1[:, :], V1_next[:, :]).then_inc(s_vmix, 16)
                    sp.dma_start(Vmix[0:64, :], V1_next[0:64, :]).then_inc(s_vmix, 16)
                    sp.dma_start(Vmix[64:P, :], V0[64:P, :]).then_inc(s_vmix, 16)
                if isinstance(o, int) and o == BATCH:
                    sp.wait_ge(s_x1b, BATCH)
                    for c in range(3):
                        sp.wait_ge(s_gated[c], BATCH)
                    ffn_weights(sp, 1)
                if exists(o):
                    sp.wait_ge(s_x1[0], p)
                    sp.wait_ge(s_x1[1], p)
                    if exists(n - 4):
                        sp.wait_ge(s_h2n, o)
                    sp.dma_start(h2[:, :, 0:64], x1[:, :, 0:64]).then_inc(s_h2, 16)
                    sp.dma_start(h2[1:P, :, 64:DIM], x1[0:P - 1, :, 64:DIM]).then_inc(s_h2, 16)
                    sp.dma_start(h2[0:1, 1, 64:DIM], x1[P - 1:P, 0, 64:DIM]).then_inc(s_h2, 16)
                if isinstance(o, int) and o == BATCH:
                    sp.wait_ge(s_ffnw, 32 * FFN_DMAS)
                if exists(o):
                    sp.sem_inc(s_params, 1)
                if exists(u):
                    if exists(p):
                        sp.wait_ge(s_o_ps[0], u)
                        sp.wait_ge(s_vmix, mixed_before)
                    sp.wait_ge(s_v[0], n)
                    sp.dma_start(V0[:, :], V0_next[:, :]).then_inc(s_V0, 16)
                if norm:
                    sp.wait_ge(s_fout, b + 1)
                    sp.dma_start(out_v[:, bass.ds(b, 1), :, :].rearrange("p o t d -> p (o t) d"), f_out[:, :, :]
                                 ).then_inc(s_fdma, 16)

            out_v = out.rearrange("b (t p) d -> p b t d", p=P)
            place_stream(0)
            sp.wait_ge(s_ffnw, 16 * FFN_DMAS)
            body(0, False)
            body(1, False)
            place_stream(1)
            for n in range(2, FULL + 1):
                body(n, False)
            switch = BATCH + 3
            with sp.Fori(FULL + 1, switch) as n:
                body(n, False)
            body(switch, False)
            with sp.Fori(LAST_NORM + 1, STEPS) as n:
                body(n, True)
            for n in range(STEPS, STEPS + 4):
                body(n, True)
            sp.wait_ge(s_fdma, 16 * BATCH)

        @block.gpsimd
        def _(pool):
            pool.wait_ge(s_tab, 16 * TAB_DMAS)
            for l in range(DEPTH):
                for t in range(TILES):
                    for kind in range(4):
                        scale = head_scale[:, l, kind // 2, :]
                        table, to = rot_const[:, t, kind, :], rot_tab[:, l, t, kind, :]
                        if kind % 2:
                            scale, table, to = (a.rearrange("p (s d) -> p s d", s=2) for a in (scale, table, to))
                            scale = scale[:, ::-1, :]
                        nc.gpsimd.tensor_tensor(to, table, scale, ALU.mult).then_inc(s_rot, 1)
            for l in range(DEPTH):
                pool.wait_ge(s_whi, l + 1)
                nc.gpsimd.tensor_tensor(wqkv_lo[:, l, :, :], wqkv_sb[:, l, :, :], wqkv_hi[:, l, :, :].bitcast(F32),
                                        ALU.subtract).then_inc(s_wlo, 1)
            pool.wait_ge(s_setup, 5)

            def a_power(half):
                part = slice(half * A_HALF, half * A_HALF + A_HALF)
                pool.wait_ge(s_ave, half + 1)
                nc.gpsimd.tensor_tensor(a_rstd[:, part, :].rearrange("p b i -> p (b i)"),
                                        a_ve[:, part, :].rearrange("p b i -> p (b i)"),
                                        minus_half[:, 0:2 * A_HALF], ALU.pow).then_inc(s_arstd, 1)

            def add_rotated(n, t, which):
                pool.wait_ge((s_q_rotd, s_k_rotd)[which][t], n + 1)
                if which == 0 and exists(n - 1):
                    pool.wait_ge(s_qT_ps[t], n)
                nc.gpsimd.tensor_tensor((qrot, krot)[which][t][:, :], rot_c[t][:, which, :], rot_s[t][:, which, :],
                                        ALU.add).then_inc((s_qrot, s_krot)[which][t], 1)

            def normalize_k(n, t):
                pool.wait_ge(s_ssf[t], n + 1)
                if exists(n - 1):
                    pool.wait_ge(s_sc8[t], n)
                nc.gpsimd.tensor_tensor(rnorm[t][:, :], ssf[:, :], minus_half[:, :], ALU.pow).then_inc(s_rnorm[t], 1)
                pool.wait_ge(s_rnorm[t], n + 1)
                pool.wait_ge(s_krot[t], n + 1)
                if exists(n - 1):
                    pool.wait_ge(s_kT_ps[t], n)
                nc.gpsimd.tensor_tensor(heads(knorm[t][:, :]), heads(krot[t][:, :]),
                                        rnorm[t][:, HEADS:].unsqueeze(2).broadcast_to([P, HEADS, DH]), ALU.mult
                                        ).then_inc(s_knorm[t], 1)

            def body(u, norm):
                p, o, b = u - 1, u - 2, u - LAST_NORM
                if exists(p):
                    normalize_k(p, 1)
                if exists(u):
                    add_rotated(u, 0, 0)
                    add_rotated(u, 0, 1)
                    normalize_k(u, 0)
                if norm:
                    pool.wait_ge(s_fve, b + 1)
                    nc.gpsimd.tensor_tensor(f_rstd[:, :], f_ve[:, :], minus_half[:, 0:TILES], ALU.pow
                                            ).then_inc(s_frstd, 1)
                if exists(u):
                    add_rotated(u, 1, 0)
                if exists(o):
                    pool.wait_ge(s_ve, o + 1)
                    nc.gpsimd.tensor_tensor(rstd[:, :], ve[:, :], minus_half[:, 0:TILES], ALU.pow).then_inc(s_rstd, 1)
                if exists(u):
                    add_rotated(u, 1, 1)
                if exists(o):
                    pool.wait_ge(s_x1[0], o + 1)
                    pool.wait_ge(s_x1[1], o + 1)
                    pool.wait_ge(s_params, o + 1)
                    if exists(o - 1):
                        pool.wait_ge(x_ready, BATCH + o)
                    nc.gpsimd.tensor_tensor(x1b[:, :, :], x1[:, :, :],
                                            b2_sb[:, :].unsqueeze(1).broadcast_to([P, TILES, DIM]), ALU.add
                                            ).then_inc(s_x1b, 1)

            a_power(0)
            body(0, False)
            a_power(1)
            walk(pool, body, 1)

        @block.tensor
        def _(pe):
            def a_transpose(b):
                pe.wait_ge(s_ain, b + 1)
                if exists(b - 1):
                    pe.wait_ge(s_axTg, b)
                nc.tensor.transpose(bank_q[:, 0:P], a_in[:, :], ident[:, :]).then_inc(s_axT_ps, 1)

            def a_scores(b):
                pe.wait_ge(s_axT, b + 1)
                pe.wait_ge(s_axTg, b + 1)
                if exists(b - 1):
                    pe.wait_ge(s_adif, b)
                for s in range(2):
                    for g in range(4):
                        dims = slice(32 * g, 32 * g + 32)
                        last = nc.tensor.matmul(
                            bank_as[64 * s:64 * s + 64, g, :],
                            a_xT[dims, 64 * s:64 * s + 64],
                            a_xTg[dims, s, :, :].rearrange("p m j -> p (m j)"), start=True, stop=True)
                last.then_inc(s_as, 1)

            def a_values(b):
                pe.wait_ge(s_aexp, b + 1)
                for half, bank in ((0, bank_t0), (1, bank_t1)):
                    if exists(b - 1):
                        pe.wait_ge(s_aT[half], b)
                    for j in range(4):
                        pair = 4 * half + j
                        last = nc.tensor.transpose(
                            bank[:, P * j:P * j + P],
                            a_exp[:, 2 * pair:2 * pair + 2, :].rearrange("p h j -> p (h j)"), ident[:, :])
                    last.then_inc(s_aT_ps[half], 1)
                pe.wait_ge(s_av, b + 1)
                if exists(b - 1):
                    pe.wait_ge(s_ao9, b)
                for half in range(2):
                    pe.wait_ge(s_aT[half], b + 1)
                    for pair in range(4 * half, 4 * half + 4):
                        for s in range(2):
                            last = nc.tensor.matmul(
                                bank_o[64 * s:64 * s + 64, 18 * pair:18 * pair + 18],
                                a_expT[:, pair, 64 * s:64 * s + 64],
                                a_v[:, s, pair, :, :].rearrange("p h d -> p (h d)"), start=True, stop=True)
                last.then_inc(s_ao_ps, 1)

            pe.wait_ge(s_const, 16 * CONST_DMAS)
            pe.wait_ge(s_setup, 5)
            a_transpose(0)
            a_scores(0)
            a_transpose(1)

            def a_body(b):
                a_scores(b + 1)
                if not isinstance(b, int) or b + 2 < BATCH:
                    a_transpose(b + 2)
                a_values(b)

            a_body(0)
            with pe.Fori(1, BATCH - 2) as b:
                a_body(b)
            a_body(BATCH - 2)
            a_values(BATCH - 1)

            def transpose_h(n):
                pe.wait_ge(s_xs, 16 * n + 16)
                if exists(n - 1):
                    pe.wait_ge(s_q_sq[1], n)
                else:
                    pe.wait_ge(s_axTg, BATCH)
                for t in range(TILES):
                    last = nc.tensor.transpose(bank_q[:, P * t:P * t + P], xs[:, t, :], ident[:, :])
                last.then_inc(s_hT_ps, 1)

            def project(n, t, which):
                bank, done = [(bank_q, s_q_ps), (bank_k, s_k_ps), (bank_v, s_v_ps)][which]
                pe.wait_ge(s_hT, n + 1)
                last_reader = (s_q_sq, s_k_sq, s_v)[which]
                if t == 1:
                    pe.wait_ge(last_reader[0], n + 1)
                elif exists(n - 1):
                    pe.wait_ge(last_reader[1], n)
                if t == 0 and exists(n - 3):
                    pe.wait_ge(s_gated[which], n - 2)
                for i, (h, w) in enumerate(((hT_hi, wqkv_hi), (hT_hi, wqkv_lo), (hT_lo, wqkv_hi))):
                    last = nc.tensor.matmul(bank[:, :], h[:, P * t:P * t + P],
                                            w[:, bass.ds(layer(n), 1), which, :].rearrange("p o n -> p (o n)"),
                                            start=(i == 0), stop=(i == 2))
                last.then_inc(done[t], 1)

            def transpose_q(n, t):
                pe.wait_ge(s_qrot[t], n + 1)
                if t == 0:
                    if exists(n - 1):
                        pe.wait_ge(s_pbT[0], n)
                    else:
                        pe.wait_ge(s_aT[0], BATCH)
                else:
                    pe.wait_ge(s_qT[0], n + 1)
                    if exists(n - 1):
                        pe.wait_ge(s_paT[1], n)
                for j in range(BLOCKS):
                    last = nc.tensor.transpose(bank_t0[:, P * j:P * j + P], qrot[t][:, P * j:P * j + P], ident[:, :])
                last.then_inc(s_qT_ps[t], 1)

            def transpose_k(n, t):
                pe.wait_ge(s_knorm[t], n + 1)
                if t == 0:
                    if exists(n - 1):
                        pe.wait_ge(s_paT[0], n)
                    else:
                        pe.wait_ge(s_aT[1], BATCH)
                else:
                    pe.wait_ge(s_kT[0], n + 1)
                    if exists(n - 1):
                        pe.wait_ge(s_pbT[1], n)
                for j in range(BLOCKS):
                    last = nc.tensor.transpose(bank_t1[:, P * j:P * j + P], knorm[t][:, P * j:P * j + P], ident[:, :])
                last.then_inc(s_kT_ps[t], 1)

            def scores(n, t):
                pe.wait_ge(s_qT[t], n + 1)
                pe.wait_ge(s_kT[t], n + 1)
                if t == 1:
                    pe.wait_ge(s_pb[0], n + 1)
                elif exists(n - 1):
                    pe.wait_ge(s_pb[1], n)
                for half in range(2):
                    nc.tensor.matmul(bank_s[:, half, :].rearrange("p (h j) -> p h j", h=4), ident_bf[:, :],
                                     mask_bf[:, t, :].unsqueeze(1).broadcast_to([P, 4, P]),
                                     start=True, stop=False, skip_group_check=True)
                for h in range(HEADS):
                    dims = slice(64 * (h % 2), 64 * (h % 2) + 64)
                    bank, col = bank_s[:, h % 2, :], P * (h // 2)
                    keys = kT[dims, h // 2, :].rearrange("p (w j) -> p w j", j=64)
                    if t == 0:
                        even, width = keys[:, 0:1, :], 64
                    else:
                        even, width = keys[:, 2:0:-1, :], P
                    nc.tensor.matmul(bank[0:64, col:col + width].rearrange("p (w j) -> p w j", j=64),
                                     qT[t][dims, h // 2, 0:64], even,
                                     start=False, stop=True, skip_group_check=True)
                    last = nc.tensor.matmul(bank[64:P, col:col + P],
                                            qT[t][dims, h // 2, 64:P],
                                            kT[dims, h // 2, P * t:P * t + P],
                                            start=False, stop=True, skip_group_check=True)
                last.then_inc(s_s_ps[t], 1)

            def transpose_p(n, t, half):
                bank = (bank_t0, bank_t1)[half if t else 1 - half]
                pe.wait_ge((s_pa, s_pb)[half][t], n + 1)
                if t == 1:
                    if exists(n + 1):
                        pe.wait_ge((s_qT, s_kT)[half][0], n + 2)
                    else:
                        pe.wait_ge((s_pbT, s_paT)[half][0], n + 1)
                elif half == 0:
                    pe.wait_ge(s_kT[1], n + 1)
                elif exists(n - 1):
                    pe.wait_ge(s_oT[1], n)
                else:
                    pe.wait_ge(s_qT[1], n + 1)
                for j in range(4):
                    last = nc.tensor.transpose(bank[:, P * j:P * j + P], probs[t][:, 4 * half + j, :], ident[:, :])
                last.then_inc((s_paT_ps, s_pbT_ps)[half][t], 1)

            def attend(n, t):
                if t == 0:
                    pe.wait_ge(s_V0, 16 * n + 16)
                    if exists(n - 1):
                        pe.wait_ge(s_x1[1], n)
                    else:
                        pe.wait_ge(s_ao9, BATCH)
                else:
                    pe.wait_ge(s_vmix, 48 * n + 48)
                    pe.wait_ge(s_x1[0], n + 1)
                for half in range(2):
                    pe.wait_ge((s_paT, s_pbT)[half][t], n + 1)
                    for h in range(half, HEADS, 2):
                        cols = slice(DH * h, DH * h + DH)
                        last = nc.tensor.matmul(bank_o[64:P, cols], probsT[:, SLOT[h], 64:P],
                                                (V1 if t else V0)[:, cols], start=True, stop=True)
                        if t == 1:
                            last = nc.tensor.matmul(bank_o[0:64, cols], probsT[:, SLOT[h], 0:64], Vmix[:, cols],
                                                    start=True, stop=True)
                if t == 0:
                    for h in range(HEADS):
                        cols = slice(DH * h, DH * h + DH)
                        last = nc.tensor.matmul(bank_o[0:64, cols], probsT[0:64, SLOT[h], 0:64], V0[0:64, cols],
                                                start=True, stop=True)
                last.then_inc(s_o_ps[t], 1)

            def transpose_o(n, t):
                bank = bank_t0 if t else bank_o
                pe.wait_ge(s_o[t], n + 1)
                if t == 0:
                    pass
                elif exists(n + 1):
                    pe.wait_ge(s_qT[1], n + 2)
                else:
                    pe.wait_ge(s_paT[1], n + 1)
                for j in range(BLOCKS):
                    last = nc.tensor.transpose(bank[:, P * j:P * j + P], o_sb[:, P * j:P * j + P], ident[:, :])
                last.then_inc(s_oT_ps[t], 1)

            def project_o(n, t):
                pe.wait_ge(s_oT[t], n + 1)
                pe.wait_ge(s_o[t], n + 1)
                if t == 1 and exists(n - 1):
                    pe.wait_ge(x_ready, BATCH + n)
                for j in range(BLOCKS):
                    last = nc.tensor.matmul(bank_o[:, 0:DIM], oT[:, j, :],
                                            wo_sb[:, bass.ds(layer(n), 1), j, :].rearrange("p o n -> p (o n)"),
                                            start=(j == 0), stop=(j == BLOCKS - 1))
                last.then_inc(s_wo_ps[t], 1)

            def transpose_h2(n):
                pe.wait_ge(s_h2n, n + 1)
                pe.wait_ge(s_k_sq[1], (n + 3) if exists(n + 2) else STEPS)
                for t in range(TILES):
                    last = nc.tensor.transpose(bank_k[:, P * t:P * t + P], h2n[:, t, :], ident[:, :])
                last.then_inc(s_h2T_ps, 1)

            def ffn_up(n):
                pe.wait_ge(s_params, n + 1)
                pe.wait_ge(s_h2T, n + 1)
                for c, (at, size) in enumerate(CHUNKS):
                    if c == 0 and exists(n + 3):
                        pe.wait_ge(s_hT, n + 4)
                    else:
                        pe.wait_ge((s_q_sq[1], s_k_sq[1], s_v[1])[c], (n + 3) if exists(n + 2) else STEPS)
                    if exists(n - 1):
                        pe.wait_ge(s_gated[c], n)
                    bank = (bank_q, bank_k, bank_v)[c]
                    for half in range(2):
                        last = nc.tensor.matmul(bank[0:size, SEQ * half:SEQ * half + SEQ],
                                                w1_sb[:, half * HID + at:half * HID + at + size], h2T[:, :],
                                                start=True, stop=True)
                    last.then_inc(s_w1_ps[c], 1)

            def ffn_down(n):
                if exists(n + 1):
                    pe.wait_ge(s_o[1], n + 2)
                else:
                    pe.wait_ge(s_x1[1], STEPS)
                for t in range(TILES):
                    for c, (at, size) in enumerate(CHUNKS):
                        pe.wait_ge(s_gated[c], n + 1)
                        last = nc.tensor.matmul(bank_o[:, DIM * t:DIM * t + DIM],
                                                gated[0:size, c, P * t:P * t + P],
                                                w2_sb[0:size, bass.ds(layer(n), 1), c, :].rearrange("p o n -> p (o n)"),
                                                start=(c == 0), stop=(c == 2))
                last.then_inc(s_w2_ps, 1)

            def body(u, norm):
                p, o, f = u - 1, u - 2, u - 3
                if exists(p):
                    transpose_q(p, 0)
                    transpose_k(p, 0)
                if exists(o):
                    transpose_o(o, 0)
                    transpose_p(o, 1, 0)
                    project_o(o, 0)
                if exists(f):
                    transpose_h2(f)
                if exists(o):
                    transpose_p(o, 1, 1)
                if exists(p):
                    scores(p, 0)
                if exists(f):
                    ffn_up(f)
                if exists(o):
                    attend(o, 1)
                if exists(u):
                    project(u, 0, 0)
                    project(u, 0, 1)
                    project(u, 0, 2)
                if exists(p):
                    transpose_q(p, 1)
                    transpose_k(p, 1)
                if exists(f):
                    ffn_down(f)
                if exists(u):
                    project(u, 1, 0)
                if exists(o):
                    transpose_o(o, 1)
                if exists(u):
                    project(u, 1, 1)
                if exists(o):
                    project_o(o, 1)
                if exists(u):
                    project(u, 1, 2)
                if exists(p):
                    transpose_p(p, 0, 0)
                    transpose_p(p, 0, 1)
                if exists(u + 1):
                    transpose_h(u + 1)
                if exists(p):
                    scores(p, 1)
                    attend(p, 0)

            pe.wait_ge(s_wlo, DEPTH)
            pe.wait_ge(s_bf, 2)
            pe.wait_ge(s_wts, 16 * WTS_DMAS)
            walk(pe, body)

        @block.scalar
        def _(act):
            def a_exps(b):
                act.wait_ge(s_adif, b + 1)
                if exists(b - 1):
                    act.wait_ge(s_aT_ps[1], b)
                nc.scalar.activation(a_exp[:, :, :], a_dif[:, :, :], ACT.Exp, scale=A_DH ** -0.5).then_inc(s_aexp, 1)

            def a_copy(b):
                act.wait_ge(s_aT_ps[0], b + 1)
                if exists(b - 1):
                    act.wait_ge(s_ao_ps, b)
                nc.scalar.activation(a_expT[:, 0:4, :].rearrange("p a b -> p (a b)"), bank_t0[:, :], ACT.Copy
                                     ).then_inc(s_aT[0], 1)

            a_exps(0)
            a_copy(0)
            a_exps(1)
            for l in range(DEPTH):
                act.wait_ge(s_wqkv, 16 * DEPTH)
                nc.scalar.activation(wqkv_hi[:, l, :, :], wqkv_sb[:, l, :, :], ACT.Copy).then_inc(s_whi, 1)
            with act.Fori(1, BATCH - 1) as b:
                a_copy(b)
                a_exps(b + 1)
            a_copy(BATCH - 1)

            def squares_of(n, t, which):
                rotd, done = ((s_q_rotd, s_q_sq), (s_k_rotd, s_k_sq))[which]
                act.wait_ge(rotd[t], n + 1)
                if t == 1:
                    act.wait_ge(s_ss[0], n + 1)
                elif exists(n - 1):
                    act.wait_ge(s_ss[1], n)
                nc.scalar.activation(squares[:, which, :], (bank_q, bank_k)[which][:, :], ACT.Square
                                     ).then_inc(done[t], 1)

            def exps(n, t, half):
                act.wait_ge(s_nbias[t], n + 1)
                if half == 0 and exists(n - 1):
                    act.wait_ge(s_pbT_ps[t], n)
                for h in range(4 * half, 4 * half + 4):
                    last = nc.scalar.activation(probs[t][:, h, :], bank_s[:, half, P * (h % 4):P * (h % 4) + P],
                                                ACT.Exp, bias=nbias[t][:, h:h + 1], scale=sc8[t][:, h:h + 1],
                                                accum_out=psums[t][:, h:h + 1])
                last.then_inc((s_pa, s_pb)[half][t], 1)

            def copy_qT(n):
                act.wait_ge(s_qT_ps[1], n + 1)
                nc.scalar.activation(qT[1][:, :, :].rearrange("p a b -> p (a b)"), bank_t0[:, :], ACT.Copy
                                     ).then_inc(s_qT[1], 1)

            def copy_oT(n, t):
                act.wait_ge(s_oT_ps[t], n + 1)
                if t == 1:
                    act.wait_ge(s_wo_ps[0], n + 1)
                elif exists(n - 1):
                    act.wait_ge(s_wo_ps[1], n)
                nc.scalar.activation(oT[:, :, :].rearrange("p a b -> p (a b)"), bank_t0 if t else bank_o, ACT.Copy
                                     ).then_inc(s_oT[t], 1)

            def copy_v(n, t):
                act.wait_ge(s_v_ps[t], n + 1)
                if exists(n - 1):
                    act.wait_ge(s_vmix if t else s_V0, 48 * n if t else 16 * n)
                nc.scalar.activation((V0_next, V1_next)[t][:, :], bank_v, ACT.Copy).then_inc(s_v[t], 1)

            def gelu_of(n):
                for c, (at, size) in enumerate(CHUNKS):
                    act.wait_ge(s_w1_ps[c], n + 1)
                    if exists(n - 1):
                        act.wait_ge(s_gated[c], n)
                    nc.scalar.activation(gelu[0:size, c, :], (bank_q, bank_k, bank_v)[c][0:size, SEQ:2 * SEQ],
                                         ACT.Gelu, bias=b1_sb[0:size, 1, c:c + 1]).then_inc(s_gelu[c], 1)

            def copy_pT(n, half):
                arrived, bank, done = ((s_paT_ps, bank_t1, s_paT), (s_pbT_ps, bank_t0, s_pbT))[half]
                act.wait_ge(arrived[0], n + 1)
                if exists(n - 1):
                    act.wait_ge(s_o_ps[1], n)
                nc.scalar.activation(probsT[:, 4 * half:4 * half + 4, :].rearrange("p a b -> p (a b)"), bank, ACT.Copy
                                     ).then_inc(done[0], 1)

            def load_table(function, uses_before):
                if not isinstance(uses_before, int) or uses_before > 0:
                    act.wait_ge(s_table, uses_before)
                nc.scalar.activation(table_use[:, :], minus_half[:, 0:1], function).then_inc(s_table, 1)

            def body(u, norm):
                p, o, f = u - 1, u - 2, u - 3
                if exists(f):
                    gelu_of(f)
                    load_table(ACT.Exp, 2 * f + 1)
                if exists(p):
                    exps(p, 0, 0)
                if exists(u):
                    squares_of(u, 0, 0)
                if exists(p):
                    exps(p, 0, 1)
                if exists(u):
                    squares_of(u, 0, 1)
                if exists(p):
                    copy_qT(p)
                if exists(o):
                    copy_oT(o, 1)
                if exists(u):
                    copy_v(u, 0)
                    squares_of(u, 1, 0)
                    squares_of(u, 1, 1)
                    copy_v(u, 1)
                if exists(p):
                    copy_pT(p, 0)
                    copy_pT(p, 1)
                    exps(p, 1, 0)
                    copy_oT(p, 0)
                    exps(p, 1, 1)
                if exists(o):
                    load_table(ACT.Gelu, 2 * o)

            act.wait_ge(s_setup, 5)
            walk(act, body)

        @block.vector
        def _(dve):
            def a_transposed(b):
                if exists(b - 1):
                    dve.wait_ge(s_axT_ps, b)
                nc.vector.tensor_scalar(a_in[:, :], a_x[:, bass.ds(b, 1), 0, :].rearrange("p o d -> p (o d)"),
                                        1.0, None, ALU.mult).then_inc(s_ain, 1)
                dve.wait_ge(s_axT_ps, b + 1)
                if exists(b - 1):
                    dve.wait_ge(s_as, b)
                nc.vector.tensor_copy(a_xT[:, :], bank_q[:, 0:P]).then_inc(s_axT, 1)
                for s in range(2):
                    last = nc.vector.tensor_tensor(
                        a_xTg[:, s, :, :],
                        bank_q[:, 64 * s:64 * s + 64].unsqueeze(1).broadcast_to([P, 4, A_KEYS]),
                        group[:, :].unsqueeze(2).broadcast_to([P, 4, A_KEYS]), ALU.mult)
                last.then_inc(s_axTg, 1)

            def a_softmax(b):
                dve.wait_ge(s_as, b + 1)
                scores = bank_as.rearrange("p g (m j) -> p g m j", j=A_KEYS)
                nc.vector.tensor_reduce(a_max[:, :], scores, AX.X, ALU.max).then_inc(s_amax, 1)
                dve.wait_ge(s_amax, b + 1)
                if exists(b - 1):
                    dve.wait_ge(s_aexp, b)
                nc.vector.tensor_tensor(a_dif[:, :, :].rearrange("p (g m) j -> p g m j", g=4), scores,
                                        a_max[:, :].rearrange("p (g m) -> p g m", g=4).unsqueeze(3
                                                              ).broadcast_to([P, 4, 4, A_KEYS]), ALU.subtract
                                        ).then_inc(s_adif, 1)

            def a_values(b):
                if exists(b - 1):
                    dve.wait_ge(s_ao_ps, b)
                for half in range(2):
                    rows = slice(64 * half, 64 * half + 64)
                    for s in range(2):
                        last = nc.vector.tensor_scalar(
                            a_v[rows, s, :, half, 0:A_DH],
                            a_xv[rows, bass.ds(b, 1), s, :].rearrange("p o (a h d) -> p (o a) h d", h=2, d=A_DH)[:, :, half, :],
                            1.0, None, ALU.mult)
                last.then_inc(s_av, 1)

            def a_copies(b):
                dve.wait_ge(s_aT_ps[1], b + 1)
                if exists(b - 1):
                    dve.wait_ge(s_ao_ps, b)
                nc.vector.tensor_copy(a_expT[:, 4:8, :].rearrange("p a b -> p (a b)"), bank_t1[:, :]).then_inc(s_aT[1], 1)

            def a_output(b):
                dve.wait_ge(s_ao_ps, b + 1)
                nc.vector.tensor_scalar(a_o9[:, bass.ds(b, 1), :, :].rearrange("p o h d -> p (o h d)"),
                                        bank_o[:, 0:A_HEADS * (A_DH + 1)], 1.0, None, ALU.mult).then_inc(s_ao9, 1)

            def a_finish(half):
                part = slice(half * A_HALF, half * A_HALF + A_HALF)
                n = half + 1
                dve.wait_ge(s_ao9, n * A_HALF)
                nc.vector.reciprocal(a_rec[:, part, :].unsqueeze(3), a_o9[:, part, :, A_DH:A_DH + 1]).then_inc(s_arec, 1)
                dve.wait_ge(s_arec, n)
                nc.vector.tensor_tensor(a_o[:, part, :, :], a_o9[:, part, :, 0:A_DH],
                                        a_rec[:, part, :].unsqueeze(3).broadcast_to([P, A_HALF, A_HEADS, A_DH]),
                                        ALU.mult).then_inc(s_ao, 1)
                dve.wait_ge(s_ao, n)
                flat = a_o[:, part, :, :].rearrange("p b h d -> p b (h d)")
                nc.vector.tensor_reduce(a_den[:, part], flat, AX.X, ALU.add).then_inc(s_aden, 1)
                dve.wait_ge(s_aden, n)
                nc.vector.reciprocal(a_rden[:, part], a_den[:, part]).then_inc(s_arden, 1)
                dve.wait_ge(s_arden, n)
                nc.vector.tensor_tensor(a_alpha[:, part], a_den[:, part], a_rden[:, part], ALU.mult).then_inc(s_aalpha, 1)
                dve.wait_ge(s_aalpha, n)
                for b in range(half * A_HALF, half * A_HALF + A_HALF):
                    last = nc.vector.scalar_tensor_tensor(
                        a_y[:, b, :], a_o[:, b, :, :].rearrange("p h d -> p (h d)"), a_alpha[:, b:b + 1],
                        a_x[:, b, 0, :], ALU.mult, ALU.add)
                last.then_inc(s_ay, 1)
                dve.wait_ge(s_ay, n)
                for b in range(half * A_HALF, half * A_HALF + A_HALF):
                    nc.vector.bn_stats(a_st[:, b, 0, :], a_y[:, b, :])
                    last = nc.vector.bn_stats(a_st[:, b, 1, :], a_x[:, b, 1, :])
                last.then_inc(s_ast, 1)
                nc.vector.memset(a_ve[:, part, :], EPS)
                dve.wait_ge(s_ast, n)
                for b in range(half * A_HALF, half * A_HALF + A_HALF):
                    for i in range(2):
                        last = nc.vector.bn_aggr(a_mv[:, b, i, :], a_st[:, b, i, :])
                last.then_inc(s_amv, 1)
                dve.wait_ge(s_amv, n)
                nc.vector.tensor_tensor(a_ve[:, part, :], a_ve[:, part, :], a_mv[:, part, :, 1], ALU.add
                                        ).then_inc(s_ave, 1)
                dve.wait_ge(s_arstd, n)
                for b in range(half * A_HALF, half * A_HALF + A_HALF):
                    for i, src in enumerate((a_y[:, b, :], a_x[:, b, 1, :])):
                        last = nc.vector.tensor_scalar(a_xn[:, b, i, :], src, a_mv[:, b, i, 0:1],
                                                       a_rstd[:, b, i:i + 1], ALU.subtract, ALU.mult)
                last.then_inc(s_axn, 1)

            def a_body(b):
                if not isinstance(b, int) or b + 2 < BATCH:
                    a_transposed(b + 2)
                a_softmax(b + 1)
                a_values(b)
                a_copies(b)
                a_output(b)

            nc.vector.memset(a_v[:, :, :, :, :], 0.0).then_inc(s_zero, 1)
            nc.vector.memset(minus_half[:, :], -0.5).then_inc(s_setup, 1)
            nc.vector.memset(hT_hi[64:P, 0:1].bitcast(F32), 0.0)
            nc.vector.memset(hT_lo[64:P, 0:1].bitcast(F32), 0.0).then_inc(s_setup, 1)
            nc.vector.memset(h2[0:1, 0, 64:DIM], 0.0).then_inc(s_setup, 1)
            dve.wait_ge(s_zero, 1)
            nc.vector.memset(a_v[0:64, :, :, 0, A_DH:A_DH + 1], 1.0).then_inc(s_setup, 1)
            nc.vector.memset(a_v[64:P, :, :, 1, A_DH:A_DH + 1], 1.0).then_inc(s_setup, 1)
            dve.wait_ge(s_ax_first, 16)
            dve.wait_ge(s_const, 16 * CONST_DMAS)
            a_transposed(0)
            dve.wait_ge(s_ax, 16 * 5)
            a_transposed(1)
            a_softmax(0)
            a_body(0)
            with dve.Fori(1, A_HALF) as b:
                a_body(b)
            a_finish(0)
            with dve.Fori(A_HALF, BATCH - 2) as b:
                a_body(b)
            a_body(BATCH - 2)
            a_values(BATCH - 1)
            a_copies(BATCH - 1)
            a_output(BATCH - 1)
            dve.wait_ge(s_tab, 16 * TAB_DMAS)
            nc.vector.tensor_copy(ident_bf[:, :], ident[:, :]).then_inc(s_bf, 1)
            nc.vector.tensor_copy(mask_bf[:, :, :], mask32[:, :, :]).then_inc(s_bf, 1)

            def rotate(n, t, which):
                bank, arrived, done = ((bank_q, s_q_ps, s_q_rotd), (bank_k, s_k_ps, s_k_rotd))[which]
                table = rot_tab[:, bass.ds(layer(n), 1), t, :, :]
                dve.wait_ge(arrived[t], n + 1)
                if exists(n - 1):
                    dve.wait_ge((s_qrot, s_krot)[which][t], n)
                nc.vector.tensor_tensor(heads(rot_c[t][:, which, :]), heads(bank[:, :]),
                                        table[:, :, 2 * which, :].broadcast_to([P, HEADS, DH]), ALU.mult)
                half = "p h (s d) -> p h s d"
                nc.vector.tensor_tensor(heads(rot_s[t][:, which, :]).rearrange(half, s=2),
                                        heads(bank[:, :]).rearrange(half, s=2)[:, :, ::-1, :],
                                        table[:, :, 2 * which + 1, :].rearrange(half, s=2
                                                                                ).broadcast_to([P, HEADS, 2, DH // 2]),
                                        ALU.mult).then_inc(done[t], 1)

            def sum_squares(n, t):
                dve.wait_ge(s_q_sq[t], n + 1)
                dve.wait_ge(s_k_sq[t], n + 1)
                nc.vector.tensor_reduce(ss[:, :], squares[:, :, :].rearrange("p w (h d) -> p (w h) d", d=DH),
                                        AX.X, ALU.add).then_inc(s_ss[t], 1)
                dve.wait_ge(s_ss[t], n + 1)
                if t == 1:
                    dve.wait_ge(s_rnorm[0], n + 1)
                elif exists(n - 1):
                    dve.wait_ge(s_rnorm[1], n)
                nc.vector.tensor_scalar(ssf[:, :], ss[:, :], NORM_FLOOR, None, ALU.max).then_inc(s_ssf[t], 1)

            def scale_of_q(n, t):
                dve.wait_ge(s_rnorm[t], n + 1)
                if exists(n - 1):
                    dve.wait_ge(s_pb[t], n)
                nc.vector.tensor_scalar(sc8[t][:, :].rearrange("p (odd j) -> p odd j", odd=2),
                                        rnorm[t][:, 0:HEADS].rearrange("p (j odd) -> p odd j", odd=2),
                                        QK_SCALE, None, ALU.mult).then_inc(s_sc8[t], 1)

            def row_max(n, t):
                dve.wait_ge(s_s_ps[t], n + 1)
                nc.vector.tensor_reduce(smax[t][:, :], bank_s[:, :, :].rearrange("p a (h j) -> p (a h) j", j=P),
                                        AX.X, ALU.max).then_inc(s_smax[t], 1)
                dve.wait_ge(s_smax[t], n + 1)
                dve.wait_ge(s_sc8[t], n + 1)
                nc.vector.scalar_tensor_tensor(nbias[t][:, :], smax[t][:, :], -1.0, sc8[t][:, :],
                                               ALU.mult, ALU.mult).then_inc(s_nbias[t], 1)

            def copy_qT(n):
                dve.wait_ge(s_qT_ps[0], n + 1)
                nc.vector.tensor_copy(qT[0][:, :, :].rearrange("p a b -> p (a b)"), bank_t0[:, :]).then_inc(s_qT[0], 1)

            def copy_kT(n, t):
                dve.wait_ge(s_kT_ps[t], n + 1)
                if exists(n - 1):
                    dve.wait_ge(s_s_ps[1], n)
                nc.vector.tensor_copy(kT[:, :, P * t:P * t + P],
                                      bank_t1[:, :].rearrange("p (a b) -> p a b", a=BLOCKS)).then_inc(s_kT[t], 1)

            def copy_pT(n, half):
                arrived, bank, done = ((s_paT_ps, bank_t0, s_paT), (s_pbT_ps, bank_t1, s_pbT))[half]
                dve.wait_ge(arrived[1], n + 1)
                dve.wait_ge(s_o_ps[0], n + 1)
                nc.vector.tensor_copy(probsT[:, 4 * half:4 * half + 4, :].rearrange("p a b -> p (a b)"),
                                      bank).then_inc(done[1], 1)

            def invert_sums(n, t):
                dve.wait_ge(s_pb[t], n + 1)
                if exists(n - 1):
                    dve.wait_ge(s_o[t], n)
                nc.vector.reciprocal(rsums[t][:, :], psums[t][:, :]).then_inc(s_rsum[t], 1)

            def normalize_o(n, t):
                dve.wait_ge(s_rsum[t], n + 1)
                dve.wait_ge(s_o_ps[t], n + 1)
                if t == 1:
                    dve.wait_ge(s_oT_ps[0], n + 1)
                elif exists(n - 1):
                    dve.wait_ge(s_oT_ps[1], n)
                by_pair = "p (j odd d) -> p j odd d"
                nc.vector.tensor_tensor(o_sb[:, :].rearrange(by_pair, odd=2, d=DH),
                                        bank_o[:, :].rearrange(by_pair, odd=2, d=DH),
                                        rsums[t][:, :].rearrange("p (odd j) -> p j odd", odd=2).unsqueeze(3
                                                                 ).broadcast_to([P, BLOCKS, 2, DH]), ALU.mult
                                        ).then_inc(s_o[t], 1)

            def add_attention(n, t):
                dve.wait_ge(s_wo_ps[t], n + 1)
                if exists(n - 1):
                    dve.wait_ge(s_h2, 48 * n)
                    dve.wait_ge(s_x1b, n)
                nc.vector.tensor_tensor(x1[:, t, :], bank_o[:, 0:DIM],
                                        X[:, bass.ds(n, 1), t, :].rearrange("p o d -> p (o d)"), ALU.add
                                        ).then_inc(s_x1[t], 1)

            def copy_hT(n):
                dve.wait_ge(s_hT_ps, n + 1)
                if exists(n - 1):
                    dve.wait_ge(s_v_ps[1], n)
                parts = (((slice(0, 64), slice(0, SEQ)), bank_q[0:64, 0:SEQ]),
                         ((slice(64, P), slice(1, SEQ)), bank_q[64:P, 0:SEQ - 1]))
                for to, src in parts:
                    last = nc.vector.tensor_copy(hT_hi[to], src)
                last.then_inc(s_hT_hi, 1)
                dve.wait_ge(s_hT_hi, n + 1)
                for to, src in parts:
                    last = nc.vector.tensor_tensor(hT_lo[to], src, hT_hi[to].bitcast(F32), ALU.subtract)
                last.then_inc(s_hT, 1)

            def statistics(n):
                dve.wait_ge(s_h2, 48 * n + 48)
                for t in range(TILES):
                    last = nc.vector.bn_stats(st[:, t, :], h2[:, t, :])
                last.then_inc(s_st, 1)
                dve.wait_ge(s_st, n + 1)
                nc.vector.memset(ve[:, :], EPS)
                for t in range(TILES):
                    last = nc.vector.bn_aggr(mv[:, t, :], st[:, t, :])
                last.then_inc(s_mv, 1)
                dve.wait_ge(s_mv, n + 1)
                nc.vector.tensor_tensor(ve[:, :], ve[:, :], mv[:, :, 1], ALU.add).then_inc(s_ve, 1)

            def normalize_h2(n):
                dve.wait_ge(s_rstd, n + 1)
                if exists(n - 1):
                    dve.wait_ge(s_h2T_ps, n)
                for t in range(TILES):
                    last = nc.vector.tensor_scalar(h2n[:, t, :], h2[:, t, :], mv[:, t, 0:1], rstd[:, t:t + 1],
                                                   ALU.subtract, ALU.mult)
                last.then_inc(s_h2n, 1)

            def copy_h2T(n):
                dve.wait_ge(s_params, n + 1)
                dve.wait_ge(s_h2T_ps, n + 1)
                if exists(n - 1):
                    dve.wait_ge(s_w1_ps[2], n)
                nc.vector.tensor_scalar(h2T[:, :], bank_k[:, 0:SEQ], ln_gb[:, 0:1], ln_gb[:, 1:2],
                                        ALU.mult, ALU.add).then_inc(s_h2T, 1)

            def gate(n):
                for c, (at, size) in enumerate(CHUNKS):
                    dve.wait_ge(s_gelu[c], n + 1)
                    if exists(n - 1):
                        dve.wait_ge(s_w2_ps, n)
                    nc.vector.scalar_tensor_tensor(gated[0:size, c, :], (bank_q, bank_k, bank_v)[c][0:size, 0:SEQ],
                                                   b1_sb[0:size, 0, c:c + 1], gelu[0:size, c, :],
                                                   ALU.add, ALU.mult).then_inc(s_gated[c], 1)

            def add_ffn(n):
                dve.wait_ge(s_w2_ps, n + 1)
                dve.wait_ge(s_x1b, n + 1)
                nc.vector.tensor_tensor(X[:, bass.ds(n + BATCH, 1), :, :].rearrange("p o t d -> p (o t) d"),
                                        bank_o[:, 0:SEQ].rearrange("p (t d) -> p t d", t=TILES), x1b[:, :, :], ALU.add
                                        ).then_inc(x_ready, 1)

            def norm_statistics(b):
                whole = "p o t d -> p (o t) d"
                dve.wait_ge(x_ready, BATCH + STEPS - BATCH + b + 1)
                if exists(b - 1):
                    dve.wait_ge(s_fout, b)
                nc.vector.tensor_tensor(f_y[:, :, :], X[:, bass.ds(b, 1), :, :].rearrange(whole),
                                        X[:, bass.ds(b + STEPS, 1), :, :].rearrange(whole), ALU.add).then_inc(s_fy, 1)
                dve.wait_ge(s_fy, b + 1)
                for t in range(TILES):
                    last = nc.vector.bn_stats(f_st[:, t, :], f_y[:, t, :])
                last.then_inc(s_fst, 1)
                dve.wait_ge(s_fst, b + 1)
                nc.vector.memset(f_ve[:, :], EPS)
                for t in range(TILES):
                    last = nc.vector.bn_aggr(f_mv[:, t, :], f_st[:, t, :])
                last.then_inc(s_fmv, 1)
                dve.wait_ge(s_fmv, b + 1)
                nc.vector.tensor_tensor(f_ve[:, :], f_ve[:, :], f_mv[:, :, 1], ALU.add).then_inc(s_fve, 1)

            def norm_output(b):
                dve.wait_ge(s_frstd, b + 1)
                if exists(b - 1):
                    dve.wait_ge(s_fdma, 16 * b)
                for t in range(TILES):
                    last = nc.vector.tensor_scalar(f_out[:, t, :], f_y[:, t, :], f_mv[:, t, 0:1],
                                                   f_rstd[:, t:t + 1], ALU.subtract, ALU.mult)
                last.then_inc(s_fout, 1)

            def body(u, norm):
                p, o, f, b = u - 1, u - 2, u - 3, u - LAST_NORM
                if exists(p):
                    copy_qT(p)
                    copy_kT(p, 0)
                    scale_of_q(p, 0)
                if exists(f):
                    normalize_h2(f)
                if exists(o):
                    copy_pT(o, 0)
                    add_attention(o, 0)
                if exists(f):
                    copy_h2T(f)
                if exists(o):
                    copy_pT(o, 1)
                    invert_sums(o, 1)
                if exists(p):
                    sum_squares(p, 1)
                    row_max(p, 0)
                if exists(f):
                    gate(f)
                if exists(o):
                    normalize_o(o, 1)
                if exists(u):
                    rotate(u, 0, 0)
                    rotate(u, 0, 1)
                if exists(p):
                    copy_kT(p, 1)
                if exists(f):
                    add_ffn(f)
                if norm:
                    norm_statistics(b)
                if exists(u):
                    sum_squares(u, 0)
                    rotate(u, 1, 0)
                    rotate(u, 1, 1)
                if exists(o):
                    add_attention(o, 1)
                if norm:
                    norm_output(b)
                if exists(u + 1):
                    copy_hT(u + 1)
                if exists(p):
                    invert_sums(p, 0)
                    scale_of_q(p, 1)
                    row_max(p, 1)
                    normalize_o(p, 0)
                if exists(o):
                    statistics(o)

            dve.wait_ge(s_rot, DEPTH * TILES * 4)
            body(-1, False)
            body(0, False)
            a_finish(1)
            walk(dve, body, 1)


_INS = ["L0_attn_x", "L0_ffn_wqkv", "L0_ffn_q_scale", "L0_ffn_k_scale", "L0_ffn_wo", "L0_ffn_ln_g",
        "L0_ffn_ln_b", "L0_ffn_w1", "L0_ffn_b1", "L0_ffn_w2", "L0_ffn_b2"]
_OUTS = [((BATCH, SEQ, DIM), "float32")]


def kernel(**inputs):
    import numpy as _np
    import concourse.bacc as _bacc
    from concourse import mybir as _mybir
    from concourse.bass_utils import run_bass_kernel_spmd as _run

    nc = _bacc.Bacc("TRN2", target_bir_lowering=False, num_devices=1)
    arrays, args = {}, []
    named = [(name, inputs[name]) for name in _INS] + list(table_constants().items())
    for name, a in named:
        a = _np.ascontiguousarray(a)
        arrays[f"in_{name}_dram"] = a
        args.append(nc.dram_tensor(f"in_{name}_dram", a.shape, _mybir.dt.from_np(a.dtype), kind="ExternalInput").ap())
    for i, (shape, dtype) in enumerate(_OUTS):
        dt = _mybir.dt.from_np(_np.dtype(dtype))
        args.append(nc.dram_tensor(f"out_{i}_dram", shape, dt, kind="ExternalOutput").ap())
    build(nc, *args)
    r = _run(nc, [arrays], core_ids=[0])
    got = tuple(r.results[0][f"out_{i}_dram"] for i in range(len(_OUTS)))
    return got[0]
```

```python
from contextlib import ExitStack

import concourse.bass as bass
from concourse import mybir

ALU = mybir.AluOpType
ACT = mybir.ActivationFunctionType
AX = mybir.AxisListType
F32 = mybir.dt.float32
F32R = mybir.dt.float32r
BF16 = mybir.dt.bfloat16

P = 128
BATCH, SEQ, DIM = 8, 256, 128
TILES = SEQ // P
DEPTH, HEADS, DH, WINDOW = 2, 8, 64, 64
INNER = HEADS * DH
BLOCKS = INNER // P
HID = int(DIM * 4 * 2 / 3)
CHUNK = -(-HID // 3)
CHUNKS = [(c * CHUNK, min(CHUNK, HID - c * CHUNK)) for c in range(3)]
STEPS = DEPTH * BATCH
QK_SCALE = 8.0
A_HEADS, A_DH = 16, 8
A_KEYS = 64
A_PAIRS = A_HEADS // 2
EPS = 1e-5
MASKED = -1e30
NORM_FLOOR = 1e-24


def table_constants():
    import numpy as np
    half = np.arange(0, DH, 2, dtype=np.float32)
    inv_freq = (1.0 / np.float32(10000.0) ** (half / np.float32(DH))).astype(np.float32)
    t = np.arange(SEQ, dtype=np.float32)
    freqs = (t[:, None] * inv_freq[None, :]).astype(np.float32)
    freqs = np.concatenate([freqs, freqs], axis=-1).astype(np.float64)
    base = (half + 0.4 * DH) / (1.4 * DH)
    scale = base[None, :].astype(np.float64) ** ((t - SEQ // 2) / float(WINDOW // 2))[:, None]
    scale = np.concatenate([scale, scale], axis=-1)
    sign = np.where(np.arange(DH) < DH // 2, -1.0, 1.0)[None, :]
    kinds = [np.cos(freqs) * scale, sign * np.sin(freqs) * scale,
             np.cos(freqs) / scale, sign * np.sin(freqs) / scale]
    rotary = np.stack(kinds, axis=1).reshape(TILES, P, 4, DH).transpose(1, 0, 2, 3)
    r = np.arange(P)[:, None]
    c = np.arange(P)[None, :]
    even = np.where(c < 64, c <= r, c - 64 >= r)
    odd = np.where(c < 64, c >= r - 64, c - 64 <= r - 64)
    allowed = np.stack([np.where(r < 64, even, odd)] * TILES, axis=1)
    allowed[:64, 0, 64:] = False
    mask = np.where(allowed, 0.0, MASKED)
    ident = np.eye(P)
    group = (np.arange(P)[:, None] // A_DH) % 4 == np.arange(4)[None, :]
    return {"rotary": np.ascontiguousarray(rotary, np.float32), "mask": mask.astype(np.float32),
            "ident": ident.astype(np.float32), "group": group.astype(np.float32)}


def build(nc, x, wqkv, q_scale, k_scale, wo, ln_g, ln_b, w1, b1, w2, b2,
          c_rotary, c_mask, c_ident, c_group, out):
    with ExitStack() as ctx:
        def sb(name, shape, dt=F32):
            return ctx.enter_context(nc.sbuf_tensor(name, shape, dt))

        def psum(name, shape):
            return ctx.enter_context(nc.psum_tensor(name, shape, F32))

        def sem(name):
            return ctx.enter_context(nc.semaphore(name))

        def sem2(name):
            return [sem(f"{name}{t}") for t in range(2)]

        banks = psum("banks", [P, 8, 512])
        bank_q, bank_k, bank_v = (banks[:, i, :] for i in range(3))
        bank_s = banks[:, 3:5, :]
        bank_t0, bank_t1, bank_o = (banks[:, i, :] for i in range(5, 8))
        bank_as = banks[:, 1:5, 0:4 * A_KEYS]
        SLOT = [4 * (h % 2) + h // 2 for h in range(HEADS)]

        ident = sb("ident", [P, P])
        ident_bf = sb("ident_bf", [P, P], BF16)
        mask32 = sb("mask32", [P, TILES, P])
        mask_bf = sb("mask_bf", [P, TILES, P], BF16)
        rot_const = sb("rot_const", [P, TILES, 4, DH])
        rot_tab = sb("rot_tab", [P, DEPTH, TILES, 4, DH])
        head_scale = sb("head_scale", [P, DEPTH, 2, DH])
        group = sb("group", [P, 4])
        minus_half = sb("minus_half", [P, 16])
        table_use = sb("table_use", [P, 1])
        wqkv_sb = sb("wqkv_sb", [P, DEPTH, 3, INNER])
        wqkv_hi = sb("wqkv_hi", [P, DEPTH, 3, INNER], F32R)
        wqkv_lo = sb("wqkv_lo", [P, DEPTH, 3, INNER], F32R)
        wo_sb = sb("wo_sb", [P, DEPTH, BLOCKS, DIM])
        w2_sb = sb("w2_sb", [CHUNK, DEPTH, 3, DIM])
        ln_gb = sb("ln_gb", [P, 2])
        b1_sb = sb("b1_sb", [CHUNK, 2, 3])
        b2_sb = sb("b2_sb", [P, DIM])

        X = sb("X", [P, (DEPTH + 1) * BATCH, TILES, DIM])

        a_x = sb("a_x", [P, BATCH, 2, DIM])
        a_xv = sb("a_xv", [P, BATCH, 2, DIM])
        a_in = sb("a_in", [P, DIM])
        a_xT = sb("a_xT", [P, P])
        a_max = sb("a_max", [P, A_HEADS])
        a_v = sb("a_v", [P, 2, A_PAIRS, 2, A_DH + 1])
        a_o9 = sb("a_o9", [P, BATCH, A_HEADS, A_DH + 1])
        a_rec = sb("a_rec", [P, BATCH, A_HEADS])
        a_o = sb("a_o", [P, BATCH, A_HEADS, A_DH])
        a_den = sb("a_den", [P, BATCH])
        a_rden = sb("a_rden", [P, BATCH])
        a_alpha = sb("a_alpha", [P, BATCH])
        a_y = sb("a_y", [P, BATCH, DIM])
        a_st = sb("a_st", [P, BATCH, 2, 6])
        a_mv = sb("a_mv", [P, BATCH, 2, 2])
        a_ve = sb("a_ve", [P, BATCH, 2])
        a_rstd = sb("a_rstd", [P, BATCH, 2])
        a_xn = sb("a_xn", [P, BATCH, 2, DIM])

        xs = sb("xs", [P, TILES, DIM])
        hT_hi = sb("hT_hi", [P, SEQ], F32R)
        hT_lo = sb("hT_lo", [P, SEQ], F32R)
        rot_c = [sb(f"rot_c{i}", [P, 2, INNER]) for i in range(2)]
        rot_s = [sb(f"rot_s{i}", [P, 2, INNER]) for i in range(2)]
        squares = sb("squares", [P, 2, INNER])
        ss = sb("ss", [P, 2 * HEADS])
        ssf = sb("ssf", [P, 2 * HEADS])
        rnorm = [sb(f"rnorm{i}", [P, 2 * HEADS]) for i in range(2)]
        qrot = [sb(f"qrot{i}", [P, INNER]) for i in range(2)]
        krot = [sb(f"krot{i}", [P, INNER]) for i in range(2)]
        knorm = [sb(f"knorm{i}", [P, INNER]) for i in range(2)]
        qT = [sb(f"qT{i}", [P, BLOCKS, P]) for i in range(2)]
        kT = sb("kT", [P, BLOCKS, SEQ])
        sc8 = [sb(f"sc8_{i}", [P, HEADS]) for i in range(2)]
        smax = [sb(f"smax{i}", [P, HEADS]) for i in range(2)]
        nbias = [sb(f"nbias{i}", [P, HEADS]) for i in range(2)]
        probs = [sb(f"probs{i}", [P, HEADS, P]) for i in range(2)]
        psums = [sb(f"psums{i}", [P, HEADS]) for i in range(2)]
        rsums = [sb(f"rsums{i}", [P, HEADS]) for i in range(2)]
        probsT = sb("probsT", [P, HEADS, P])
        V0_next = sb("V0_next", [P, INNER])
        V0 = sb("V0", [P, INNER])
        V1_next = sb("V1_next", [P, INNER])
        V1 = sb("V1", [P, INNER])
        Vmix = sb("Vmix", [P, INNER])
        o_sb = sb("o_sb", [P, INNER])
        oT = sb("oT", [P, BLOCKS, P])
        x1_parts = sb("x1_parts", [P, TILES, 3, DIM // 2])
        x1 = x1_parts[:, :, ::2, :]
        h2 = x1_parts[:, :, 0:2, :].rearrange("p t s d -> p t (s d)")
        x1b = mask32
        h2n = sb("h2n", [P, TILES, DIM])
        st = sb("st", [P, TILES, 6])
        mv = sb("mv", [P, TILES, 2])
        ve = sb("ve", [P, TILES])
        rstd = sb("rstd", [P, TILES])
        h2T = sb("h2T", [P, SEQ])
        last_steps = X[:, (DEPTH + 1) * BATCH - 6:(DEPTH + 1) * BATCH, :, :].rearrange("p (l n) t d -> p l (n t d)", l=2)
        w1_raw = last_steps[:, :, 0:2 * HID]
        split = wqkv_sb[:, 0, :, :].rearrange("p k (c n) -> p (k c) n", n=SEQ)
        gelu, gated = split[0:CHUNK, 0:3, :], split[0:CHUNK, 3:6, :]
        split = wqkv_sb[:, 1, :, :].rearrange("p k (c t d) -> p (k c) t d", t=TILES, d=DIM)
        f_y, f_out = split[:, 0, :, :], split[:, 1, :, :]
        f_st = sb("f_st", [P, TILES, 6])
        f_mv = sb("f_mv", [P, TILES, 2])
        f_ve = sb("f_ve", [P, TILES])
        f_rstd = sb("f_rstd", [P, TILES])

        with ExitStack() as first:
            def sb_first(name, shape):
                return first.enter_context(nc.sbuf_tensor(name, shape, F32))

            a_dif = sb_first("a_dif", [P, A_HEADS, A_KEYS])
            a_exp = sb_first("a_exp", [P, A_HEADS, A_KEYS])
            a_expT = sb_first("a_expT", [P, A_PAIRS, P])
            a_xTg = sb_first("a_xTg", [P, 2, 4, A_KEYS])
        w1_hi, w1_lo, w1_next_hi, w1_next_lo = (
            sb(name, [P, 2 * HID], F32R) for name in ("w1_hi", "w1_lo", "w1_next_hi", "w1_next_lo"))
        h2T_hi = sb("h2T_hi", [P, SEQ], F32R)
        h2T_lo = sb("h2T_lo", [P, SEQ], F32R)

        s_ax_first = sem("s_ax_first")
        s_ax = sem("s_ax")
        s_whi, s_wlo = sem("s_whi"), sem("s_wlo")
        s_w1, s_w1_hi, s_w1_lo = sem("s_w1"), sem("s_w1_hi"), sem("s_w1_lo")
        s_const = sem("s_const")
        s_tab = sem("s_tab")
        s_wqkv = sem("s_wqkv")
        s_wts = sem("s_wts")
        s_ffnw = sem("s_ffnw")
        s_zero = sem("s_zero")
        s_table = sem("s_table")
        s_setup = sem("s_setup")
        s_bf = sem("s_bf")
        s_rot = sem("s_rot")
        s_ain = sem("s_ain")
        s_axT_ps = sem("s_axT_ps")
        s_axT = sem("s_axT")
        s_axTg = sem("s_axTg")
        s_as = sem("s_as")
        s_amax = sem("s_amax")
        s_adif = sem("s_adif")
        s_aexp = sem("s_aexp")
        s_aT_ps = sem2("s_aT_ps")
        s_aT = sem2("s_aT")
        s_av = sem("s_av")
        s_ao_ps = sem("s_ao_ps")
        s_ao9 = sem("s_ao9")
        s_arec = sem("s_arec")
        s_ao = sem("s_ao")
        s_aden = sem("s_aden")
        s_arden = sem("s_arden")
        s_aalpha = sem("s_aalpha")
        s_ay = sem("s_ay")
        s_ast = sem("s_ast")
        s_amv = sem("s_amv")
        s_ave = sem("s_ave")
        s_arstd = sem("s_arstd")
        s_axn = sem("s_axn")
        s_ax_dma = sem("s_ax_dma")
        x_ready = sem("x_ready")
        s_xs = sem("s_xs")
        s_hT_ps = sem("s_hT_ps")
        s_hT_hi = sem("s_hT_hi")
        s_hT = sem("s_hT")
        s_q_ps, s_k_ps, s_v_ps = sem2("s_q_ps"), sem2("s_k_ps"), sem2("s_v_ps")
        s_q_rotd, s_k_rotd = sem2("s_q_rotd"), sem2("s_k_rotd")
        s_q_sq, s_k_sq = sem2("s_q_sq"), sem2("s_k_sq")
        s_v = sem2("s_v")
        s_V0 = sem("s_V0")
        s_vmix = sem("s_vmix")
        s_ss, s_ssf, s_rnorm = sem2("s_ss"), sem2("s_ssf"), sem2("s_rnorm")
        s_qrot, s_krot, s_knorm = sem2("s_qrot"), sem2("s_krot"), sem2("s_knorm")
        s_qT_ps, s_kT_ps, s_qT, s_kT = sem2("s_qT_ps"), sem2("s_kT_ps"), sem2("s_qT"), sem2("s_kT")
        s_s_ps = sem2("s_s_ps")
        s_sc8, s_smax, s_nbias = sem2("s_sc8"), sem2("s_smax"), sem2("s_nbias")
        s_pa, s_pb = sem2("s_pa"), sem2("s_pb")
        s_paT_ps, s_pbT_ps, s_paT, s_pbT = sem2("s_paT_ps"), sem2("s_pbT_ps"), sem2("s_paT"), sem2("s_pbT")
        s_o_ps, s_rsum, s_o = sem2("s_o_ps"), sem2("s_rsum"), sem2("s_o")
        s_oT_ps, s_oT, s_wo_ps, s_x1 = sem2("s_oT_ps"), sem2("s_oT"), sem2("s_wo_ps"), sem2("s_x1")
        s_h2 = sem("s_h2")
        s_x1b = sem("s_x1b")
        s_st, s_mv, s_ve, s_rstd, s_h2n = sem("s_st"), sem("s_mv"), sem("s_ve"), sem("s_rstd"), sem("s_h2n")
        s_h2T_ps, s_h2T_full, s_h2T_hi, s_h2T = (sem(n) for n in ("s_h2T_ps", "s_h2T_full", "s_h2T_hi", "s_h2T"))
        s_params = sem("s_params")
        s_w1_ps, s_gelu, s_gated = ([sem(f"{n}{c}") for c in range(3)] for n in ("s_w1_ps", "s_gelu", "s_gated"))
        s_w2_ps = sem("s_w2_ps")
        s_fy, s_fst, s_fmv, s_fve, s_frstd, s_fout, s_fdma = (
            sem(n) for n in ("s_fy", "s_fst", "s_fmv", "s_fve", "s_frstd", "s_fout", "s_fdma"))

        def exists(n):
            return not isinstance(n, int) or 0 <= n < STEPS

        def layer(n):
            return n // BATCH

        def heads(ap):
            return ap.rearrange("p (h d) -> p h d", h=HEADS)

        shifted = (((slice(0, 64), slice(0, SEQ)), bank_v[0:64, 0:SEQ]),
                   ((slice(64, P), slice(1, SEQ)), bank_v[64:P, 0:SEQ - 1]))

        FULL = 3
        LAST_NORM = DEPTH * BATCH - BATCH + 3

        def ending(u):
            return exists(u - 2) and not exists(u - 1)

        def walk(eng, body, first=-1):
            for u in range(first, FULL):
                body(u, False)
            with eng.Fori(FULL, LAST_NORM) as u:
                body(u, False)
            with eng.Fori(LAST_NORM, STEPS - 1) as u:
                body(u, True)
            for u in range(STEPS - 1, STEPS + 3):
                body(u, True)

        def ffn_weights(eng, l):
            eng.dma_start(ln_gb[:, 0:1], ln_g[l].rearrange("(p o) -> p o", o=1)).then_inc(s_ffnw, 16)
            eng.dma_start(ln_gb[:, 1:2], ln_b[l].rearrange("(p o) -> p o", o=1)).then_inc(s_ffnw, 16)
            for half in range(2):
                for c, (at, size) in enumerate(CHUNKS):
                    eng.dma_start(b1_sb[0:size, half, c:c + 1],
                                  b1[l, half * HID + at:half * HID + at + size].rearrange("(p o) -> p o", o=1)
                                  ).then_inc(s_ffnw, 16)
            eng.dma_start(b2_sb[:, :], b2[l].partition_broadcast(P)).then_inc(s_ffnw, 16)

        FFN_DMAS = 9
        CONST_DMAS = 2
        TAB_DMAS = 4
        WTS_DMAS = 4
        A_HALF = BATCH // 2

        block = ctx.enter_context(nc.Block())

        @block.sync
        def _(sp):
            xq = x.rearrange("b (q two) d -> q b two d", two=2)
            sp.dma_start(a_x[:, 0:1, :, :], xq[:, 0:1]).then_inc(s_ax_first, 16)
            sp.dma_start(ident[:, :], c_ident).then_inc(s_const, 16)
            sp.dma_start(group[:, :], c_group).then_inc(s_const, 16)
            sp.dma_start(a_x[:, 1:BATCH, :, :], xq[:, 1:BATCH]).then_inc(s_ax, 16)
            xv = x.rearrange("b (s j two) d -> j b s two d", s=2, two=2)[:, :, :, 0, :]
            for half in range(2):
                for s in range(2):
                    sp.dma_start(a_xv[64 * half:64 * half + 64, :, s, :], xv[:, :, s, :]).then_inc(s_ax, 16)
            sp.dma_start(mask32[:, :, :], c_mask).then_inc(s_tab, 16)
            sp.dma_start(rot_const[:, :, :, :], c_rotary).then_inc(s_tab, 16)
            sp.dma_start(head_scale[:, :, 0, :], q_scale.partition_broadcast(P)).then_inc(s_tab, 16)
            sp.dma_start(head_scale[:, :, 1, :], k_scale.partition_broadcast(P)).then_inc(s_tab, 16)
            for l in range(DEPTH):
                sp.dma_start(wqkv_sb[:, l, :, :], wqkv[l].rearrange("p (k n) -> p k n", k=3)).then_inc(s_wqkv, 16)
            sp.dma_start(wo_sb[:, :, :, :].rearrange("p l k n -> p (l k) n"),
                         wo.rearrange("l (k p) n -> p (l k) n", p=P)).then_inc(s_wts, 16)
            for l in range(DEPTH):
                sp.dma_start(w2_sb[:, l, 0:2, :],
                             w2[l, 0:2 * CHUNK, :].rearrange("(c p) n -> p c n", p=CHUNK)).then_inc(s_wts, 16)
            sp.dma_start(w2_sb[0:HID - 2 * CHUNK, :, 2, :],
                         w2[:, 2 * CHUNK:HID, :].rearrange("l p n -> p l n")).then_inc(s_wts, 16)
            ffn_weights(sp, 0)
            for l in range(DEPTH):
                sp.dma_start(w1_raw[:, l, :], w1[l]).then_inc(s_w1, 16)

            def place_stream(half):
                part = slice(half * A_HALF, half * A_HALF + A_HALF)
                sp.wait_ge(s_axn, half + 1)
                for s in range(2):
                    for odd in range(2):
                        sp.dma_start(X[odd:P:2, part, s, :], a_xn[64 * s:64 * s + 64, part, odd, :]
                                     ).then_inc(s_ax_dma, 16)
                sp.wait_ge(s_ax_dma, 64 * half + 64)
                sp.sem_inc(x_ready, A_HALF)

            def count(value):
                return value if isinstance(value, int) else sp.to_reg(value)

            def body(n, norm):
                u, p, o, b = count(n - 1), count(n - 2), count(n - 3), n - 1 - LAST_NORM
                V0_before, mixed_before = count(16 * n - 16), count(48 * n - 48)
                if exists(n):
                    sp.wait_ge(x_ready, n + 1)
                    if exists(n - 1):
                        sp.wait_ge(s_hT_ps, n)
                    sp.dma_start(xs[:, :, :], X[:, bass.ds(n, 1), :, :].rearrange("p o t d -> p (o t) d")
                                 ).then_inc(s_xs, 16)
                if exists(p):
                    if exists(n - 3):
                        sp.wait_ge(s_o_ps[1], p)
                    sp.wait_ge(s_v[1], u)
                    sp.wait_ge(s_V0, V0_before)
                    sp.dma_start(V1[:, :], V1_next[:, :]).then_inc(s_vmix, 16)
                    sp.dma_start(Vmix[0:64, :], V1_next[0:64, :]).then_inc(s_vmix, 16)
                    sp.dma_start(Vmix[64:P, :], V0[64:P, :]).then_inc(s_vmix, 16)
                if isinstance(o, int) and o == BATCH:
                    sp.wait_ge(s_x1b, BATCH)
                    for c in range(3):
                        sp.wait_ge(s_gated[c], BATCH)
                    ffn_weights(sp, 1)
                    sp.wait_ge(s_w1_lo, DEPTH)
                    for to, src in ((w1_hi, w1_next_hi), (w1_lo, w1_next_lo)):
                        sp.dma_start(to[:, :].bitcast(F32), src[:, :].bitcast(F32)).then_inc(s_ffnw, 16)
                if exists(o):
                    if exists(n - 4):
                        sp.wait_ge(s_h2n, o)
                    sp.wait_ge(s_x1[0], p)
                    sp.dma_start(x1_parts[0:1, 1, 1, :], x1_parts[P - 1:P, 0, 2, :]).then_inc(s_h2, 16)
                    sp.wait_ge(s_x1[1], p)
                    sp.dma_start(x1_parts[1:P, :, 1, :], x1_parts[0:P - 1, :, 2, :]).then_inc(s_h2, 16)
                if isinstance(o, int) and o == BATCH:
                    sp.wait_ge(s_ffnw, 16 * (2 * FFN_DMAS + 2))
                if exists(o):
                    sp.sem_inc(s_params, 1)
                if exists(u):
                    if exists(p):
                        sp.wait_ge(s_o_ps[0], u)
                        sp.wait_ge(s_vmix, mixed_before)
                    sp.wait_ge(s_v[0], n)
                    sp.dma_start(V0[:, :], V0_next[:, :]).then_inc(s_V0, 16)
                if norm:
                    sp.wait_ge(s_fout, b + 1)
                    sp.dma_start(out_v[:, bass.ds(b, 1), :, :].rearrange("p o t d -> p (o t) d"), f_out[:, :, :]
                                 ).then_inc(s_fdma, 16)

            out_v = out.rearrange("b (t p) d -> p b t d", p=P)
            place_stream(0)
            sp.wait_ge(s_ffnw, 16 * FFN_DMAS)
            for n in range(FULL + 1):
                body(n, False)
            place_stream(1)
            switch = BATCH + 3
            with sp.Fori(FULL + 1, switch) as n:
                body(n, False)
            body(switch, False)
            with sp.Fori(LAST_NORM + 1, STEPS) as n:
                body(n, True)
            for n in range(STEPS, STEPS + 4):
                body(n, True)
            sp.wait_ge(s_fdma, 16 * BATCH)

        @block.gpsimd
        def _(pool):
            pool.wait_ge(s_tab, 16 * TAB_DMAS)
            for l in range(DEPTH):
                for t in range(TILES):
                    for kind in range(4):
                        scale = head_scale[:, l, kind // 2, :]
                        table, to = rot_const[:, t, kind, :], rot_tab[:, l, t, kind, :]
                        if kind % 2:
                            scale, table, to = (a.rearrange("p (s d) -> p s d", s=2) for a in (scale, table, to))
                            scale = scale[:, ::-1, :]
                        nc.gpsimd.tensor_tensor(to, table, scale, ALU.mult).then_inc(s_rot, 1)
            for l in range(DEPTH):
                pool.wait_ge(s_whi, l + 1)
                nc.gpsimd.tensor_tensor(wqkv_lo[:, l, :, :], wqkv_sb[:, l, :, :], wqkv_hi[:, l, :, :].bitcast(F32),
                                        ALU.subtract).then_inc(s_wlo, 1)
            pool.wait_ge(s_setup, 5)

            def a_power(half):
                part = slice(half * A_HALF, half * A_HALF + A_HALF)
                pool.wait_ge(s_ave, half + 1)
                nc.gpsimd.tensor_tensor(a_rstd[:, part, :].rearrange("p b i -> p (b i)"),
                                        a_ve[:, part, :].rearrange("p b i -> p (b i)"),
                                        minus_half[:, 0:2 * A_HALF], ALU.pow).then_inc(s_arstd, 1)

            def add_rotated(n, t, which):
                pool.wait_ge((s_q_rotd, s_k_rotd)[which][t], n + 1)
                if which == 0 and exists(n - 1):
                    pool.wait_ge(s_qT_ps[t], n)
                nc.gpsimd.tensor_tensor((qrot, krot)[which][t][:, :], rot_c[t][:, which, :], rot_s[t][:, which, :],
                                        ALU.add).then_inc((s_qrot, s_krot)[which][t], 1)

            def normalize_k(n, t):
                pool.wait_ge(s_ssf[t], n + 1)
                if exists(n - 1):
                    pool.wait_ge(s_sc8[t], n)
                nc.gpsimd.tensor_tensor(rnorm[t][:, :], ssf[:, :], minus_half[:, :], ALU.pow).then_inc(s_rnorm[t], 1)
                pool.wait_ge(s_rnorm[t], n + 1)
                pool.wait_ge(s_krot[t], n + 1)
                if exists(n - 1):
                    pool.wait_ge(s_kT_ps[t], n)
                nc.gpsimd.tensor_tensor(heads(knorm[t][:, :]), heads(krot[t][:, :]),
                                        rnorm[t][:, HEADS:].unsqueeze(2).broadcast_to([P, HEADS, DH]), ALU.mult
                                        ).then_inc(s_knorm[t], 1)

            def reciprocal_deviation(n):
                pool.wait_ge(s_ve, n + 1)
                nc.gpsimd.tensor_tensor(rstd[:, :], ve[:, :], minus_half[:, 0:TILES], ALU.pow).then_inc(s_rstd, 1)

            def body(u, norm):
                o, b = u - 2, u - LAST_NORM
                if exists(u):
                    add_rotated(u, 0, 0)
                    add_rotated(u, 0, 1)
                    normalize_k(u, 0)
                if exists(u):
                    add_rotated(u, 1, 0)
                if ending(u):
                    reciprocal_deviation(o)
                if norm:
                    pool.wait_ge(s_fve, b + 1)
                    nc.gpsimd.tensor_tensor(f_rstd[:, :], f_ve[:, :], minus_half[:, 0:TILES], ALU.pow
                                            ).then_inc(s_frstd, 1)
                if exists(o) and not ending(u):
                    reciprocal_deviation(o)
                if exists(u):
                    add_rotated(u, 1, 1)
                if exists(o):
                    pool.wait_ge(s_x1[0], o + 1)
                    pool.wait_ge(s_x1[1], o + 1)
                    pool.wait_ge(s_params, o + 1)
                    if exists(o - 1):
                        pool.wait_ge(x_ready, BATCH + o)
                    halves = "p (s d) -> p s d"
                    nc.gpsimd.tensor_tensor(x1b[:, :, :].rearrange("p t (s d) -> p t s d", s=2), x1,
                                            b2_sb[:, :].rearrange(halves, s=2).unsqueeze(1).broadcast_to(
                                                [P, TILES, 2, DIM // 2]), ALU.add).then_inc(s_x1b, 1)
                if exists(u):
                    normalize_k(u, 1)

            a_power(0)
            body(0, False)
            for l, (hi, lo) in enumerate(((w1_hi, w1_lo), (w1_next_hi, w1_next_lo))):
                pool.wait_ge(s_w1_hi, l + 1)
                nc.gpsimd.tensor_tensor(lo[:, :], w1_raw[:, l, :], hi[:, :].bitcast(F32), ALU.subtract).then_inc(s_w1_lo, 1)
            body(1, False)
            a_power(1)
            walk(pool, body, 2)

        @block.tensor
        def _(pe):
            def a_transpose(b):
                pe.wait_ge(s_ain, b + 1)
                if exists(b - 1):
                    pe.wait_ge(s_axTg, b)
                nc.tensor.transpose(bank_q[:, 0:P], a_in[:, :], ident[:, :]).then_inc(s_axT_ps, 1)

            def a_scores(b):
                pe.wait_ge(s_axT, b + 1)
                pe.wait_ge(s_axTg, b + 1)
                if exists(b - 1):
                    pe.wait_ge(s_adif, b)
                for g in range(4):
                    dims = slice(32 * g, 32 * g + 32)
                    for s in range(2):
                        last = nc.tensor.matmul(
                            bank_as[64 * s:64 * s + 64, g, :],
                            a_xT[dims, 64 * s:64 * s + 64],
                            a_xTg[dims, s, :, :].rearrange("p m j -> p (m j)"), start=True, stop=True)
                last.then_inc(s_as, 1)

            def a_values(b):
                pe.wait_ge(s_aexp, b + 1)
                for half, bank in ((0, bank_t0), (1, bank_t1)):
                    if exists(b - 1):
                        pe.wait_ge(s_aT[half], b)
                    for j in range(4):
                        pair = 4 * half + j
                        last = nc.tensor.transpose(
                            bank[:, P * j:P * j + P],
                            a_exp[:, 2 * pair:2 * pair + 2, :].rearrange("p h j -> p (h j)"), ident[:, :])
                    last.then_inc(s_aT_ps[half], 1)
                pe.wait_ge(s_av, b + 1)
                if exists(b - 1):
                    pe.wait_ge(s_ao9, b)
                for half in range(2):
                    pe.wait_ge(s_aT[half], b + 1)
                    for pair in range(4 * half, 4 * half + 4):
                        for s in range(2):
                            last = nc.tensor.matmul(
                                bank_o[64 * s:64 * s + 64, 18 * pair:18 * pair + 18],
                                a_expT[:, pair, 64 * s:64 * s + 64],
                                a_v[:, s, pair, :, :].rearrange("p h d -> p (h d)"), start=True, stop=True)
                last.then_inc(s_ao_ps, 1)

            pe.wait_ge(s_const, 16 * CONST_DMAS)
            pe.wait_ge(s_setup, 5)
            a_transpose(0)
            a_scores(0)
            a_transpose(1)

            def a_body(b):
                a_scores(b + 1)
                if not isinstance(b, int) or b + 2 < BATCH:
                    a_transpose(b + 2)
                a_values(b)

            a_body(0)
            with pe.Fori(1, BATCH - 2) as b:
                a_body(b)
            a_body(BATCH - 2)
            a_values(BATCH - 1)

            def transpose_h(n):
                pe.wait_ge(s_xs, 16 * n + 16)
                if exists(n - 1):
                    pe.wait_ge(s_v[1], n)
                else:
                    pe.wait_ge(s_adif, BATCH)
                for t in range(TILES):
                    last = nc.tensor.transpose(bank_v[:, P * t:P * t + P], xs[:, t, :], ident[:, :])
                last.then_inc(s_hT_ps, 1)

            def project(n, t, which):
                bank, done = [(bank_q, s_q_ps), (bank_k, s_k_ps), (bank_v, s_v_ps)][which]
                pe.wait_ge(s_hT, n + 1)
                last_reader = (s_q_sq, s_k_sq, s_v)[which]
                if t == 1:
                    pe.wait_ge(last_reader[0], n + 1)
                elif exists(n - 1):
                    pe.wait_ge(last_reader[1], n)
                if t == 0 and exists(n - 3):
                    pe.wait_ge(s_gated[which], n - 2)
                for i, (h, w) in enumerate(((hT_hi, wqkv_hi), (hT_hi, wqkv_lo), (hT_lo, wqkv_hi))):
                    last = nc.tensor.matmul(bank[:, :], h[:, P * t:P * t + P],
                                            w[:, bass.ds(layer(n), 1), which, :].rearrange("p o n -> p (o n)"),
                                            start=(i == 0), stop=(i == 2))
                last.then_inc(done[t], 1)

            def transpose_q(n, t):
                pe.wait_ge(s_qrot[t], n + 1)
                if t == 0:
                    if exists(n - 1):
                        pe.wait_ge(s_pbT[0], n)
                    else:
                        pe.wait_ge(s_aT[0], BATCH)
                else:
                    pe.wait_ge(s_qT[0], n + 1)
                    if exists(n - 1):
                        pe.wait_ge(s_paT[1], n)
                for j in range(BLOCKS):
                    last = nc.tensor.transpose(bank_t0[:, P * j:P * j + P], qrot[t][:, P * j:P * j + P], ident[:, :])
                last.then_inc(s_qT_ps[t], 1)

            def transpose_k(n, t):
                pe.wait_ge(s_knorm[t], n + 1)
                if t == 0:
                    if exists(n - 1):
                        pe.wait_ge(s_paT[0], n)
                    else:
                        pe.wait_ge(s_aT[1], BATCH)
                else:
                    pe.wait_ge(s_kT[0], n + 1)
                    if exists(n - 1):
                        pe.wait_ge(s_pbT[1], n)
                for j in range(BLOCKS):
                    last = nc.tensor.transpose(bank_t1[:, P * j:P * j + P], knorm[t][:, P * j:P * j + P], ident[:, :])
                last.then_inc(s_kT_ps[t], 1)

            def scores(n, t):
                pe.wait_ge(s_qT[t], n + 1)
                pe.wait_ge(s_kT[t], n + 1)
                if t == 1:
                    pe.wait_ge(s_pb[0], n + 1)
                elif exists(n - 1):
                    pe.wait_ge(s_pb[1], n)
                for half in range(2):
                    nc.tensor.matmul(bank_s[:, half, :].rearrange("p (h j) -> p h j", h=4), ident_bf[:, :],
                                     mask_bf[:, t, :].unsqueeze(1).broadcast_to([P, 4, P]),
                                     start=True, stop=False, skip_group_check=True)
                for h in range(HEADS):
                    dims = slice(64 * (h % 2), 64 * (h % 2) + 64)
                    bank, col = bank_s[:, h % 2, :], P * (h // 2)
                    keys = kT[dims, h // 2, :].rearrange("p (w j) -> p w j", j=64)
                    if t == 0:
                        even, width = keys[:, 0:1, :], 64
                    else:
                        even, width = keys[:, 2:0:-1, :], P
                    nc.tensor.matmul(bank[0:64, col:col + width].rearrange("p (w j) -> p w j", j=64),
                                     qT[t][dims, h // 2, 0:64], even,
                                     start=False, stop=True, skip_group_check=True)
                    last = nc.tensor.matmul(bank[64:P, col:col + P],
                                            qT[t][dims, h // 2, 64:P],
                                            kT[dims, h // 2, P * t:P * t + P],
                                            start=False, stop=True, skip_group_check=True)
                last.then_inc(s_s_ps[t], 1)

            def transpose_p(n, t, half):
                bank = (bank_t0, bank_t1)[half if t else 1 - half]
                pe.wait_ge((s_pa, s_pb)[half][t], n + 1)
                if t == 1:
                    if exists(n + 1):
                        pe.wait_ge((s_qT, s_kT)[half][0], n + 2)
                    else:
                        pe.wait_ge((s_pbT, s_paT)[half][0], n + 1)
                elif half == 0:
                    pe.wait_ge(s_kT[1], n + 1)
                elif exists(n - 1):
                    pe.wait_ge(s_oT[1], n)
                else:
                    pe.wait_ge(s_qT[1], n + 1)
                for j in range(4):
                    last = nc.tensor.transpose(bank[:, P * j:P * j + P], probs[t][:, 4 * half + j, :], ident[:, :])
                last.then_inc((s_paT_ps, s_pbT_ps)[half][t], 1)

            def attend(n, t):
                if t == 0:
                    pe.wait_ge(s_V0, 16 * n + 16)
                    if exists(n - 1):
                        pe.wait_ge(s_x1[1], n)
                    else:
                        pe.wait_ge(s_ao9, BATCH)
                else:
                    pe.wait_ge(s_vmix, 48 * n + 48)
                    pe.wait_ge(s_x1[0], n + 1)
                for half in range(2):
                    pe.wait_ge((s_paT, s_pbT)[half][t], n + 1)
                    for h in range(half, HEADS, 2):
                        cols = slice(DH * h, DH * h + DH)
                        last = nc.tensor.matmul(bank_o[64:P, cols], probsT[:, SLOT[h], 64:P],
                                                (V1 if t else V0)[:, cols], start=True, stop=True)
                        if t == 1:
                            last = nc.tensor.matmul(bank_o[0:64, cols], probsT[:, SLOT[h], 0:64], Vmix[:, cols],
                                                    start=True, stop=True)
                if t == 0:
                    for h in range(HEADS):
                        cols = slice(DH * h, DH * h + DH)
                        last = nc.tensor.matmul(bank_o[0:64, cols], probsT[0:64, SLOT[h], 0:64], V0[0:64, cols],
                                                start=True, stop=True)
                last.then_inc(s_o_ps[t], 1)

            def transpose_o(n, t):
                bank = bank_t0 if t else bank_o
                pe.wait_ge(s_o[t], n + 1)
                if t == 1 and exists(n + 1):
                    pe.wait_ge(s_qT[1], n + 2)
                elif t == 1:
                    pe.wait_ge(s_paT[1], n + 1)
                for j in range(BLOCKS):
                    last = nc.tensor.transpose(bank[:, P * j:P * j + P], o_sb[:, P * j:P * j + P], ident[:, :])
                last.then_inc(s_oT_ps[t], 1)

            def project_o(n, t):
                pe.wait_ge(s_oT[t], n + 1)
                pe.wait_ge(s_o[t], n + 1)
                if t == 1 and exists(n - 1) and exists(n + 1):
                    pe.wait_ge(x_ready, BATCH + n)
                for j in range(BLOCKS):
                    last = nc.tensor.matmul(bank_o[:, 0:DIM], oT[:, j, :],
                                            wo_sb[:, bass.ds(layer(n), 1), j, :].rearrange("p o n -> p (o n)"),
                                            start=(j == 0), stop=(j == BLOCKS - 1))
                last.then_inc(s_wo_ps[t], 1)

            def transpose_h2(n):
                pe.wait_ge(s_h2n, n + 1)
                pe.wait_ge(s_k_sq[1], (n + 3) if exists(n + 2) else STEPS)
                for t in range(TILES):
                    last = nc.tensor.transpose(bank_k[:, P * t:P * t + P], h2n[:, t, :], ident[:, :])
                last.then_inc(s_h2T_ps, 1)

            def ffn_up(n, c):
                at, size = CHUNKS[c]
                if c == 0:
                    pe.wait_ge(s_params, n + 1)
                    pe.wait_ge(s_h2T_hi, n + 1)
                if c == 2 and exists(n + 3):
                    pe.wait_ge(s_hT, n + 4)
                else:
                    pe.wait_ge((s_q_sq[1], s_k_sq[1], s_v[1])[c], (n + 3) if exists(n + 2) else STEPS)
                if exists(n - 1):
                    pe.wait_ge(s_gated[c], n)
                bank = (bank_q, bank_k, bank_v)[c]
                for half in range(2):
                    for i, (w, h) in enumerate(((w1_hi, h2T_hi), (w1_lo, h2T_hi), (w1_hi, h2T_lo))):
                        if c == 0 and i == 2:
                            pe.wait_ge(s_h2T, n + 1)
                        last = nc.tensor.matmul(bank[0:size, SEQ * half:SEQ * half + SEQ],
                                                w[:, half * HID + at:half * HID + at + size], h[:, :],
                                                start=(i == 0), stop=(i == 2))
                last.then_inc(s_w1_ps[c], 1)

            def ffn_down(n):
                if exists(n + 2):
                    pe.wait_ge(s_o[1], n + 2)
                else:
                    pe.wait_ge(s_x1[1], STEPS)
                for t in range(TILES):
                    for c, (at, size) in enumerate(CHUNKS):
                        pe.wait_ge(s_gated[c], n + 1)
                        last = nc.tensor.matmul(bank_o[:, DIM * t:DIM * t + DIM],
                                                gated[0:size, c, P * t:P * t + P],
                                                w2_sb[0:size, bass.ds(layer(n), 1), c, :].rearrange("p o n -> p (o n)"),
                                                start=(c == 0), stop=(c == 2))
                last.then_inc(s_w2_ps, 1)

            def body(u, norm):
                p, o, f = u - 1, u - 2, u - 3
                if exists(p):
                    transpose_q(p, 0)
                    transpose_k(p, 0)
                if exists(o):
                    transpose_o(o, 0)
                if exists(f):
                    transpose_h2(f)
                if exists(o):
                    transpose_p(o, 1, 0)
                    project_o(o, 0)
                if ending(u):
                    transpose_p(o, 1, 1)
                    ffn_up(f, 0)
                    attend(o, 1)
                    ffn_up(f, 1)
                    transpose_o(o, 1)
                    ffn_up(f, 2)
                    project_o(o, 1)
                    ffn_down(f)
                    return
                if exists(f):
                    ffn_up(f, 0)
                    ffn_up(f, 1)
                if exists(o):
                    transpose_p(o, 1, 1)
                if exists(f):
                    ffn_up(f, 2)
                if exists(p):
                    scores(p, 0)
                if exists(o):
                    attend(o, 1)
                if exists(u):
                    project(u, 0, 0)
                    project(u, 0, 1)
                    project(u, 0, 2)
                if exists(p):
                    transpose_q(p, 1)
                    transpose_k(p, 1)
                if exists(f):
                    ffn_down(f)
                if exists(o):
                    transpose_o(o, 1)
                if exists(u):
                    project(u, 1, 0)
                    project(u, 1, 1)
                if exists(o):
                    project_o(o, 1)
                if exists(u):
                    project(u, 1, 2)
                if exists(p):
                    transpose_p(p, 0, 0)
                    transpose_p(p, 0, 1)
                if exists(p):
                    scores(p, 1)
                if exists(u + 1):
                    transpose_h(u + 1)
                if exists(p):
                    attend(p, 0)

            pe.wait_ge(s_wlo, DEPTH)
            pe.wait_ge(s_bf, 2)
            pe.wait_ge(s_wts, 16 * WTS_DMAS)
            for u in range(-1, FULL):
                body(u, False)
            pe.wait_ge(s_w1_lo, DEPTH)
            walk(pe, body, FULL)

        @block.scalar
        def _(act):
            def a_exps(b):
                act.wait_ge(s_adif, b + 1)
                if exists(b - 1):
                    act.wait_ge(s_aT_ps[1], b)
                nc.scalar.activation(a_exp[:, :, :], a_dif[:, :, :], ACT.Exp, scale=A_DH ** -0.5).then_inc(s_aexp, 1)

            def a_copy(b):
                for half, bank in ((0, bank_t0), (1, bank_t1)):
                    act.wait_ge(s_aT_ps[half], b + 1)
                    if exists(b - 1):
                        act.wait_ge(s_ao_ps, b)
                    nc.scalar.activation(a_expT[:, 4 * half:4 * half + 4, :].rearrange("p a b -> p (a b)"), bank,
                                         ACT.Copy).then_inc(s_aT[half], 1)

            a_exps(0)
            a_copy(0)
            a_exps(1)
            for l in range(DEPTH):
                act.wait_ge(s_wqkv, 16 * DEPTH)
                nc.scalar.activation(wqkv_hi[:, l, :, :], wqkv_sb[:, l, :, :], ACT.Copy).then_inc(s_whi, 1)
            with act.Fori(1, BATCH - 1) as b:
                a_copy(b)
                a_exps(b + 1)
            a_copy(BATCH - 1)

            def squares_of(n, t, which):
                rotd, done = ((s_q_rotd, s_q_sq), (s_k_rotd, s_k_sq))[which]
                act.wait_ge(rotd[t], n + 1)
                if t == 1:
                    act.wait_ge(s_ss[0], n + 1)
                elif exists(n - 1):
                    act.wait_ge(s_ss[1], n)
                nc.scalar.activation(squares[:, which, :], (bank_q, bank_k)[which][:, :], ACT.Square
                                     ).then_inc(done[t], 1)

            def exps(n, t, half):
                act.wait_ge(s_nbias[t], n + 1)
                if half == 0 and exists(n - 1):
                    act.wait_ge(s_pbT_ps[t], n)
                for h in range(4 * half, 4 * half + 4):
                    last = nc.scalar.activation(probs[t][:, h, :], bank_s[:, half, P * (h % 4):P * (h % 4) + P],
                                                ACT.Exp, bias=nbias[t][:, h:h + 1], scale=sc8[t][:, h:h + 1],
                                                accum_out=psums[t][:, h:h + 1])
                last.then_inc((s_pa, s_pb)[half][t], 1)

            def copy_qT(n):
                act.wait_ge(s_qT_ps[1], n + 1)
                nc.scalar.activation(qT[1][:, :, :].rearrange("p a b -> p (a b)"), bank_t0[:, :], ACT.Copy
                                     ).then_inc(s_qT[1], 1)

            def copy_oT(n, t):
                act.wait_ge(s_oT_ps[t], n + 1)
                if t == 1:
                    act.wait_ge(s_wo_ps[0], n + 1)
                elif exists(n - 1):
                    act.wait_ge(s_wo_ps[1], n)
                nc.scalar.activation(oT[:, :, :].rearrange("p a b -> p (a b)"), bank_t0 if t else bank_o, ACT.Copy
                                     ).then_inc(s_oT[t], 1)

            def copy_v(n, t):
                act.wait_ge(s_v_ps[t], n + 1)
                if exists(n - 1):
                    act.wait_ge(s_vmix if t else s_V0, 48 * n if t else 16 * n)
                nc.scalar.activation((V0_next, V1_next)[t][:, :], bank_v, ACT.Copy).then_inc(s_v[t], 1)

            def gelu_of(n, chunks):
                for c in chunks:
                    size = CHUNKS[c][1]
                    act.wait_ge(s_w1_ps[c], n + 1)
                    if exists(n - 1):
                        act.wait_ge(s_gated[c], n)
                    nc.scalar.activation(gelu[0:size, c, :], (bank_q, bank_k, bank_v)[c][0:size, SEQ:2 * SEQ],
                                         ACT.Gelu, bias=b1_sb[0:size, 1, c:c + 1]).then_inc(s_gelu[c], 1)

            def copy_pT(n, t, half):
                bank = (bank_t0, bank_t1)[half if t else 1 - half]
                act.wait_ge((s_paT_ps, s_pbT_ps)[half][t], n + 1)
                if t == 1:
                    act.wait_ge(s_o_ps[0], n + 1)
                elif exists(n - 1):
                    act.wait_ge(s_o_ps[1], n)
                nc.scalar.activation(probsT[:, 4 * half:4 * half + 4, :].rearrange("p a b -> p (a b)"), bank, ACT.Copy
                                     ).then_inc((s_paT, s_pbT)[half][t], 1)

            def load_table(function, uses_before):
                if not isinstance(uses_before, int) or uses_before > 0:
                    act.wait_ge(s_table, uses_before)
                nc.scalar.activation(table_use[:, :], minus_half[:, 0:1], function).then_inc(s_table, 1)

            def round_hT(n):
                act.wait_ge(s_hT_ps, n + 1)
                if exists(n - 1):
                    act.wait_ge(s_v_ps[1], n)
                for to, src in shifted:
                    last = nc.scalar.activation(hT_hi[to], src, ACT.Copy)
                last.then_inc(s_hT_hi, 1)

            def body(u, norm):
                p, o, f = u - 1, u - 2, u - 3
                if ending(u):
                    copy_pT(o, 1, 1)
                    load_table(ACT.Gelu, 2 * f)
                    gelu_of(f, (0,))
                    copy_oT(o, 1)
                    gelu_of(f, (1, 2))
                    return
                if exists(f):
                    gelu_of(f, (0, 1))
                if exists(o):
                    copy_pT(o, 1, 1)
                if exists(f):
                    gelu_of(f, (2,))
                if exists(p) and exists(f):
                    load_table(ACT.Exp, 2 * f + 1)
                if exists(p):
                    exps(p, 0, 0)
                if exists(u):
                    squares_of(u, 0, 0)
                    copy_v(u, 0)
                if exists(p):
                    copy_qT(p)
                if exists(u):
                    squares_of(u, 0, 1)
                if exists(o):
                    copy_oT(o, 1)
                if exists(p):
                    exps(p, 0, 1)
                if exists(u):
                    copy_v(u, 1)
                    squares_of(u, 1, 0)
                    squares_of(u, 1, 1)
                if exists(p):
                    copy_pT(p, 0, 0)
                    copy_pT(p, 0, 1)
                if exists(u + 1):
                    round_hT(u + 1)
                if exists(p):
                    exps(p, 1, 0)
                    copy_oT(p, 0)
                    exps(p, 1, 1)
                if exists(o) and not ending(u + 1):
                    load_table(ACT.Gelu, 2 * o)

            act.wait_ge(s_setup, 5)
            body(-1, False)
            act.wait_ge(s_w1, 16 * DEPTH)
            act.wait_ge(s_aexp, BATCH)
            act.wait_ge(s_ao_ps, BATCH)
            for l, hi in enumerate((w1_hi, w1_next_hi)):
                nc.scalar.activation(hi[:, :], w1_raw[:, l, :], ACT.Copy).then_inc(s_w1_hi, 1)
            walk(act, body, 0)

        @block.vector
        def _(dve):
            def a_even_tokens(b):
                if exists(b - 1):
                    dve.wait_ge(s_axT_ps, b)
                nc.vector.tensor_scalar(a_in[:, :], a_x[:, bass.ds(b, 1), 0, :].rearrange("p o d -> p (o d)"),
                                        1.0, None, ALU.mult).then_inc(s_ain, 1)

            def a_transposed(b):
                dve.wait_ge(s_axT_ps, b + 1)
                if exists(b - 1):
                    dve.wait_ge(s_as, b)
                nc.vector.tensor_copy(a_xT[:, :], bank_q[:, 0:P]).then_inc(s_axT, 1)
                for s in range(2):
                    last = nc.vector.tensor_tensor(
                        a_xTg[:, s, :, :],
                        bank_q[:, 64 * s:64 * s + 64].unsqueeze(1).broadcast_to([P, 4, A_KEYS]),
                        group[:, :].unsqueeze(2).broadcast_to([P, 4, A_KEYS]), ALU.mult)
                last.then_inc(s_axTg, 1)

            def a_softmax(b):
                dve.wait_ge(s_as, b + 1)
                scores = bank_as.rearrange("p g (m j) -> p g m j", j=A_KEYS)
                nc.vector.tensor_reduce(a_max[:, :], scores, AX.X, ALU.max).then_inc(s_amax, 1)
                dve.wait_ge(s_amax, b + 1)
                if exists(b - 1):
                    dve.wait_ge(s_aexp, b)
                nc.vector.tensor_tensor(a_dif[:, :, :].rearrange("p (g m) j -> p g m j", g=4), scores,
                                        a_max[:, :].rearrange("p (g m) -> p g m", g=4).unsqueeze(3
                                                              ).broadcast_to([P, 4, 4, A_KEYS]), ALU.subtract
                                        ).then_inc(s_adif, 1)

            def a_values(b):
                if exists(b - 1):
                    dve.wait_ge(s_ao_ps, b)
                for half in range(2):
                    rows = slice(64 * half, 64 * half + 64)
                    for s in range(2):
                        last = nc.vector.tensor_scalar(
                            a_v[rows, s, :, half, 0:A_DH],
                            a_xv[rows, bass.ds(b, 1), s, :].rearrange("p o (a h d) -> p (o a) h d", h=2, d=A_DH)[:, :, half, :],
                            1.0, None, ALU.mult)
                last.then_inc(s_av, 1)

            def a_output(b):
                dve.wait_ge(s_ao_ps, b + 1)
                nc.vector.tensor_scalar(a_o9[:, bass.ds(b, 1), :, :].rearrange("p o h d -> p (o h d)"),
                                        bank_o[:, 0:A_HEADS * (A_DH + 1)], 1.0, None, ALU.mult).then_inc(s_ao9, 1)

            def a_shares(half):
                part = slice(half * A_HALF, half * A_HALF + A_HALF)
                n = half + 1
                dve.wait_ge(s_ao9, n * A_HALF)
                nc.vector.reciprocal(a_rec[:, part, :].unsqueeze(3), a_o9[:, part, :, A_DH:A_DH + 1]).then_inc(s_arec, 1)
                dve.wait_ge(s_arec, n)
                nc.vector.tensor_tensor(a_o[:, part, :, :], a_o9[:, part, :, 0:A_DH],
                                        a_rec[:, part, :].unsqueeze(3).broadcast_to([P, A_HALF, A_HEADS, A_DH]),
                                        ALU.mult).then_inc(s_ao, 1)
                dve.wait_ge(s_ao, n)
                flat = a_o[:, part, :, :].rearrange("p b h d -> p b (h d)")
                nc.vector.tensor_reduce(a_den[:, part], flat, AX.X, ALU.add).then_inc(s_aden, 1)
                dve.wait_ge(s_aden, n)
                nc.vector.reciprocal(a_rden[:, part], a_den[:, part]).then_inc(s_arden, 1)
                dve.wait_ge(s_arden, n)
                nc.vector.tensor_tensor(a_alpha[:, part], a_den[:, part], a_rden[:, part], ALU.mult).then_inc(s_aalpha, 1)
                dve.wait_ge(s_aalpha, n)
                for b in range(half * A_HALF, half * A_HALF + A_HALF):
                    last = nc.vector.scalar_tensor_tensor(
                        a_y[:, b, :], a_o[:, b, :, :].rearrange("p h d -> p (h d)"), a_alpha[:, b:b + 1],
                        a_x[:, b, 0, :], ALU.mult, ALU.add)
                last.then_inc(s_ay, 1)

            def a_statistics(half):
                part = slice(half * A_HALF, half * A_HALF + A_HALF)
                n = half + 1
                dve.wait_ge(s_ay, n)
                for b in range(half * A_HALF, half * A_HALF + A_HALF):
                    nc.vector.bn_stats(a_st[:, b, 0, :], a_y[:, b, :])
                    last = nc.vector.bn_stats(a_st[:, b, 1, :], a_x[:, b, 1, :])
                last.then_inc(s_ast, 1)
                nc.vector.memset(a_ve[:, part, :], EPS)
                dve.wait_ge(s_ast, n)
                for b in range(half * A_HALF, half * A_HALF + A_HALF):
                    for i in range(2):
                        last = nc.vector.bn_aggr(a_mv[:, b, i, :], a_st[:, b, i, :])
                last.then_inc(s_amv, 1)
                dve.wait_ge(s_amv, n)
                nc.vector.tensor_tensor(a_ve[:, part, :], a_ve[:, part, :], a_mv[:, part, :, 1], ALU.add
                                        ).then_inc(s_ave, 1)

            def a_normalize(half):
                dve.wait_ge(s_arstd, half + 1)
                for b in range(half * A_HALF, half * A_HALF + A_HALF):
                    for i, src in enumerate((a_y[:, b, :], a_x[:, b, 1, :])):
                        last = nc.vector.tensor_scalar(a_xn[:, b, i, :], src, a_mv[:, b, i, 0:1],
                                                       a_rstd[:, b, i:i + 1], ALU.subtract, ALU.mult)
                last.then_inc(s_axn, 1)

            def a_body(b):
                ahead = not isinstance(b, int) or b + 2 < BATCH
                if ahead:
                    a_even_tokens(b + 2)
                a_values(b)
                a_softmax(b + 1)
                if ahead:
                    a_transposed(b + 2)
                a_output(b)

            nc.vector.memset(a_v[:, :, :, :, :], 0.0).then_inc(s_zero, 1)
            nc.vector.memset(minus_half[:, :], -0.5).then_inc(s_setup, 1)
            nc.vector.memset(hT_hi[64:P, 0:1].bitcast(F32), 0.0)
            nc.vector.memset(hT_lo[64:P, 0:1].bitcast(F32), 0.0).then_inc(s_setup, 1)
            nc.vector.memset(x1_parts[0:1, 0, 1, :], 0.0).then_inc(s_setup, 1)
            dve.wait_ge(s_zero, 1)
            nc.vector.memset(a_v[0:64, :, :, 0, A_DH:A_DH + 1], 1.0).then_inc(s_setup, 1)
            nc.vector.memset(a_v[64:P, :, :, 1, A_DH:A_DH + 1], 1.0).then_inc(s_setup, 1)
            dve.wait_ge(s_ax_first, 16)
            dve.wait_ge(s_const, 16 * CONST_DMAS)
            a_even_tokens(0)
            a_transposed(0)
            dve.wait_ge(s_ax, 16 * 5)
            a_even_tokens(1)
            a_transposed(1)
            a_softmax(0)
            a_body(0)
            with dve.Fori(1, A_HALF) as b:
                a_body(b)
            a_shares(0)
            a_body(A_HALF)
            a_statistics(0)
            a_body(A_HALF + 1)
            a_normalize(0)
            for b in range(A_HALF + 2, BATCH - 1):
                a_body(b)
            a_values(BATCH - 1)
            a_output(BATCH - 1)
            dve.wait_ge(s_tab, 16 * TAB_DMAS)
            nc.vector.tensor_copy(ident_bf[:, :], ident[:, :]).then_inc(s_bf, 1)
            nc.vector.tensor_copy(mask_bf[:, :, :], mask32[:, :, :]).then_inc(s_bf, 1)

            def rotate(n, t, which):
                bank, arrived, done = ((bank_q, s_q_ps, s_q_rotd), (bank_k, s_k_ps, s_k_rotd))[which]
                table = rot_tab[:, bass.ds(layer(n), 1), t, :, :]
                dve.wait_ge(arrived[t], n + 1)
                if exists(n - 1):
                    dve.wait_ge((s_qrot, s_krot)[which][t], n)
                nc.vector.tensor_tensor(heads(rot_c[t][:, which, :]), heads(bank[:, :]),
                                        table[:, :, 2 * which, :].broadcast_to([P, HEADS, DH]), ALU.mult)
                half = "p h (s d) -> p h s d"
                nc.vector.tensor_tensor(heads(rot_s[t][:, which, :]).rearrange(half, s=2),
                                        heads(bank[:, :]).rearrange(half, s=2)[:, :, ::-1, :],
                                        table[:, :, 2 * which + 1, :].rearrange(half, s=2
                                                                                ).broadcast_to([P, HEADS, 2, DH // 2]),
                                        ALU.mult).then_inc(done[t], 1)

            def sum_squares(n, t):
                dve.wait_ge(s_q_sq[t], n + 1)
                dve.wait_ge(s_k_sq[t], n + 1)
                nc.vector.tensor_reduce(ss[:, :], squares[:, :, :].rearrange("p w (h d) -> p (w h) d", d=DH),
                                        AX.X, ALU.add).then_inc(s_ss[t], 1)
                dve.wait_ge(s_ss[t], n + 1)
                if t == 1:
                    dve.wait_ge(s_rnorm[0], n + 1)
                elif exists(n - 1):
                    dve.wait_ge(s_rnorm[1], n)
                nc.vector.tensor_scalar(ssf[:, :], ss[:, :], NORM_FLOOR, None, ALU.max).then_inc(s_ssf[t], 1)

            def scale_of_q(n, t):
                dve.wait_ge(s_rnorm[t], n + 1)
                if exists(n - 1):
                    dve.wait_ge(s_pb[t], n)
                nc.vector.tensor_scalar(sc8[t][:, :].rearrange("p (odd j) -> p odd j", odd=2),
                                        rnorm[t][:, 0:HEADS].rearrange("p (j odd) -> p odd j", odd=2),
                                        QK_SCALE, None, ALU.mult).then_inc(s_sc8[t], 1)

            def row_max(n, t):
                dve.wait_ge(s_s_ps[t], n + 1)
                nc.vector.tensor_reduce(smax[t][:, :], bank_s[:, :, :].rearrange("p a (h j) -> p (a h) j", j=P),
                                        AX.X, ALU.max).then_inc(s_smax[t], 1)
                dve.wait_ge(s_smax[t], n + 1)
                dve.wait_ge(s_sc8[t], n + 1)
                nc.vector.scalar_tensor_tensor(nbias[t][:, :], smax[t][:, :], -1.0, sc8[t][:, :],
                                               ALU.mult, ALU.mult).then_inc(s_nbias[t], 1)

            def copy_qT(n):
                dve.wait_ge(s_qT_ps[0], n + 1)
                nc.vector.tensor_copy(qT[0][:, :, :].rearrange("p a b -> p (a b)"), bank_t0[:, :]).then_inc(s_qT[0], 1)

            def copy_kT(n, t):
                dve.wait_ge(s_kT_ps[t], n + 1)
                if exists(n - 1):
                    dve.wait_ge(s_s_ps[1], n)
                nc.vector.tensor_copy(kT[:, :, P * t:P * t + P],
                                      bank_t1[:, :].rearrange("p (a b) -> p a b", a=BLOCKS)).then_inc(s_kT[t], 1)

            def copy_paT(n):
                dve.wait_ge(s_paT_ps[1], n + 1)
                dve.wait_ge(s_o_ps[0], n + 1)
                nc.vector.tensor_copy(probsT[:, 0:4, :].rearrange("p a b -> p (a b)"), bank_t0).then_inc(s_paT[1], 1)

            def invert_sums(n, t):
                dve.wait_ge(s_pb[t], n + 1)
                if exists(n - 1):
                    dve.wait_ge(s_o[t], n)
                nc.vector.reciprocal(rsums[t][:, :], psums[t][:, :]).then_inc(s_rsum[t], 1)

            def normalize_o(n, t):
                dve.wait_ge(s_rsum[t], n + 1)
                dve.wait_ge(s_o_ps[t], n + 1)
                if t == 1:
                    dve.wait_ge(s_oT_ps[0], n + 1)
                elif exists(n - 1):
                    dve.wait_ge(s_oT_ps[1], n)
                by_pair = "p (j odd d) -> p j odd d"
                nc.vector.tensor_tensor(o_sb[:, :].rearrange(by_pair, odd=2, d=DH),
                                        bank_o[:, :].rearrange(by_pair, odd=2, d=DH),
                                        rsums[t][:, :].rearrange("p (odd j) -> p j odd", odd=2).unsqueeze(3
                                                                 ).broadcast_to([P, BLOCKS, 2, DH]), ALU.mult
                                        ).then_inc(s_o[t], 1)

            def add_attention(n, t):
                dve.wait_ge(s_wo_ps[t], n + 1)
                if exists(n - 1):
                    dve.wait_ge(s_h2, 32 * n)
                    dve.wait_ge(s_h2n, n)
                    dve.wait_ge(s_x1b, n)
                nc.vector.tensor_tensor(x1[:, t, :, :], bank_o[:, 0:DIM].rearrange("p (s d) -> p s d", s=2),
                                        X[:, bass.ds(n, 1), t, :].rearrange("p o (s d) -> p (o s) d", s=2), ALU.add
                                        ).then_inc(s_x1[t], 1)

            def rest_of_hT(n):
                dve.wait_ge(s_hT_hi, n + 1)
                if exists(n - 1):
                    dve.wait_ge(s_v_ps[1], n)
                for to, src in shifted:
                    last = nc.vector.tensor_tensor(hT_lo[to], src, hT_hi[to].bitcast(F32), ALU.subtract)
                last.then_inc(s_hT, 1)

            def statistics(n):
                dve.wait_ge(s_h2, 32 * n + 32)
                for t in range(TILES):
                    last = nc.vector.bn_stats(st[:, t, :], h2[:, t, :])
                last.then_inc(s_st, 1)
                dve.wait_ge(s_st, n + 1)
                nc.vector.memset(ve[:, :], EPS)
                for t in range(TILES):
                    last = nc.vector.bn_aggr(mv[:, t, :], st[:, t, :])
                last.then_inc(s_mv, 1)
                dve.wait_ge(s_mv, n + 1)
                nc.vector.tensor_tensor(ve[:, :], ve[:, :], mv[:, :, 1], ALU.add).then_inc(s_ve, 1)

            def normalize_h2(n):
                dve.wait_ge(s_rstd, n + 1)
                if exists(n - 1):
                    dve.wait_ge(s_h2T_ps, n)
                for t in range(TILES):
                    last = nc.vector.tensor_scalar(h2n[:, t, :], h2[:, t, :], mv[:, t, 0:1], rstd[:, t:t + 1],
                                                   ALU.subtract, ALU.mult)
                last.then_inc(s_h2n, 1)

            def copy_h2T(n):
                dve.wait_ge(s_params, n + 1)
                dve.wait_ge(s_h2T_ps, n + 1)
                if exists(n - 1):
                    dve.wait_ge(s_w1_ps[2], n)
                nc.vector.tensor_scalar(h2T[:, :], bank_k[:, 0:SEQ], ln_gb[:, 0:1], ln_gb[:, 1:2],
                                        ALU.mult, ALU.add).then_inc(s_h2T_full, 1)

            def round_h2T(n):
                dve.wait_ge(s_h2T_full, n + 1)
                nc.vector.tensor_copy(h2T_hi[:, :], h2T[:, :]).then_inc(s_h2T_hi, 1)

            def rest_of_h2T(n):
                dve.wait_ge(s_h2T_hi, n + 1)
                nc.vector.tensor_tensor(h2T_lo[:, :], h2T[:, :], h2T_hi[:, :].bitcast(F32), ALU.subtract).then_inc(s_h2T, 1)

            def gate(n, chunks=range(3)):
                for c in chunks:
                    size = CHUNKS[c][1]
                    dve.wait_ge(s_gelu[c], n + 1)
                    if exists(n - 1):
                        dve.wait_ge(s_w2_ps, n)
                    nc.vector.scalar_tensor_tensor(gated[0:size, c, :], (bank_q, bank_k, bank_v)[c][0:size, 0:SEQ],
                                                   b1_sb[0:size, 0, c:c + 1], gelu[0:size, c, :],
                                                   ALU.add, ALU.mult).then_inc(s_gated[c], 1)

            def add_ffn(n):
                dve.wait_ge(s_w2_ps, n + 1)
                dve.wait_ge(s_x1b, n + 1)
                nc.vector.tensor_tensor(X[:, bass.ds(n + BATCH, 1), :, :].rearrange("p o t d -> p (o t) d"),
                                        bank_o[:, 0:SEQ].rearrange("p (t d) -> p t d", t=TILES), x1b[:, :, :], ALU.add
                                        ).then_inc(x_ready, 1)

            def norm_statistics(b):
                whole = "p o t d -> p (o t) d"
                dve.wait_ge(x_ready, BATCH + STEPS - BATCH + b + 1)
                if exists(b - 1):
                    dve.wait_ge(s_fout, b)
                nc.vector.tensor_tensor(f_y[:, :, :], X[:, bass.ds(b, 1), :, :].rearrange(whole),
                                        X[:, bass.ds(b + STEPS, 1), :, :].rearrange(whole), ALU.add).then_inc(s_fy, 1)
                dve.wait_ge(s_fy, b + 1)
                for t in range(TILES):
                    last = nc.vector.bn_stats(f_st[:, t, :], f_y[:, t, :])
                last.then_inc(s_fst, 1)
                dve.wait_ge(s_fst, b + 1)
                nc.vector.memset(f_ve[:, :], EPS)
                for t in range(TILES):
                    last = nc.vector.bn_aggr(f_mv[:, t, :], f_st[:, t, :])
                last.then_inc(s_fmv, 1)
                dve.wait_ge(s_fmv, b + 1)
                nc.vector.tensor_tensor(f_ve[:, :], f_ve[:, :], f_mv[:, :, 1], ALU.add).then_inc(s_fve, 1)

            def norm_output(b):
                dve.wait_ge(s_frstd, b + 1)
                if exists(b - 1):
                    dve.wait_ge(s_fdma, 16 * b)
                for t in range(TILES):
                    last = nc.vector.tensor_scalar(f_out[:, t, :], f_y[:, t, :], f_mv[:, t, 0:1],
                                                   f_rstd[:, t:t + 1], ALU.subtract, ALU.mult)
                last.then_inc(s_fout, 1)

            def body(u, norm):
                p, o, f, b = u - 1, u - 2, u - 3, u - LAST_NORM
                if exists(o):
                    invert_sums(o, 1)
                if ending(u):
                    normalize_o(o, 1)
                    gate(f, (0, 1))
                    add_attention(o, 1)
                    gate(f, (2,))
                elif exists(f):
                    gate(f)
                if exists(p):
                    row_max(p, 0)
                if exists(o) and not ending(u):
                    normalize_o(o, 1)
                if exists(u):
                    rotate(u, 0, 0)
                    rotate(u, 0, 1)
                if exists(p):
                    copy_kT(p, 1)
                if exists(f):
                    add_ffn(f)
                if exists(u):
                    sum_squares(u, 0)
                    rotate(u, 1, 0)
                if exists(o) and not ending(u):
                    add_attention(o, 1)
                if exists(u):
                    rotate(u, 1, 1)
                if exists(p):
                    invert_sums(p, 0)
                    scale_of_q(p, 1)
                if ending(u):
                    statistics(o)
                    normalize_h2(o)
                if norm:
                    norm_statistics(b)
                if exists(o) and not ending(u):
                    statistics(o)
                if exists(p):
                    row_max(p, 1)
                    normalize_o(p, 0)
                if exists(o) and not ending(u):
                    normalize_h2(o)
                if exists(u):
                    copy_qT(u)
                if exists(o):
                    copy_h2T(o)
                if exists(u):
                    copy_kT(u, 0)
                if exists(o):
                    round_h2T(o)
                if exists(u):
                    scale_of_q(u, 0)
                if exists(o):
                    rest_of_h2T(o)
                if exists(p):
                    copy_paT(p)
                if exists(u + 1):
                    rest_of_hT(u + 1)
                if exists(p):
                    add_attention(p, 0)
                if exists(u):
                    sum_squares(u, 1)
                if norm:
                    norm_output(b)

            dve.wait_ge(s_rot, DEPTH * TILES * 4)
            body(-1, False)
            body(0, False)
            a_shares(1)
            body(1, False)
            a_statistics(1)
            body(2, False)
            a_normalize(1)
            walk(dve, body, 3)


_INS = ["L0_attn_x", "L0_ffn_wqkv", "L0_ffn_q_scale", "L0_ffn_k_scale", "L0_ffn_wo", "L0_ffn_ln_g",
        "L0_ffn_ln_b", "L0_ffn_w1", "L0_ffn_b1", "L0_ffn_w2", "L0_ffn_b2"]
_OUTS = [((BATCH, SEQ, DIM), "float32")]


def kernel(**inputs):
    import numpy as _np
    import concourse.bacc as _bacc
    from concourse import mybir as _mybir
    from concourse.bass_utils import run_bass_kernel_spmd as _run

    nc = _bacc.Bacc("TRN2", target_bir_lowering=False, num_devices=1)
    arrays, args = {}, []
    named = [(name, inputs[name]) for name in _INS] + list(table_constants().items())
    for name, a in named:
        a = _np.ascontiguousarray(a)
        arrays[f"in_{name}_dram"] = a
        args.append(nc.dram_tensor(f"in_{name}_dram", a.shape, _mybir.dt.from_np(a.dtype), kind="ExternalInput").ap())
    for i, (shape, dtype) in enumerate(_OUTS):
        dt = _mybir.dt.from_np(_np.dtype(dtype))
        args.append(nc.dram_tensor(f"out_{i}_dram", shape, dt, kind="ExternalOutput").ap())
    build(nc, *args)
    r = _run(nc, [arrays], core_ids=[0])
    got = tuple(r.results[0][f"out_{i}_dram"] for i in range(len(_OUTS)))
    return got[0]
```
